# Optimizing a Trainium2 kernel written in Bass

```python
import numpy as np
import jax
import jax.numpy as jnp

def _softmax(x, axis=-1):
    return jax.nn.softmax(x, axis=axis)

def _gelu(x):
    return jax.nn.gelu(x, approximate=True)

def _silu(x):
    return jax.nn.silu(x)

def _sigmoid(x):
    return jax.nn.sigmoid(x)

def _layernorm(x, axis=-1, eps=1e-05):
    m = jnp.mean(x, axis=axis, keepdims=True)
    v = jnp.var(x, axis=axis, keepdims=True)
    return (x - m) / jnp.sqrt(v + eps)

def _scatter_add(tgt, idx, src, axis=0):
    return tgt.at[idx].add(src)

def _segment_sum(src, seg, n):
    return jax.ops.segment_sum(src, seg, n)
kernel_name = 'mk_conv_attn_hybrid_d2_conv_nchw384_r2_a39cf0'

def setup_inputs(seed: int=0):
    np.random.seed(seed)
    _w = jnp.asarray

    def _rec_inputs():
        import jax
        import jax.numpy as jnp
        _gk = jax.random.key(seed)
        x = -0.0002221 + 1 * jax.random.normal(jax.random.fold_in(_gk, 1), (16, 192, 32, 32), jnp.float32)
        return x
    x = _rec_inputs()

    def _L0_conv_setup():
        import jax, jax.numpy as jnp
        import numpy as np
        B, C, H, W = (16, 192, 32, 32)
        S, R, GR = (16, 8, 32)
        EPS = 1e-06

        def _ssm1d(x, a_logit, U, V, Win, bin_, Wg, bg, Wout, bout, Wskip, bskip, reverse):
            if reverse:
                x = x[:, ::-1]
            u = jnp.einsum('nld,sd->nls', x, Win) + bin_
            g = jax.nn.sigmoid(jnp.einsum('nld,sd->nls', x, Wg) + bg)
            a = jax.nn.sigmoid(a_logit)
            A = jnp.diag(a) + (U @ V.T).T
            gu = jnp.swapaxes(g * u, 0, 1)
            h0 = jnp.zeros((x.shape[0], a.shape[0]), x.dtype)

            def step(h, gu_t):
                h = h @ A + gu_t
                return (h, h)
            _, hs = jax.lax.scan(step, h0, gu)
            hs = jnp.swapaxes(hs, 0, 1)
            y = jnp.einsum('nls,ds->nld', hs, Wout) + bout + jnp.einsum('nld,ed->nle', x, Wskip) + bskip
            if reverse:
                y = y[:, ::-1]
            return y

        def _forward(x, rp, cp, g1_w, g1_b, g2_w, g2_b, norm_w, norm_b):
            Bx, Cx, Hx, Wx = x.shape
            rows = jnp.transpose(x, (0, 2, 3, 1)).reshape(Bx * Hx, Wx, Cx)
            cols = jnp.transpose(x, (0, 3, 2, 1)).reshape(Bx * Wx, Hx, Cx)
            yr = _ssm1d(rows, *rp, False) + _ssm1d(rows, *rp, True)
            yc = _ssm1d(cols, *cp, False) + _ssm1d(cols, *cp, True)
            yr = jnp.transpose(yr.reshape(Bx, Hx, Wx, Cx), (0, 3, 1, 2))
            yc = jnp.transpose(yc.reshape(Bx, Wx, Hx, Cx), (0, 3, 2, 1))
            y = (yr + yc) * 0.25
            mean = x.mean(axis=1, keepdims=True)
            var = ((x - mean) ** 2).mean(axis=1, keepdims=True)
            xn = (x - mean) / jnp.sqrt(var + EPS)
            xn = xn * norm_w[None, :, None, None] + norm_b[None, :, None, None]
            h1 = jax.nn.gelu(jnp.einsum('bchw,oc->bohw', xn, g1_w) + g1_b[None, :, None, None], approximate=False)
            g = jax.nn.sigmoid(jnp.einsum('bghw,cg->bchw', h1, g2_w) + g2_b[None, :, None, None])
            return g * y + (1.0 - g) * x
        key = jax.random.key(seed)
        ks = jax.random.split(key, 16)

        def rn(k, shape, s):
            return jax.random.normal(k, shape, dtype=jnp.float32) * s
        inp = {'x': jax.random.normal(ks[0], (B, C, H, W), dtype=jnp.float32)}
        i = 1
        for p in ('row', 'col'):
            inp[p + '_a_logit'] = jnp.zeros((S,), jnp.float32)
            inp[p + '_U'] = rn(ks[i], (S, R), 0.02)
            i += 1
            inp[p + '_V'] = rn(ks[i], (S, R), 0.02)
            i += 1
            inp[p + '_Win'] = rn(ks[i], (S, C), 1.0 / np.sqrt(C))
            i += 1
            inp[p + '_bin'] = jnp.zeros((S,), jnp.float32)
            inp[p + '_Wg'] = rn(ks[i], (S, C), 1.0 / np.sqrt(C))
            i += 1
            inp[p + '_bg'] = jnp.zeros((S,), jnp.float32)
            inp[p + '_Wout'] = rn(ks[i], (C, S), 1.0 / np.sqrt(S))
            i += 1
            inp[p + '_bout'] = jnp.zeros((C,), jnp.float32)
            inp[p + '_Wskip'] = rn(ks[i], (C, C), 1.0 / np.sqrt(C))
            i += 1
            inp[p + '_bskip'] = jnp.zeros((C,), jnp.float32)
        inp['g1_w'] = rn(ks[i], (GR, C), 1.0 / np.sqrt(C))
        i += 1
        inp['g1_b'] = jnp.zeros((GR,), jnp.float32)
        inp['g2_w'] = rn(ks[i], (C, GR), 1.0 / np.sqrt(GR))
        i += 1
        inp['g2_b'] = jnp.zeros((C,), jnp.float32)
        inp['norm_w'] = jnp.ones((C,), jnp.float32)
        inp['norm_b'] = jnpp = jnp.zeros((C,), jnp.float32)
        inp['norm_b'] = jnp.zeros((C,), jnp.float32)
        return inp
    _L0_conv_all = _L0_conv_setup()
    _L0_conv_in = {k: v for k, v in _L0_conv_all.items() if k in ('row_a_logit', 'row_U', 'row_V', 'row_Win', 'row_bin', 'row_Wg', 'row_bg', 'row_Wout', 'row_bout', 'row_Wskip', 'row_bskip', 'col_a_logit', 'col_U', 'col_V', 'col_Win', 'col_bin', 'col_Wg', 'col_bg', 'col_Wout', 'col_bout', 'col_Wskip', 'col_bskip', 'g1_w', 'g1_b', 'g2_w', 'g2_b', 'norm_w', 'norm_b')}
    del _L0_conv_all

    def _L1_attn_setup():
        import jax, jax.numpy as jnp
        import numpy as np
        H, D = (6, 32)
        WIN = 33
        PAD = (WIN - 1) // 2
        key = jax.random.key(seed)
        ks = jax.random.split(key, 9)
        B, L, E = (8, 1025, 192)
        s = 1.0 / np.sqrt(E).astype(np.float32)
        return {'x': jax.random.normal(ks[0], (B, L, E), jnp.float32), 'Wq': jax.random.normal(ks[1], (E, E), jnp.float32) * s, 'bq': jax.random.normal(ks[2], (E,), jnp.float32) * 0.01, 'Wk': jax.random.normal(ks[3], (E, E), jnp.float32) * s, 'bk': jax.random.normal(ks[4], (E,), jnp.float32) * 0.01, 'Wv': jax.random.normal(ks[5], (E, E), jnp.float32) * s, 'bv': jax.random.normal(ks[6], (E,), jnp.float32) * 0.01, 'Wo': jax.random.normal(ks[7], (E, E), jnp.float32) * s, 'bo': jax.random.normal(ks[8], (E,), jnp.float32) * 0.01}
    _L1_attn_all = _L1_attn_setup()
    _L1_attn_in = {k: v for k, v in _L1_attn_all.items() if k in ('Wq', 'bq', 'Wk', 'bk', 'Wv', 'bv', 'Wo', 'bo')}
    del _L1_attn_all

    def _L1_ffn_setup():
        import jax, jax.numpy as jnp
        import numpy as np
        NUM_EXPERTS = 4
        TOP_K = 2
        DIM = 192
        HID = 4 * DIM
        key = jax.random.key(seed)
        ks = jax.random.split(key, 5)
        B, S = (16, 1024)
        scale_in = 1.0 / np.sqrt(DIM)
        scale_hid = 1.0 / np.sqrt(HID)
        return {'x': jax.random.normal(ks[0], (B, S, DIM), dtype=jnp.float32), 'gate_w': jax.random.normal(ks[1], (DIM, NUM_EXPERTS), dtype=jnp.float32) * scale_in, 'gate_b': jnp.zeros((NUM_EXPERTS,), dtype=jnp.float32), 'w1': jax.random.normal(ks[2], (NUM_EXPERTS, DIM, HID), dtype=jnp.float32) * scale_in, 'b1': jnp.zeros((NUM_EXPERTS, HID), dtype=jnp.float32), 'w2': jax.random.normal(ks[3], (NUM_EXPERTS, HID, DIM), dtype=jnp.float32) * scale_hid, 'b2': jnp.zeros((NUM_EXPERTS, DIM), dtype=jnp.float32)}
    _L1_ffn_all = _L1_ffn_setup()
    _L1_ffn_in = {k: v for k, v in _L1_ffn_all.items() if k in ('gate_w', 'gate_b', 'w1', 'b1', 'w2', 'b2')}
    del _L1_ffn_all
    return {'x': x, 'L0_conv_row_a_logit': _L0_conv_in['row_a_logit'], 'L0_conv_row_U': _L0_conv_in['row_U'], 'L0_conv_row_V': _L0_conv_in['row_V'], 'L0_conv_row_Win': _L0_conv_in['row_Win'], 'L0_conv_row_bin': _L0_conv_in['row_bin'], 'L0_conv_row_Wg': _L0_conv_in['row_Wg'], 'L0_conv_row_bg': _L0_conv_in['row_bg'], 'L0_conv_row_Wout': _L0_conv_in['row_Wout'], 'L0_conv_row_bout': _L0_conv_in['row_bout'], 'L0_conv_row_Wskip': _L0_conv_in['row_Wskip'], 'L0_conv_row_bskip': _L0_conv_in['row_bskip'], 'L0_conv_col_a_logit': _L0_conv_in['col_a_logit'], 'L0_conv_col_U': _L0_conv_in['col_U'], 'L0_conv_col_V': _L0_conv_in['col_V'], 'L0_conv_col_Win': _L0_conv_in['col_Win'], 'L0_conv_col_bin': _L0_conv_in['col_bin'], 'L0_conv_col_Wg': _L0_conv_in['col_Wg'], 'L0_conv_col_bg': _L0_conv_in['col_bg'], 'L0_conv_col_Wout': _L0_conv_in['col_Wout'], 'L0_conv_col_bout': _L0_conv_in['col_bout'], 'L0_conv_col_Wskip': _L0_conv_in['col_Wskip'], 'L0_conv_col_bskip': _L0_conv_in['col_bskip'], 'L0_conv_g1_w': _L0_conv_in['g1_w'], 'L0_conv_g1_b': _L0_conv_in['g1_b'], 'L0_conv_g2_w': _L0_conv_in['g2_w'], 'L0_conv_g2_b': _L0_conv_in['g2_b'], 'L0_conv_norm_w': _L0_conv_in['norm_w'], 'L0_conv_norm_b': _L0_conv_in['norm_b'], 'L1_attn_Wq': _L1_attn_in['Wq'], 'L1_attn_bq': _L1_attn_in['bq'], 'L1_attn_Wk': _L1_attn_in['Wk'], 'L1_attn_bk': _L1_attn_in['bk'], 'L1_attn_Wv': _L1_attn_in['Wv'], 'L1_attn_bv': _L1_attn_in['bv'], 'L1_attn_Wo': _L1_attn_in['Wo'], 'L1_attn_bo': _L1_attn_in['bo'], 'L1_ffn_gate_w': _L1_ffn_in['gate_w'], 'L1_ffn_gate_b': _L1_ffn_in['gate_b'], 'L1_ffn_w1': _L1_ffn_in['w1'], 'L1_ffn_b1': _L1_ffn_in['b1'], 'L1_ffn_w2': _L1_ffn_in['w2'], 'L1_ffn_b2': _L1_ffn_in['b2']}

def reference(x, L0_conv_row_a_logit, L0_conv_row_U, L0_conv_row_V, L0_conv_row_Win, L0_conv_row_bin, L0_conv_row_Wg, L0_conv_row_bg, L0_conv_row_Wout, L0_conv_row_bout, L0_conv_row_Wskip, L0_conv_row_bskip, L0_conv_col_a_logit, L0_conv_col_U, L0_conv_col_V, L0_conv_col_Win, L0_conv_col_bin, L0_conv_col_Wg, L0_conv_col_bg, L0_conv_col_Wout, L0_conv_col_bout, L0_conv_col_Wskip, L0_conv_col_bskip, L0_conv_g1_w, L0_conv_g1_b, L0_conv_g2_w, L0_conv_g2_b, L0_conv_norm_w, L0_conv_norm_b, L1_attn_Wq, L1_attn_bq, L1_attn_Wk, L1_attn_bk, L1_attn_Wv, L1_attn_bv, L1_attn_Wo, L1_attn_bo, L1_ffn_gate_w, L1_ffn_gate_b, L1_ffn_w1, L1_ffn_b1, L1_ffn_w2, L1_ffn_b2):
    import jax
    import jax.numpy as jnp

    def _L0_conv_ref(x, row_a_logit, row_U, row_V, row_Win, row_bin, row_Wg, row_bg, row_Wout, row_bout, row_Wskip, row_bskip, col_a_logit, col_U, col_V, col_Win, col_bin, col_Wg, col_bg, col_Wout, col_bout, col_Wskip, col_bskip, g1_w, g1_b, g2_w, g2_b, norm_w, norm_b):
        import jax, jax.numpy as jnp
        import numpy as np
        B, C, H, W = (16, 192, 32, 32)
        S, R, GR = (16, 8, 32)
        EPS = 1e-06

        def _ssm1d(x, a_logit, U, V, Win, bin_, Wg, bg, Wout, bout, Wskip, bskip, reverse):
            if reverse:
                x = x[:, ::-1]
            u = jnp.einsum('nld,sd->nls', x, Win) + bin_
            g = jax.nn.sigmoid(jnp.einsum('nld,sd->nls', x, Wg) + bg)
            a = jax.nn.sigmoid(a_logit)
            A = jnp.diag(a) + (U @ V.T).T
            gu = jnp.swapaxes(g * u, 0, 1)
            h0 = jnp.zeros((x.shape[0], a.shape[0]), x.dtype)

            def step(h, gu_t):
                h = h @ A + gu_t
                return (h, h)
            _, hs = jax.lax.scan(step, h0, gu)
            hs = jnp.swapaxes(hs, 0, 1)
            y = jnp.einsum('nls,ds->nld', hs, Wout) + bout + jnp.einsum('nld,ed->nle', x, Wskip) + bskip
            if reverse:
                y = y[:, ::-1]
            return y

        def _forward(x, rp, cp, g1_w, g1_b, g2_w, g2_b, norm_w, norm_b):
            Bx, Cx, Hx, Wx = x.shape
            rows = jnp.transpose(x, (0, 2, 3, 1)).reshape(Bx * Hx, Wx, Cx)
            cols = jnp.transpose(x, (0, 3, 2, 1)).reshape(Bx * Wx, Hx, Cx)
            yr = _ssm1d(rows, *rp, False) + _ssm1d(rows, *rp, True)
            yc = _ssm1d(cols, *cp, False) + _ssm1d(cols, *cp, True)
            yr = jnp.transpose(yr.reshape(Bx, Hx, Wx, Cx), (0, 3, 1, 2))
            yc = jnp.transpose(yc.reshape(Bx, Wx, Hx, Cx), (0, 3, 2, 1))
            y = (yr + yc) * 0.25
            mean = x.mean(axis=1, keepdims=True)
            var = ((x - mean) ** 2).mean(axis=1, keepdims=True)
            xn = (x - mean) / jnp.sqrt(var + EPS)
            xn = xn * norm_w[None, :, None, None] + norm_b[None, :, None, None]
            h1 = jax.nn.gelu(jnp.einsum('bchw,oc->bohw', xn, g1_w) + g1_b[None, :, None, None], approximate=False)
            g = jax.nn.sigmoid(jnp.einsum('bghw,cg->bchw', h1, g2_w) + g2_b[None, :, None, None])
            return g * y + (1.0 - g) * x
        rp = (row_a_logit, row_U, row_V, row_Win, row_bin, row_Wg, row_bg, row_Wout, row_bout, row_Wskip, row_bskip)
        cp = (col_a_logit, col_U, col_V, col_Win, col_bin, col_Wg, col_bg, col_Wout, col_bout, col_Wskip, col_bskip)
        return _forward(x, rp, cp, g1_w, g1_b, g2_w, g2_b, norm_w, norm_b)

    def _L1_attn_ref(x, Wq, bq, Wk, bk, Wv, bv, Wo, bo):
        import jax, jax.numpy as jnp
        import numpy as np
        H, D = (6, 32)
        WIN = 33
        PAD = (WIN - 1) // 2
        B, L, E = x.shape
        scale = 1.0 / np.sqrt(D).astype(np.float32)

        def proj(W, b):
            return (x @ W + b).reshape(B, L, H, D).transpose(0, 2, 1, 3)
        Q, K, V = (proj(Wq, bq), proj(Wk, bk), proj(Wv, bv))
        s_cls = jnp.einsum('bhqd,bhkd->bhqk', Q[:, :, :1], K) * scale
        out_cls = jnp.einsum('bhqk,bhkd->bhqd', jax.nn.softmax(s_cls, -1), V)
        Lr = L - 1
        pos = jnp.arange(1, L)
        idx = pos[:, None] + jnp.arange(WIN)[None, :] - PAD
        valid = (idx >= 1) & (idx < L)
        idxc = jnp.clip(idx, 0, L - 1)
        Kw = K[:, :, idxc]
        Vw = V[:, :, idxc]
        cls_k = jnp.broadcast_to(K[:, :, :1, None, :], (B, H, Lr, 1, D))
        cls_v = jnp.broadcast_to(V[:, :, :1, None, :], (B, H, Lr, 1, D))
        Kw = jnp.concatenate([Kw, cls_k], axis=3)
        Vw = jnp.concatenate([Vw, cls_v], axis=3)
        mask = jnp.concatenate([valid, jnp.ones((Lr, 1), bool)], axis=-1)
        s_rest = jnp.einsum('bhld,bhlwd->bhlw', Q[:, :, 1:], Kw) * scale
        s_rest = jnp.where(mask[None, None], s_rest, -jnp.inf)
        a_rest = jax.nn.softmax(s_rest, axis=-1)
        out_rest = jnp.einsum('bhlw,bhlwd->bhld', a_rest, Vw)
        out = jnp.concatenate([out_cls, out_rest], axis=2)
        out = out.transpose(0, 2, 1, 3).reshape(B, L, E)
        return out @ Wo + bo

    def _L1_ffn_ref(x, gate_w, gate_b, w1, b1, w2, b2):
        import jax, jax.numpy as jnp
        import numpy as np
        NUM_EXPERTS = 4
        TOP_K = 2
        DIM = 192
        HID = 4 * DIM
        scores = jnp.einsum('bsd,de->bse', x, gate_w) + gate_b
        probs = jax.nn.softmax(scores, axis=-1)
        topk_vals, topk_idx = jax.lax.top_k(probs, TOP_K)
        mask = jnp.sum(jax.nn.one_hot(topk_idx, NUM_EXPERTS, dtype=probs.dtype), axis=-2)
        masked = probs * mask
        masked = masked / (jnp.sum(masked, axis=-1, keepdims=True) + 1e-09)
        h = jax.nn.gelu(jnp.einsum('bsd,edh->ebsh', x, w1) + b1[:, None, None, :], approximate=False)
        y = jnp.einsum('ebsh,ehd->ebsd', h, w2) + b2[:, None, None, :]
        out = jnp.einsum('bse,ebsd->bsd', masked, y)
        return out

    def _gn(v, G=32, eps=1e-05):
        B_, C_, H_, W_ = v.shape
        g = v.reshape(B_, G, C_ // G, H_, W_)
        m = jnp.mean(g, axis=(2, 3, 4), keepdims=True)
        s = jnp.var(g, axis=(2, 3, 4), keepdims=True)
        return ((g - m) / jnp.sqrt(s + eps)).reshape(v.shape)

    def _ln_c(v, eps=1e-06):
        m = jnp.mean(v, axis=1, keepdims=True)
        s = jnp.var(v, axis=1, keepdims=True)
        return (v - m) / jnp.sqrt(s + eps)

    def _ln_t(v, eps=1e-05):
        m = jnp.mean(v, axis=-1, keepdims=True)
        s = jnp.var(v, axis=-1, keepdims=True)
        return (v - m) / jnp.sqrt(s + eps)

    def _to_tokens(v):
        B_, C_, H_, W_ = v.shape
        return v.reshape(B_, C_, H_ * W_).transpose(0, 2, 1)

    def _from_tokens(t, like):
        B_, C_, H_, W_ = like.shape
        return t.transpose(0, 2, 1).reshape(B_, C_, H_, W_)
    x = x + _L0_conv_ref(_gn(x), L0_conv_row_a_logit, L0_conv_row_U, L0_conv_row_V, L0_conv_row_Win, L0_conv_row_bin, L0_conv_row_Wg, L0_conv_row_bg, L0_conv_row_Wout, L0_conv_row_bout, L0_conv_row_Wskip, L0_conv_row_bskip, L0_conv_col_a_logit, L0_conv_col_U, L0_conv_col_V, L0_conv_col_Win, L0_conv_col_bin, L0_conv_col_Wg, L0_conv_col_bg, L0_conv_col_Wout, L0_conv_col_bout, L0_conv_col_Wskip, L0_conv_col_bskip, L0_conv_g1_w, L0_conv_g1_b, L0_conv_g2_w, L0_conv_g2_b, L0_conv_norm_w, L0_conv_norm_b)
    t = _to_tokens(x)
    t = t + _L1_attn_ref(_ln_t(t), L1_attn_Wq, L1_attn_bq, L1_attn_Wk, L1_attn_bk, L1_attn_Wv, L1_attn_bv, L1_attn_Wo, L1_attn_bo)
    t = t + _L1_ffn_ref(_ln_t(t), L1_ffn_gate_w, L1_ffn_gate_b, L1_ffn_w1, L1_ffn_b1, L1_ffn_w2, L1_ffn_b2)
    x = _from_tokens(t, x)
    return x

_drawn_inputs = setup_inputs


def setup_inputs(seed=0):
    import zlib

    import numpy as np

    out = dict(_drawn_inputs(seed))
    spreads = {'L0_conv_row_a_logit': (0.0, 0.8),
     'L0_conv_row_bin': (0.0, 0.1),
     'L0_conv_row_bg': (0.0, 0.8),
     'L0_conv_row_bout': (0.0, 0.284),
     'L0_conv_row_bskip': (0.0, 0.324),
     'L0_conv_col_a_logit': (0.0, 0.8),
     'L0_conv_col_bin': (0.0, 0.279),
     'L0_conv_col_bg': (0.0, 0.8),
     'L0_conv_col_bout': (0.0, 0.299),
     'L0_conv_col_bskip': (0.0, 0.1),
     'L0_conv_g1_b': (0.0, 0.313),
     'L0_conv_g2_b': (0.0, 0.287),
     'L0_conv_norm_w': (1.0, 0.2),
     'L0_conv_norm_b': (0.0, 0.387),
     'L1_ffn_gate_b': (0.0, 0.1),
     'L1_ffn_b1': (0.0, 0.1),
     'L1_ffn_b2': (0.0, 0.1)}
    factors = {'L0_conv_row_U': 8.0,
     'L0_conv_row_V': 8.0,
     'L0_conv_col_U': 8.0,
     'L0_conv_col_V': 8.0,
     'L1_attn_bq': 25.26,
     'L1_attn_bk': 64.0,
     'L1_attn_bv': 3.599,
     'L1_attn_bo': 3.735}
    for name, (base, spread) in spreads.items():
        noise = np.random.default_rng([zlib.crc32(name.encode()), seed]).standard_normal(out[name].shape)
        drawn = base * np.exp(spread * noise) if base else spread * noise
        out[name] = jnp.asarray(drawn.astype(out[name].dtype))
    for name, factor in factors.items():
        out[name] = (out[name] * factor).astype(out[name].dtype)
    return out
```

```python
from contextlib import ExitStack

import concourse.bass as bass
from concourse import mybir

F32 = mybir.dt.float32
F16 = mybir.dt.float16
BF16 = mybir.dt.bfloat16
ALU = mybir.AluOpType
ACT = mybir.ActivationFunctionType
AX = mybir.AxisListType

B, C, GH, GW = 16, 192, 32, 32
T = GH * GW
NT = T // 128
NP = NT // 2
HC = C // 2
S = 16
KP, KC = 128 // S, GW // (128 // S)
HEADS, HD = 6, 32
HH = HEADS // 2
PAD = 16
QB = 93
NB = (T - 1) // QB
KW = QB + 2 * PAD
KS = KW + 1
QS = QB + 1
E, HID = 4, 768
HK = HID // 128
NH = 512
NHALF = T // NH
GROUP = C // 32
NCHUNK = NHALF * E * HK

X_UP, W_UP, H_UP = 1024.0, 64.0, 8.0
NEG = -1e30

PER = dict(
    x_loaded=16, gn_channel=1, gn_mean=1, gn_spread=1, gn_var=1, gn_eps=1, gn_rstd=1, xg_ready=2, xs_ready=2,
    proj_done=1, tanh_done=1, gu_ready=2, gu_moved=16 * 2 * KP, scan_done=1, hs_copied=1, hs_moved=16 * 2 * KP,
    hs_permuted=1, hs_placed=16, xgT_done=NP, stats_read=NP, h1_done=1, mixln_eps=1, mixln_rstd=1, h1_pre=1,
    h1_gelu=1, h1T_done=1, h1T_copied=1, mix_done=NP, mix_tanh=NP, mixed=NP,
    ln1_eps=1, ln1_rstd=1, xn1_ready=1, xn1T_done=1, win_act=1, win_dve=1, piece_done=18, piece_act=9, piece_dve=9,
    score_done=2 * NB, max_done=2 * NB, exp_done=2 * NB, pT_done=2 * NB, pT_copied=2 * NB, pv_done=NB,
    o_normed=NB, cls_weight=1, cls_exp=1, cls_coef=1, cls_mult=1, cls_sum=1, oT_done=6, oT_copied=6,
    wo_done=NP, x2_ready=NP, ln2_eps=1, ln2_rstd=1, xn2_ready=1, xn2T_done=1, xh_ready=2, xl_ready=2,
    route_done=1, route_shift=1, route_exp=1, gates_ready=1,
    ffn1_done=NCHUNK, gelu_done=NCHUNK, hh_ready=NCHUNK, hl_ready=NCHUNK, ffn2_chunk=NCHUNK,
    ffn_added=NHALF * E, outT_done=1, out_act=1, out_dve=1, out_stored=16,
)


def window_view(t, offset, dims):
    base = t[:]
    return bass.AP(tensor=base.tensor, offset=base.offset + offset, ap=[[base.ap[0][0], dims[0]]] + dims[1:])


def hybrid_kernel(nc, x, proj_w, y_wa, y_wb, y_scale, eye, gavg, cavg, norm_w, norm_b, g1_wT, g1_b, g2_wT, bias_row,
                  scan_v, scan_u, scan_a, wq, wk, wv, wo, bq, bk, bv, mask, w1a, w1b, w2, b1, gate_wa, gate_wb,
                  gate_b, before, after, out, powers):
    ctx = ExitStack()
    with ctx:
        def sb(name, shape, dt=F32):
            return ctx.enter_context(nc.sbuf_tensor(name, shape, dt))

        def sem(name):
            return ctx.enter_context(nc.semaphore(name))

        EYE = sb("EYE", [128, 128])
        EYEB = sb("EYEB", [QS, QS], BF16)
        GAVG = sb("GAVG", [HC, HC])
        MASKB = sb("MASKB", [QS, 3, HH * KS], BF16)
        PROJ = sb("PROJ", [97, 2, 128])
        WY = sb("WY", [113, 2, C])
        WG1 = sb("WG1", [HC, 2, 32])
        BG1 = sb("BG1", [128, 32])
        WG2 = sb("WG2", [128, 4, C])
        SCAN = sb("SCAN", [128, 2, 2 * KC - 1, 128])
        WQ, WK, WV, WO = (sb(n, [HC, 2, C]) for n in ("WQ", "WK", "WV", "WO"))
        BQ, BQS, BK, BV = (sb(n, [HC, 2]) for n in ("BQ", "BQS", "BK", "BV"))
        ONES3 = sb("ONES3", [3, 128], BF16)
        ROWS3 = sb("ROWS3", [3, 6 * C], BF16)
        W1AH = sb("W1AH", [128, E * HID], F16)
        W1AL = sb("W1AL", [128, E * HID], F16)
        W1B = sb("W1B", [128, E * HID], F16)
        W2H = sb("W2H", [128, E * HK, C], F16)
        W2L = sb("W2L", [128, E * HK, C], F16)
        B1 = sb("B1", [128, E * HK])
        GWAH, GWAL, GWB = (sb(n, [128, E], F16) for n in ("GWAH", "GWAL", "GWB"))
        GB = sb("GB", [128, E])
        BEFORE, AFTER = sb("BEFORE", [128, E, E]), sb("AFTER", [128, E, E])
        MHALF = sb("MHALF", [128, 8])
        SPARES = sb("SPARES", [1, 2])
        SPARE, PSPARE = SPARES[:, 0:1], SPARES[:, 1:2]

        XR = sb("XR", [HC, 2, T])
        XG = sb("XG", [113, 2, T])
        XS = sb("XS", [HC, 2, T])
        GST = sb("GST", [HC, 2, 2, 6])
        MV = sb("MV", [HC, 2, 2])
        GM, GD, GV, GR, GR1, GNB = (sb(n, [HC, 2]) for n in ("GM", "GD", "GV", "GR", "GR1", "GNB"))
        TGU = sb("TGU", [128, T])
        TG, GU = TGU[64:128, :], TGU[0:64, :]
        GUP = sb("GUP", [128, 2, KC, GW])
        HSP = sb("HSP", [128, 2, KC, GW])
        TST = sb("TST", [128, NT, 6])
        TMV = sb("TMV", [128, NT, 2])
        TV, TR = sb("TV", [128, NT]), sb("TR", [128, NT])
        H1 = sb("H1", [128, NT, 32])
        H1T = sb("H1T", [128, 2, 128])
        TM = sb("TM", [128, 2 * C])
        EM = sb("EM", [128, 2 * C])
        X1 = sb("X1", [128, NT, C])
        XN = sb("XN", [128, NT, 256])
        HST = XN[0:S].rearrange("s a b -> s (a b)")[:, 0:T].rearrange("s (w h) -> s w h", w=GW)
        HST2 = X1[0:S].rearrange("s a b -> s (a b)")[:, 0:T]
        XW = sb("XW", [HC, 2, NB, KS])
        QT = sb("QT", [HC, 2, NB, QS])
        KBD = sb("KBD", [HC, 2, NB, HH, KS])
        VW = sb("VW", [KS, NB, C])
        NMX = sb("NMX", [QS, NB, 2, HH])
        DEN = sb("DEN", [QS, NB, 2, HH])
        RDEN = sb("RDEN", [QS, NB, 2, HH])
        PS = sb("PS", [QS, 2, HH, KS])
        PT = sb("PT", [KS, 2, HH, QS])
        OS = sb("OS", [QS, NB, C])
        OT = XG[0:HC, :, :]
        CM = sb("CM", [1, HEADS])
        CW = sb("CW", [1, NB, HEADS])
        CSUM = sb("CSUM", [1, HEADS])
        CP = VW[0:1, :, :]
        CO = sb("CO", [1, C])
        XH = sb("XH", [128, 2, T], F16)
        XL = sb("XL", [128, 2, T], F16)
        SC = sb("SC", [128, NT, E])
        SE = sb("SE", [128, NT, E])
        SM = sb("SM", [128, NT])
        CMPA, CMPB = sb("CMPA", [128, NT, E, E]), sb("CMPB", [128, NT, E, E])
        WIN = sb("WIN", [128, NT, E])
        GATE = sb("GATE", [128, NT, E])
        HF = sb("HF", [128, 2, NH])
        HHI = sb("HHI", [128, 2, NH], F16)
        HLO = sb("HLO", [128, 2, NH], F16)
        OUT = XS

        PSUM = ctx.enter_context(nc.psum_tensor("PSUM", [128, 8, 512], F32))
        Q = PSUM[:, 0:4, :]

        weights_ready = sem("weights_ready")
        with ExitStack() as setup:
            def ssem(name):
                return setup.enter_context(nc.semaphore(name))

            loaded, dve_step, act_step, pe_step = ssem("loaded"), ssem("dve_step"), ssem("act_step"), ssem("pe_step")
            powers_stored, scan_loaded, rows_split, rows_moved = (
                ssem(n) for n in ("powers_stored", "scan_loaded", "rows_split", "rows_moved"))
            pool_step = ssem("pool_step")
            STG = setup.enter_context(nc.sbuf_tensor("STG", [128, 1, 8], F32))
            Y_A, Y_B = XN[0:113, 0:2, 0:C], XN[0:113, 2:4, 0:C]
            YSC = SM[0:113, 0:1]
            NW, NBI, CAVG = STG[0:HC, 0, 0:2], STG[0:HC, 0, 2:4], XN[0:HC, 4, 0:HC]
            G1W = X1[0:HC, 0, 0:64].rearrange("p (j o) -> p j o", j=2)
            G1N = X1[0:HC, 1, 0:64].rearrange("p (j o) -> p j o", j=2)
            NBB = X1[0:HC, 2:4, 0:128]
            G1B = XN[0:1, 5, 0:32]
            ONE1 = XN[0:1, 5, 32:160]
            PW = OS[0:2 * S, :, :].rearrange("p a b -> p (a b)")[:, 0:32 * 32].rearrange("p (k s) -> p k s", k=32)
            MIR = OT[0:2 * S, :, :].rearrange("p a b -> p (a b)")[:, 0:63 * 32].rearrange("p (k s) -> p k s", k=63)
            SV = GUP[0:S, 0, 0, 0:2 * S]
            SU = GUP[0:S, 0, 1, 0:2 * S]
            SA = GUP[0:2 * S, 0, 2, 0:1]
            SIG = GUP[0:2 * S, 0, 2, 1:2]
            DIA = GUP[0:2 * S, 0, 3, 0:2 * S]
            AT = GUP[0:2 * S, 1, 0, 0:2 * S]
            ROW = XR[0:1, 0:2, :].rearrange("p a b -> p (a b)")[:, 0:6 * C]
            ROWR = XS[0:1, 0:2, :].rearrange("p a b -> p (a b)")[:, 0:6 * C]
            ROWP = QT[0:1, :, :, :].rearrange("p a b c -> p (a b c)")[:, 0:9 * C].bitcast(BF16)
            MSK = OS[0:QS, 6:12, :] if False else QT
            N_LOADS = 0
            loads = []
            W2S = KBD
            with nc.Block() as block:
                big = XG[0:1, 0, 0:1]
                PIECE = 1536
                STAGE = [X1[:].rearrange("p a b -> p (a b)"), XN[:].rearrange("p a b -> p (a b)")[:, 0:PIECE]]
                small = [
                    (EYE[:], eye), (GAVG[:], gavg), (PROJ[:], proj_w), (WG2[:], g2_wT),
                    (WQ[:], wq), (WK[:], wk), (WV[:], wv), (WO[:], wo), (BQ[:], bq), (BK[:], bk), (BV[:], bv),
                    (B1[:], b1), (GB[:], gate_b), (BEFORE[:], before), (AFTER[:], after),
                    (Y_A, y_wa), (Y_B, y_wb), (YSC, y_scale), (CAVG, cavg), (NW, norm_w), (NBI, norm_b),
                    (G1W, g1_wT), (G1B, g1_b), (SV, scan_v), (SU, scan_u), (SA, scan_a), (ROW, bias_row),
                    (VW[0:QS, 0:6, :].rearrange("p a b -> p (a b)")[:, 0:3 * HH * KS], mask),
                    (OT.rearrange("p a b -> p (a b)")[0:1, 0:1], None),
                    (HF[:, 0, 0:E], gate_wa), (HF[:, 0, 4:4 + E], gate_wb),
                ]
                small = [s for s in small if s[1] is not None]
                pieces = []
                for k in range(E * HID // PIECE):
                    pieces.append(("a", k, w1a[:, k * PIECE:(k + 1) * PIECE]))
                    pieces.append(("b", k, w1b[:, k * PIECE:(k + 1) * PIECE]))
                for k in range(E * HK * C // PIECE):
                    pieces.append(("2", k, w2[:, k * PIECE:(k + 1) * PIECE]))
                W2HF = W2H[:].rearrange("p a b -> p (a b)")
                W2LF = W2L[:].rearrange("p a b -> p (a b)")
                piece_loaded, piece_free = [ssem("piece_loaded0"), ssem("piece_loaded1")], ssem("piece_free")
                setup_done = ssem("setup_done")

                @block.sync
                def _(sp):
                    for dst, src in small:
                        sp.dma_start(dst, src).then_inc(loaded, 16)
                    sp.wait_ge(rows_split, 1)
                    sp.dma_start(ROWS3[:], ROWP.rearrange("p (k n) -> p k n", k=3)).then_inc(rows_moved, 16)
                    sp.wait_ge(powers_stored, 1)
                    sp.dma_start(powers, MIR).then_inc(scan_loaded, 16)
                    sp.wait_ge(scan_loaded, 16)
                    for kind in range(2):
                        for i in range(KP):
                            src = bass.AP(tensor=powers.tensor,
                                          offset=powers.offset + kind * S * 63 * 32 + kind * S + (31 - 24 - i) * 32,
                                          ap=[[63 * 32, S], [KP * 32, 2 * KC - 1], [32, KP], [1, S]])
                            for d in range(2 * KC - 1):
                                s1 = bass.AP(tensor=powers.tensor, offset=src.offset + d * KP * 32,
                                             ap=[[63 * 32, S], [32, KP], [1, S]])
                                sp.dma_start(SCAN[S * i:S * i + S, kind, d, :].rearrange("p (k s) -> p k s", k=KP), s1
                                             ).then_inc(scan_loaded, 16)
                    sp.wait_ge(setup_done, 1)
                    for n, (_, _, src) in enumerate(pieces):
                        if n >= 2:
                            sp.wait_ge(piece_free, n - 1)
                        sp.dma_start(STAGE[n % 2], src).then_inc(piece_loaded[n % 2], 16)
                    sp.wait_ge(scan_loaded, 16 * (1 + 2 * KP * (2 * KC - 1)))
                    sp.wait_ge(rows_moved, 16)

                n_dve = [0]
                marks = {}

                @block.vector
                def _(dve):
                    def link(ins):
                        n_dve[0] += 1
                        ins.then_inc(dve_step, 1)
                        dve.wait_ge(dve_step, n_dve[0])

                    for t in (XW, KBD, XG):
                        dve.memset(t[:], 0.0)
                    dve.memset(ONES3[:], 1.0)
                    dve.memset(SPARES[:], 0.0)
                    dve.memset(ONE1, 1.0)
                    link(dve.memset(MHALF[:], -0.5))
                    link(dve.memset(XG[96:97, :, :], 1.0))
                    dve.wait_ge(loaded, 16 * len(small))
                    dve.tensor_copy(EYEB[:], EYE[0:QS, 0:QS])
                    dve.tensor_copy(MASKB[:].rearrange("p a b -> p (a b)"),
                                    VW[0:QS, 0:6, :].rearrange("p a b -> p (a b)")[:, 0:3 * HH * KS])
                    dve.tensor_scalar(BQS[:], BQ[:], HD ** -0.5, None, ALU.mult)
                    link(dve.tensor_tensor(Y_A, Y_A, Y_B, ALU.add))
                    link(dve.tensor_scalar(WY[:], Y_A, YSC, None, ALU.mult))
                    for j in range(2):
                        link(dve.tensor_tensor(WY[0:HC, j, j * HC:(j + 1) * HC], WY[0:HC, j, j * HC:(j + 1) * HC],
                                               EYE[0:HC, 0:HC], ALU.subtract))
                    for j in range(2):
                        link(dve.tensor_scalar(G1N[:, j, :], G1W[:, j, :], NW[:, j:j + 1], None, ALU.mult))
                        link(dve.tensor_scalar(NBB[:, j, :], XG[0:HC, 0, 0:128], NBI[:, j:j + 1], None, ALU.add))
                    marks["g1"] = n_dve[0]
                    dve.wait_ge(pe_step, 2)
                    link(dve.tensor_copy(BG1[:], PSUM[:, 1, 0:32]))
                    for j in range(2):
                        link(dve.tensor_tensor(WG1[:, j, :], G1N[:, j, :], PSUM[0:HC, 0, 0:32], ALU.subtract))
                    link(dve.tensor_scalar(ROW[:, 2 * C:], ROW[:, 2 * C:], W_UP * H_UP, None, ALU.mult))
                    n = 6 * C
                    link(dve.tensor_copy(ROWP[:, 0:n], ROW))
                    link(dve.tensor_tensor(ROWR, ROW, ROWP[:, 0:n], ALU.subtract))
                    link(dve.tensor_copy(ROWP[:, n:2 * n], ROWR))
                    link(dve.tensor_tensor(ROWR, ROWR, ROWP[:, n:2 * n], ALU.subtract))
                    dve.tensor_copy(ROWP[:, 2 * n:3 * n], ROWR).then_inc(rows_split, 1)
                    dve.wait_ge(act_step, 1)
                    link(dve.tensor_scalar(SIG, SIG, 0.5, 0.5, ALU.mult, ALU.add))
                    link(dve.tensor_scalar(DIA, EYE[0:2 * S, 0:2 * S], SIG, None, ALU.mult))
                    link(dve.tensor_copy(PW[:, 0, :], EYE[0:2 * S, 0:2 * S]))
                    dve.wait_ge(pe_step, 3)
                    link(dve.tensor_tensor(PW[:, 1, :], DIA, PSUM[0:2 * S, 2, 0:2 * S], ALU.add))
                    marks["power"] = n_dve[0]
                    m, seen = 1, 3
                    while m < 32:
                        seen += 1
                        dve.wait_ge(pe_step, seen)
                        link(dve.tensor_copy(AT, PSUM[0:2 * S, 3, 0:2 * S]))
                        k = min(m, 31 - m)
                        if k:
                            seen += 1
                            dve.wait_ge(pe_step, seen)
                            link(dve.tensor_copy(PW[:, m + 1:m + 1 + k, :],
                                                 PSUM[0:2 * S, 4, 0:32 * k].rearrange("p (k s) -> p k s", k=k)))
                        m *= 2
                    link(dve.tensor_copy(MIR[:, 31:63, :], PW))
                    for k in range(1, 32):
                        dve.tensor_copy(MIR[:, 31 - k, :], PW[:, k, :])
                    link(dve.tensor_scalar(MIR[:, 31, :], PW[:, 0, :], 2.0, None, ALU.mult))
                    dve.sem_inc(powers_stored, 1) if False else None
                    dve.memset(STG[0:1, 0, 4:5], 0.0).then_inc(powers_stored, 1)
                    link(dve.tensor_scalar(GWAH[:], HF[:, 0, 0:E], W_UP, None, ALU.mult))
                    link(dve.scalar_tensor_tensor(GWAL[:], HF[:, 0, 0:E], W_UP, GWAH[:], ALU.mult, ALU.subtract))
                    link(dve.tensor_scalar(GWB[:], HF[:, 0, 4:8], W_UP, None, ALU.mult))
                    link(dve.scalar_tensor_tensor(GWB[64:128], HF[64:128, 0, 4:8], W_UP, GWB[64:128], ALU.mult,
                                                  ALU.subtract))
                    dve.memset(STG[0:1, 0, 5:6], 0.0).then_inc(setup_done, 1)
                    for n, (kind, k, _) in enumerate(pieces):
                        dve.wait_ge(piece_loaded[n % 2], 16 * (n // 2 + 1))
                        sl = slice(k * PIECE, (k + 1) * PIECE)
                        hi = {"a": W1AH, "b": W1B, "2": W2HF}[kind][:, sl]
                        link(dve.tensor_scalar(hi, STAGE[n % 2], W_UP, None, ALU.mult))
                        if kind == "b":
                            last = dve.scalar_tensor_tensor(W1B[64:128, sl], STAGE[n % 2][64:128], W_UP,
                                                            W1B[64:128, sl], ALU.mult, ALU.subtract)
                        else:
                            lo = {"a": W1AL, "2": W2LF}[kind][:, sl]
                            last = dve.scalar_tensor_tensor(lo, STAGE[n % 2], W_UP, hi, ALU.mult, ALU.subtract)
                        last.then_inc(piece_free, 1)
                    dve.wait_ge(piece_free, len(pieces))
                    dve.memset(STG[0:1, 0, 6:7], 0.0).then_inc(weights_ready, 1)

                @block.scalar
                def _(act):
                    act.wait_ge(loaded, 16 * len(small))
                    act.activation(SIG, SA, ACT.Tanh, scale=0.5).then_inc(act_step, 1)

                @block.tensor
                def _(pe):
                    pe.wait_ge(loaded, 16 * len(small))
                    pe.wait_ge(dve_step, marks["g1"])
                    for j in range(2):
                        mm = pe.matmul(PSUM[0:HC, 0, 0:32], CAVG, G1N[:, j, :], start=(j == 0), stop=(j == 1))
                    mm.then_inc(pe_step, 1)
                    pe.matmul(PSUM[:, 1, 0:32], ONE1, G1B, start=True, stop=False)
                    for j in range(2):
                        mm = pe.matmul(PSUM[:, 1, 0:32], NBB[:, j, :], G1W[:, j, :], start=False, stop=(j == 1))
                    mm.then_inc(pe_step, 1)
                    pe.matmul(PSUM[0:2 * S, 2, 0:2 * S], SV, SU, start=True, stop=True).then_inc(pe_step, 1)
                    m = 1
                    steps = marks["power"]
                    pe.wait_ge(dve_step, steps)
                    while m < 32:
                        pe.transpose(PSUM[0:2 * S, 3, 0:2 * S], PW[:, m, :], EYE[0:2 * S, 0:2 * S]).then_inc(pe_step, 1)
                        steps += 1
                        pe.wait_ge(dve_step, steps)
                        k = min(m, 31 - m)
                        if k:
                            pe.matmul(PSUM[0:2 * S, 4, 0:32 * k], AT, PW[:, 1:1 + k, :], start=True, stop=True
                                      ).then_inc(pe_step, 1)
                            steps += 1
                            pe.wait_ge(dve_step, steps)
                        m *= 2

        s = {n: sem("i_" + n) for n in PER}
        dve_link = sem("dve_link")

        def at(name, i, k):
            return i * PER[name] + k

        def bank(n):
            return PSUM[:, n, :]

        def windows(copy, j, give):
            copy(XW[:, j, 1:NB - 1, 0:KW],
                 window_view(PSUM, j * T + QB - PAD + 1, [HC, [QB, NB - 2], [1, KW]]))
            copy(XW[:, j, 0, PAD - 1:KW], window_view(PSUM, j * T, [HC, [1, KW - PAD + 1]]))
            last = (NB - 1) * QB - PAD + 1
            copy(XW[:, j, NB - 1, 0:T - last], window_view(PSUM, j * T + last, [HC, [1, T - last]]))
            copy(XW[:, j, :, KW], window_view(PSUM, j * T, [HC, [0, NB]])).then_inc(give, 1)

        SPANS = [(0, 4), (4, 8), (8, NB)]

        def evacuate_piece(eng, n, give):
            src = bank(n % 4)
            is_act = eng is act_engine
            if n < 6:
                oh, (b0, b1) = n // 3, SPANS[n % 3]
                k = b1 - b0
                parts = [(QT[:, oh, b0:b1, 1:QS], src[0:HC, 0:k * QB].rearrange("p (b q) -> p b q", b=k))]
                if n % 3 == 2:
                    col = src[0:HC, 400:401].broadcast_to((HC, NB))
                    parts.append((QT[:, oh, :, 0], col))
                for dst, ps in parts:
                    if is_act:
                        last = eng.activation(dst, ps, ACT.Identity, bias=BQS[:, oh:oh + 1], scale=HD ** -0.5)
                    else:
                        last = eng.tensor_scalar(dst, ps, BQ[:, oh:oh + 1], HD ** -0.5, ALU.add, ALU.mult)
            elif n < 12:
                oh, (b0, b1) = (n - 6) // 3, SPANS[n % 3]
                k = b1 - b0
                for h in range(HH):
                    p = slice(h * HD, (h + 1) * HD)
                    dst = KBD[p, oh, b0:b1, h, :]
                    ps = src[p, 0:k * KS].rearrange("p (b q) -> p b q", b=k)
                    if is_act:
                        last = eng.activation(dst, ps, ACT.Identity, bias=BK[p, oh:oh + 1])
                    else:
                        last = eng.tensor_scalar(dst, ps, BK[p, oh:oh + 1], None, ALU.add)
            else:
                b0 = 2 * (n - 12)
                k = min(2, NB - b0)
                dst = VW[:, b0:b0 + k, :]
                ps = src[0:KS, 0:k * C].rearrange("p (b q) -> p b q", b=k)
                last = eng.copy(dst, ps) if is_act else eng.tensor_copy(dst, ps)
            last.then_inc(give, 1)

        act_engine = nc.scalar
        OSPANS = [(0, 4), (4, 8), (8, NB)]

        def evacuate_oT(eng, n, i):
            oh, (b0, b1) = n // 3, OSPANS[n % 3]
            eng.wait_ge(s["oT_done"], at("oT_done", i, n + 1))
            src = bank(n % 4)
            w = (b1 - b0) * QB
            parts = [(OT[:, oh, 1 + b0 * QB:1 + b1 * QB], src[0:HC, 0:w])]
            if n % 3 == 2:
                parts.append((OT[:, oh, 0:1], src[0:HC, 400:401]))
            for dst, ps in parts:
                if eng is act_engine:
                    last = eng.activation(dst, ps, ACT.Identity, bias=BV[:, oh:oh + 1])
                else:
                    last = eng.tensor_scalar(dst, ps, BV[:, oh:oh + 1], None, ALU.add)
            last.then_inc(s["oT_copied"], 1)

        block = ctx.enter_context(nc.Block())

        @block.sync
        def _(sp):
            with sp.Fori(0, B) as i:
                for kind in range(2):
                    sp.wait_ge(s["gu_ready"], at("gu_ready", i, kind + 1))
                    src = GU[32 * kind:32 * kind + S, :].rearrange("s (c i n) -> s c i n", c=KC, i=KP)
                    for k in range(KP):
                        sp.dma_start(GUP[S * k:S * k + S, kind, :, :], src[:, :, k, :]).then_inc(s["gu_moved"], 16)
                sp.wait_ge(s["hs_copied"], at("hs_copied", i, 1))
                for kind in range(2):
                    dst = (HST.rearrange("s (c i) n -> s c i n", i=KP) if kind == 0 else
                           XG[97:113, 1, :].rearrange("s (c i n) -> s c i n", c=KC, i=KP))
                    for k in range(KP):
                        sp.dma_start(dst[:, :, k, :], HSP[S * k:S * k + S, kind, :, :]).then_inc(s["hs_moved"], 16)
                sp.wait_ge(s["hs_permuted"], at("hs_permuted", i, 1))
                sp.dma_start(XG[97:113, 0, :], HST2).then_inc(s["hs_placed"], 16)

        @block.gpsimd
        def _(pool):
            with pool.Fori(0, B) as i:
                def rstd(dst, src, width, wait, give):
                    pool.wait_ge(s[wait], at(wait, i, 1))
                    pool.tensor_tensor(dst, src, MHALF[0:dst.shape[0], 0:width], ALU.pow).then_inc(s[give], 1)

                rstd(GR[:], GV[:], 2, "gn_eps", "gn_rstd")
                rstd(TR[:], TV[:], NT, "mixln_eps", "mixln_rstd")
                pool.wait_ge(s["hs_moved"], at("hs_moved", i, 16 * 2 * KP))
                pool.tensor_tensor(PSPARE, PSPARE, PSPARE, ALU.mult)
                pool.tensor_copy(HST2.rearrange("s (h w) -> s h w", h=GH), HST.rearrange("s w h -> s h w")
                                 ).then_inc(s["hs_permuted"], 1)
                rstd(TR[:], TV[:], NT, "ln1_eps", "ln1_rstd")
                pool.wait_ge(s["cls_coef"], at("cls_coef", i, 1))
                pool.tensor_tensor(CP.rearrange("p b (h d) -> p b h d", h=HEADS),
                                   OS[0:1, :, :].rearrange("p b (h d) -> p b h d", h=HEADS),
                                   CW[:].unsqueeze(3).broadcast_to((1, NB, HEADS, HD)), ALU.mult
                                   ).then_inc(s["cls_mult"], 1)
                rstd(TR[:], TV[:], NT, "ln2_eps", "ln2_rstd")

        @block.scalar
        def _(act):
            with act.Fori(0, B) as i:
                act.wait_ge(s["xs_ready"], at("xs_ready", i, 0))
                act.dma_start(XR[:], x[bass.ds(i, 1)].rearrange("o p j t -> (o p) j t")).then_inc(s["x_loaded"], 16)
                act.wait_ge(s["proj_done"], at("proj_done", i, 1))
                act.activation(TG.rearrange("p (a b) -> p a b", a=2), PSUM[64:128, 0:2, :], ACT.Tanh, scale=0.5
                               ).then_inc(s["tanh_done"], 1)
                act.wait_ge(s["h1_pre"], at("h1_pre", i, 1))
                act.activation(H1[:], H1[:], ACT.Gelu).then_inc(s["h1_gelu"], 1)
                act.wait_ge(s["scan_done"], at("scan_done", i, 1))
                act.activation(HSP[:].rearrange("p a b c -> p (a b c)"), PSUM[:, 2, 0:2 * KC * GW], ACT.Copy
                               ).then_inc(s["hs_copied"], 1)
                act.wait_ge(s["h1T_done"], at("h1T_done", i, 1))
                act.activation(H1T[:].rearrange("p a b -> p (a b)"), PSUM[:, 2, 0:256], ACT.Copy
                               ).then_inc(s["h1T_copied"], 1)
                for tp in range(NP):
                    act.wait_ge(s["mix_done"], at("mix_done", i, tp + 1))
                    if tp:
                        act.wait_ge(s["mixed"], at("mixed", i, tp))
                    act.activation(TM[:], PSUM[:, 0, 0:2 * C], ACT.Tanh, scale=0.5).then_inc(s["mix_tanh"], 1)
                act.wait_ge(s["xn1T_done"], at("xn1T_done", i, 1))
                windows(act.copy, 0, s["win_act"])
                for n in range(0, 18, 2):
                    act.wait_ge(s["piece_done"], at("piece_done", i, n + 1))
                    evacuate_piece(act, n, s["piece_act"])
                for n in range(2 * NB):
                    b, oh = n // 2, n % 2
                    act.wait_ge(s["max_done"], at("max_done", i, n + 1))
                    if n >= 2:
                        act.wait_ge(s["pT_done"], at("pT_done", i, n - 1))
                    for h in range(HH):
                        e = act.activation(PS[:, n % 2, h, :], PSUM[0:QS, n % 2, h * KS:(h + 1) * KS], ACT.Exp,
                                           bias=NMX[:, b, oh, h:h + 1], accum_out=DEN[:, b, oh, h:h + 1])
                    e.then_inc(s["exp_done"], 1)
                act.wait_ge(s["cls_weight"], at("cls_weight", i, 1))
                act.activation(CW[:], CW[:], ACT.Exp).then_inc(s["cls_exp"], 1)
                for n in range(6):
                    if n % 2 == 0:
                        evacuate_oT(act, n, i)
                act.wait_ge(s["xn2T_done"], at("xn2T_done", i, 1))
                for a in range(2):
                    act.activation(XH[:, a, :].rearrange("p (a b) -> p a b", a=2), PSUM[:, 2 * a:2 * a + 2, :],
                                   ACT.Copy, scale=X_UP).then_inc(s["xh_ready"], 1)
                act.wait_ge(s["route_shift"], at("route_shift", i, 1))
                act.activation(SE[:], SC[:], ACT.Exp).then_inc(s["route_exp"], 1)
                for n in range(NCHUNK):
                    ek = n % (E * HK)
                    act.wait_ge(s["ffn1_done"], at("ffn1_done", i, n + 1))
                    if n >= 2:
                        act.wait_ge(s["hl_ready"], at("hl_ready", i, n - 1))
                    act.activation(HF[:, n % 2, :], PSUM[:, 4 + n % 2, :], ACT.Gelu, scale=1 / (X_UP * W_UP),
                                   bias=B1[:, ek:ek + 1]).then_inc(s["gelu_done"], 1)
                act.wait_ge(s["outT_done"], at("outT_done", i, 1))
                act.copy(OUT[:, 0, :].rearrange("p (a b) -> p a b", a=2), PSUM[0:HC, 0:2, :]).then_inc(s["out_act"], 1)
                act.wait_ge(s["out_act"], at("out_act", i, 1))
                act.wait_ge(s["out_dve"], at("out_dve", i, 1))
                act.dma_start(out[bass.ds(i, 1)].rearrange("o p j t -> (o p) j t"), OUT[:]
                              ).then_inc(s["out_stored"], 16)
            act.wait_ge(s["out_stored"], 16 * B)

        links = [0]
        LINKS = 44

        @block.vector
        def _(dve):
            with dve.Fori(0, B) as i:
                def link(ins):
                    links[0] += 1
                    ins.then_inc(dve_link, 1)
                    dve.wait_ge(dve_link, i * LINKS + links[0])

                def token_norm(src, eps, eps_sem, rstd_sem, give, twice=False):
                    for t in range(NT):
                        last = dve.bn_stats(TST[:, t, :], src[:, t, :])
                    link(last)
                    dve.memset(SPARE, 0.0)
                    for t in range(NT):
                        last = dve.bn_aggr(TMV[:, t, :], TST[:, t, :])
                    link(last)
                    dve.tensor_scalar(TV[:], TMV[:, :, 1], eps, None, ALU.add).then_inc(s[eps_sem], 1)
                    dve.wait_ge(s[rstd_sem], at(rstd_sem, i, 1))
                    for t in range(NT):
                        last = dve.tensor_scalar(XN[:, t, 0:C], src[:, t, :], TMV[:, t, 0:1], TR[:, t:t + 1],
                                                 ALU.subtract, ALU.mult)
                    if twice:
                        for t in range(NT):
                            last = dve.tensor_scalar(XN[:, t, C:256], src[:, t, 128:C], TMV[:, t, 0:1],
                                                     TR[:, t:t + 1], ALU.subtract, ALU.mult)
                    last.then_inc(s[give], 1)

                dve.wait_ge(s["x_loaded"], at("x_loaded", i, 16))
                for j in range(2):
                    for h in range(2):
                        last = dve.bn_stats(GST[:, j, h, :], XR[:, j, 512 * h:512 * h + 512])
                link(last)
                dve.memset(SPARE, 0.0)
                for j in range(2):
                    last = dve.bn_aggr(MV[:, j, :], GST[:, j, :, :].rearrange("p a b -> p (a b)"))
                last.then_inc(s["gn_channel"], 1)
                dve.wait_ge(s["gn_channel"], at("gn_channel", i, 1))
                dve.wait_ge(s["gn_mean"], at("gn_mean", i, 1))
                link(dve.tensor_copy(GM[:], PSUM[0:HC, 0, 0:2]))
                link(dve.tensor_tensor(GD[:], MV[:, :, 0], GM[:], ALU.subtract))
                link(dve.tensor_tensor(GD[:], GD[:], GD[:], ALU.mult))
                dve.tensor_tensor(GD[:], GD[:], MV[:, :, 1], ALU.add).then_inc(s["gn_spread"], 1)
                dve.wait_ge(s["gn_var"], at("gn_var", i, 1))
                dve.tensor_scalar(GV[:], PSUM[0:HC, 0, 2:4], 1e-5, None, ALU.add).then_inc(s["gn_eps"], 1)
                dve.wait_ge(s["gn_rstd"], at("gn_rstd", i, 1))
                link(dve.scalar_tensor_tensor(GNB[:], GM[:], -1.0, GR[:], ALU.mult, ALU.mult))
                link(dve.tensor_scalar(GR1[:], GR[:], 1.0, None, ALU.add))
                dve.wait_ge(s["mix_done"], at("mix_done", i, 0))
                for j in range(2):
                    dve.tensor_scalar(XG[0:HC, j, :], XR[:, j, :], GM[:, j:j + 1], GR[:, j:j + 1], ALU.subtract,
                                      ALU.mult).then_inc(s["xg_ready"], 1)
                dve.wait_ge(s["out_stored"], at("out_stored", i, 0))
                for j in range(2):
                    dve.tensor_scalar(XS[:, j, :], XR[:, j, :], GR1[:, j:j + 1], GNB[:, j:j + 1], ALU.mult,
                                      ALU.add).then_inc(s["xs_ready"], 1)
                dve.wait_ge(s["tanh_done"], at("tanh_done", i, 1))
                one = 1.0
                dve.scalar_tensor_tensor(GU[0:S, :].rearrange("p (w h) -> p h w", w=GW),
                                         TG[0:S, :].rearrange("p (h w) -> p h w", w=GW), one,
                                         PSUM[0:S, 0:2, :].rearrange("p a (h w) -> p (a h) w", w=GW),
                                         ALU.add, ALU.mult).then_inc(s["gu_ready"], 1)
                dve.scalar_tensor_tensor(GU[32:32 + S, :].rearrange("p (a b) -> p a b", a=2),
                                         TG[32:32 + S, :].rearrange("p (a b) -> p a b", a=2), one,
                                         PSUM[32:32 + S, 0:2, :],
                                         ALU.add, ALU.mult).then_inc(s["gu_ready"], 1)
                for tp in range(NP):
                    dve.wait_ge(s["xgT_done"], at("xgT_done", i, tp + 1))
                    for t in range(2):
                        last = dve.bn_stats(TST[:, 2 * tp + t, :], PSUM[:, tp % 2, t * C:(t + 1) * C])
                    last.then_inc(s["stats_read"], 1)
                dve.wait_ge(s["stats_read"], at("stats_read", i, NP))
                dve.memset(SPARE, 0.0)
                for t in range(NT):
                    last = dve.bn_aggr(TMV[:, t, :], TST[:, t, :])
                link(last)
                dve.tensor_scalar(TV[:], TMV[:, :, 1], 1e-6, None, ALU.add).then_inc(s["mixln_eps"], 1)
                dve.wait_ge(s["mixln_rstd"], at("mixln_rstd", i, 1))
                dve.wait_ge(s["h1_done"], at("h1_done", i, 1))
                link(dve.tensor_tensor(H1[:], PSUM[:, 3, 0:256].rearrange("p (t o) -> p t o", t=NT),
                                       TR[:].unsqueeze(2).broadcast_to((128, NT, 32)), ALU.mult))
                dve.tensor_tensor(H1[:], H1[:], BG1[:].unsqueeze(1).broadcast_to((128, NT, 32)), ALU.add
                                  ).then_inc(s["h1_pre"], 1)
                for tp in range(NP):
                    dve.wait_ge(s["mix_tanh"], at("mix_tanh", i, tp + 1))
                    link(dve.scalar_tensor_tensor(EM[:], TM[:], 1.0, PSUM[:, 1 + tp % 2, 0:2 * C], ALU.add, ALU.mult))
                    dve.scalar_tensor_tensor(X1[:, 2 * tp:2 * tp + 2, :].rearrange("p a b -> p (a b)"), EM[:], 0.5,
                                             PSUM[:, 3, 0:2 * C], ALU.mult, ALU.add).then_inc(s["mixed"], 1)
                dve.wait_ge(s["mixed"], at("mixed", i, NP))
                token_norm(X1, 1e-5, "ln1_eps", "ln1_rstd", "xn1_ready")
                dve.wait_ge(s["xn1T_done"], at("xn1T_done", i, 1))
                windows(dve.tensor_copy, 1, s["win_dve"])
                for n in range(1, 18, 2):
                    dve.wait_ge(s["piece_done"], at("piece_done", i, n + 1))
                    evacuate_piece(dve, n, s["piece_dve"])

                def after_scores(n):
                    b, oh = n // 2, n % 2
                    dve.wait_ge(s["pT_done"], at("pT_done", i, n + 1))
                    if n >= 2:
                        dve.wait_ge(s["pv_done"], at("pv_done", i, (n - 2) // 2))
                    dve.tensor_copy(PT[:, n % 2, :, :], PSUM[0:KS, 2 + n % 2, 0:HH * QS].rearrange(
                        "p (h q) -> p h q", h=HH)).then_inc(s["pT_copied"], 1)

                def normalize(b):
                    dve.wait_ge(s["exp_done"], at("exp_done", i, 2 * b + 2))
                    link(dve.reciprocal(RDEN[:, b, :, :], DEN[:, b, :, :]))
                    dve.wait_ge(s["pv_done"], at("pv_done", i, b + 1))
                    dve.tensor_tensor(OS[:, b, :].rearrange("p (h d) -> p h d", h=HEADS),
                                      PSUM[0:QS, 4 + b % 2, 0:C].rearrange("p (h d) -> p h d", h=HEADS),
                                      RDEN[:, b, :, :].rearrange("p a h -> p (a h)").unsqueeze(2).broadcast_to(
                                          (QS, HEADS, HD)), ALU.mult).then_inc(s["o_normed"], 1)

                for n in range(2 * NB + 2):
                    if n < 2 * NB:
                        dve.wait_ge(s["score_done"], at("score_done", i, n + 1))
                        dve.tensor_reduce(NMX[:, n // 2, n % 2, :],
                                          PSUM[0:QS, n % 2, 0:HH * KS].rearrange("p (h k) -> p h k", h=HH), AX.X,
                                          ALU.max, negate=True).then_inc(s["max_done"], 1)
                    if n >= 2:
                        after_scores(n - 2)
                    if n >= 3 and n % 2 == 1:
                        normalize((n - 3) // 2)
                nm = NMX[0:1].rearrange("p b a h -> p b (a h)")
                link(dve.tensor_reduce(CM[:], NMX[0:1].rearrange("p b a h -> p (a h) b"), AX.X, ALU.min))
                dve.scalar_tensor_tensor(CW[:], nm, -1.0, CM[:].unsqueeze(1).broadcast_to((1, NB, HEADS)), ALU.mult,
                                         ALU.add).then_inc(s["cls_weight"], 1)
                dve.wait_ge(s["cls_exp"], at("cls_exp", i, 1))
                link(dve.tensor_tensor(CW[:], CW[:], DEN[0:1].rearrange("p b a h -> p b (a h)"), ALU.mult))
                link(dve.tensor_reduce(CSUM[:], CW[:].rearrange("p b h -> p h b"), AX.X, ALU.add))
                link(dve.reciprocal(CSUM[:], CSUM[:]))
                dve.tensor_tensor(CW[:], CW[:], CSUM[:].unsqueeze(1).broadcast_to((1, NB, HEADS)), ALU.mult
                                  ).then_inc(s["cls_coef"], 1)
                dve.wait_ge(s["cls_mult"], at("cls_mult", i, 1))
                dve.tensor_reduce(CO[:], CP.rearrange("p b c -> p c b"), AX.X, ALU.add).then_inc(s["cls_sum"], 1)
                for n in range(6):
                    if n % 2:
                        evacuate_oT(dve, n, i)
                for tp in range(NP):
                    dve.wait_ge(s["wo_done"], at("wo_done", i, tp + 1))
                    xp = X1[:, 2 * tp:2 * tp + 2, :].rearrange("p a b -> p (a b)")
                    dve.tensor_tensor(xp, xp, PSUM[:, 4 + tp % 2, 0:2 * C], ALU.add).then_inc(s["x2_ready"], 1)
                dve.wait_ge(s["x2_ready"], at("x2_ready", i, NP))
                token_norm(X1, 1e-5, "ln2_eps", "ln2_rstd", "xn2_ready", twice=True)
                for a in range(2):
                    dve.wait_ge(s["xh_ready"], at("xh_ready", i, a + 1))
                    dve.scalar_tensor_tensor(XL[:, a, :].rearrange("p (a b) -> p a b", a=2),
                                             PSUM[:, 2 * a:2 * a + 2, :], X_UP,
                                             XH[:, a, :].rearrange("p (a b) -> p a b", a=2), ALU.mult, ALU.subtract
                                             ).then_inc(s["xl_ready"], 1)
                dve.wait_ge(s["route_done"], at("route_done", i, 1))
                gb = GB[:].unsqueeze(1).broadcast_to((128, NT, E))
                link(dve.scalar_tensor_tensor(SC[:], PSUM[:, 6, 0:NT * E].rearrange("p (t e) -> p t e", t=NT),
                                              1 / (X_UP * W_UP), gb, ALU.mult, ALU.add))
                link(dve.tensor_reduce(SM[:], SC[:], AX.X, ALU.max))
                sm = SM[:].unsqueeze(2).broadcast_to((128, NT, E))
                dve.tensor_tensor(SC[:], SC[:], sm, ALU.subtract).then_inc(s["route_shift"], 1)
                dve.wait_ge(s["route_exp"], at("route_exp", i, 1))
                link(dve.tensor_reduce(SM[:], SE[:], AX.X, ALU.add))
                link(dve.reciprocal(SM[:], SM[:]))
                link(dve.tensor_tensor(SE[:], SE[:], sm, ALU.mult))
                mine = SE[:].unsqueeze(3).broadcast_to((128, NT, E, E))
                other = SE[:].unsqueeze(2).broadcast_to((128, NT, E, E))
                dve.tensor_tensor(CMPA[:], mine, other, ALU.is_ge)
                link(dve.tensor_tensor(CMPB[:], mine, other, ALU.is_gt))
                dve.tensor_tensor(CMPA[:], CMPA[:], AFTER[:].unsqueeze(1).broadcast_to((128, NT, E, E)), ALU.mult)
                link(dve.tensor_tensor(CMPB[:], CMPB[:], BEFORE[:].unsqueeze(1).broadcast_to((128, NT, E, E)),
                                       ALU.mult))
                link(dve.tensor_tensor(CMPA[:], CMPA[:], CMPB[:], ALU.add))
                link(dve.tensor_reduce(WIN[:], CMPA[:], AX.X, ALU.add))
                link(dve.scalar_tensor_tensor(WIN[:], WIN[:], 2.0, SE[:], ALU.is_ge, ALU.mult))
                link(dve.tensor_reduce(SM[:], WIN[:], AX.X, ALU.add))
                link(dve.tensor_scalar(SM[:], SM[:], 1e-9, None, ALU.add))
                link(dve.reciprocal(SM[:], SM[:]))
                dve.scalar_tensor_tensor(GATE[:], WIN[:], 1 / (W_UP * H_UP), sm, ALU.mult, ALU.mult
                                         ).then_inc(s["gates_ready"], 1)
                dve.wait_ge(s["gates_ready"], at("gates_ready", i, 1))

                def split(n):
                    dve.wait_ge(s["gelu_done"], at("gelu_done", i, n + 1))
                    if n >= 2:
                        dve.wait_ge(s["ffn2_chunk"], at("ffn2_chunk", i, n - 1))
                    dve.tensor_scalar(HHI[:, n % 2, :], HF[:, n % 2, :], H_UP, None, ALU.mult
                                      ).then_inc(s["hh_ready"], 1)
                    dve.wait_ge(s["hh_ready"], at("hh_ready", i, n + 1))
                    dve.scalar_tensor_tensor(HLO[:, n % 2, :], HF[:, n % 2, :], H_UP, HHI[:, n % 2, :], ALU.mult,
                                             ALU.subtract).then_inc(s["hl_ready"], 1)

                def add_expert(g):
                    half, e = divmod(g, E)
                    dve.wait_ge(s["ffn2_chunk"], at("ffn2_chunk", i, (g + 1) * HK))
                    if g:
                        dve.wait_ge(s["ffn_added"], at("ffn_added", i, g))
                    for q in range(4):
                        t = 4 * half + q
                        last = dve.scalar_tensor_tensor(X1[:, t, :], PSUM[:, 6 + q // 2, (q % 2) * C:(q % 2 + 1) * C],
                                                        GATE[:, t, e:e + 1], X1[:, t, :], ALU.mult, ALU.add)
                    last.then_inc(s["ffn_added"], 1)

                for n in range(NCHUNK):
                    split(n)
                    if n % HK == HK - 1:
                        add_expert(n // HK)
                dve.wait_ge(s["outT_done"], at("outT_done", i, 1))
                dve.tensor_copy(OUT[:, 1, :].rearrange("p (a b) -> p a b", a=2), PSUM[0:HC, 2:4, :]
                                ).then_inc(s["out_dve"], 1)
                assert links[0] == LINKS, links[0]

        @block.tensor
        def _(pe):
            with pe.Fori(0, B) as i:
                pe.wait_ge(s["out_act"], at("out_act", i, 0))
                pe.wait_ge(s["out_dve"], at("out_dve", i, 0))
                pe.wait_ge(s["gn_channel"], at("gn_channel", i, 1))
                pe.matmul(PSUM[0:HC, 0, 0:2], GAVG[:], MV[:, :, 0], start=True, stop=True).then_inc(s["gn_mean"], 1)
                pe.wait_ge(s["gn_spread"], at("gn_spread", i, 1))
                pe.matmul(PSUM[0:HC, 0, 2:4], GAVG[:], GD[:], start=True, stop=True).then_inc(s["gn_var"], 1)
                for half in range(2):
                    for j in range(2):
                        if half == 0:
                            pe.wait_ge(s["xg_ready"], at("xg_ready", i, j + 1))
                        k = 97 - j
                        mm = pe.matmul(bank(half), PROJ[0:k, j, :], XG[0:k, j, half * 512:(half + 1) * 512],
                                       start=(j == 0), stop=(j == 1))
                mm.then_inc(s["proj_done"], 1)
                for t in range(NT):
                    for j in range(2):
                        mm = pe.matmul(PSUM[:, 3, t * 32:(t + 1) * 32], XG[0:HC, j, t * 128:(t + 1) * 128],
                                       WG1[:, j, :], start=(j == 0), stop=(j == 1))
                mm.then_inc(s["h1_done"], 1)
                pe.wait_ge(s["gu_ready"], at("gu_ready", i, 2))
                for tp in range(NP):
                    if tp >= 2:
                        pe.wait_ge(s["stats_read"], at("stats_read", i, tp - 1))
                    for t in range(2):
                        for j in range(2):
                            c = (2 * tp + t) * 128
                            mm = pe.transpose(PSUM[:, tp % 2, t * C + j * HC:t * C + (j + 1) * HC],
                                              XG[0:HC, j, c:c + 128], EYE[0:HC, 0:HC])
                    mm.then_inc(s["xgT_done"], 1)
                pe.wait_ge(s["h1_gelu"], at("h1_gelu", i, 1))
                pe.wait_ge(s["gu_moved"], at("gu_moved", i, 16 * 2 * KP))
                for kind in range(2):
                    for ct in range(KC):
                        for cp in range(KC):
                            mm = pe.matmul(PSUM[:, 2, (kind * KC + ct) * GW:(kind * KC + ct + 1) * GW],
                                           SCAN[:, kind, ct - cp + KC - 1, :], GUP[:, kind, cp, :],
                                           start=(cp == 0), stop=(cp == KC - 1))
                mm.then_inc(s["scan_done"], 1)
                pe.wait_ge(s["hs_copied"], at("hs_copied", i, 1))
                for g in range(2):
                    mm = pe.transpose(PSUM[:, 2, g * 128:(g + 1) * 128],
                                      H1[:, 4 * g:4 * g + 4, :].rearrange("p a b -> p (a b)"), EYE[:])
                mm.then_inc(s["h1T_done"], 1)
                pe.wait_ge(s["h1T_copied"], at("h1T_copied", i, 1))
                pe.wait_ge(s["hs_moved"], at("hs_moved", i, 16 * 2 * KP))
                pe.wait_ge(s["hs_placed"], at("hs_placed", i, 16))
                pe.wait_ge(s["xs_ready"], at("xs_ready", i, 2))
                pe.wait_ge(s["h1_pre"], at("h1_pre", i, 1))
                for tp in range(NP):
                    if tp:
                        pe.wait_ge(s["mixed"], at("mixed", i, tp))
                    for t in range(2):
                        tt = 2 * tp + t
                        tok = slice(tt * 128, tt * 128 + 128)
                        col = slice(t * C, (t + 1) * C)
                        pe.matmul(PSUM[:, 0, col], H1T[:, tt // 4, :], WG2[:, tt % 4, :], start=True, stop=False)
                        pe.matmul(PSUM[:, 0, col], ONES3[:], ROWS3[:, 0:C], start=False, stop=True)
                        for j in range(2):
                            pe.matmul(PSUM[:, 1 + tp % 2, col], XG[0:113, j, tok], WY[:, j, :], start=(j == 0),
                                      stop=(j == 1))
                        for j in range(2):
                            mm = pe.transpose(PSUM[:, 3, t * C + j * HC:t * C + (j + 1) * HC], XS[:, j, tok],
                                              EYE[0:HC, 0:HC])
                    mm.then_inc(s["mix_done"], 1)
                pe.wait_ge(s["mixed"], at("mixed", i, NP))
                pe.wait_ge(s["xn1_ready"], at("xn1_ready", i, 1))
                for t in range(NT):
                    for j in range(2):
                        mm = pe.transpose(PSUM[0:HC, 2 * j + t // 4, (t % 4) * 128:(t % 4 + 1) * 128],
                                          XN[:, t, j * HC:(j + 1) * HC], EYE[:])
                mm.then_inc(s["xn1T_done"], 1)
                pe.wait_ge(s["win_act"], at("win_act", i, 1))
                pe.wait_ge(s["win_dve"], at("win_dve", i, 1))
                for n in range(18):
                    if n >= 4:
                        m = n - 4
                        nm = ("piece_act", "piece_dve")[m % 2]
                        pe.wait_ge(s[nm], at(nm, i, m // 2 + 1))
                    if n < 12:
                        W = WQ if n < 6 else WK
                        oh, (b0, b1) = (n % 6) // 3, SPANS[n % 3]
                        keys = slice(PAD, PAD + QB) if n < 6 else slice(0, KS)
                        width = (b1 - b0) * (QB if n < 6 else KS)
                        for j in range(2):
                            mm = pe.matmul(PSUM[0:HC, n % 4, 0:width], W[:, j, oh * HC:(oh + 1) * HC],
                                           XW[:, j, b0:b1, keys], start=(j == 0), stop=(j == 1))
                        if n < 6 and n % 3 == 2:
                            for j in range(2):
                                mm = pe.matmul(PSUM[0:HC, n % 4, 400:401], W[:, j, oh * HC:(oh + 1) * HC],
                                               XW[:, j, 0, KW:KS], start=(j == 0), stop=(j == 1))
                    else:
                        for b in range(2 * (n - 12), min(2 * (n - 12) + 2, NB)):
                            for j in range(2):
                                mm = pe.matmul(PSUM[0:KS, n % 4, (b % 2) * C:(b % 2 + 1) * C], XW[:, j, b, :],
                                               WV[:, j, :], start=(j == 0), stop=(j == 1))
                    mm.then_inc(s["piece_done"], 1)
                pe.wait_ge(s["piece_act"], at("piece_act", i, 9))
                pe.wait_ge(s["piece_dve"], at("piece_dve", i, 9))

                def scores(n):
                    b, oh = n // 2, n % 2
                    if n >= 2:
                        pe.wait_ge(s["exp_done"], at("exp_done", i, n - 1))
                    pe.matmul(PSUM[0:QS, n % 2, 0:HH * KS], QT[:, oh, b, :],
                              KBD[:, oh, b, :, :].rearrange("p h k -> p (h k)"), start=True, stop=False)
                    v = 0 if b == 0 else 2 if b == NB - 1 else 1
                    pe.matmul(PSUM[0:QS, n % 2, 0:HH * KS], EYEB[:], MASKB[:, v, :], start=False, stop=True
                              ).then_inc(s["score_done"], 1)

                def turn(n):
                    pe.wait_ge(s["exp_done"], at("exp_done", i, n + 1))
                    if n >= 2:
                        pe.wait_ge(s["pT_copied"], at("pT_copied", i, n - 1))
                    for h in range(HH):
                        mm = pe.transpose(PSUM[0:KS, 2 + n % 2, h * QS:(h + 1) * QS], PS[:, n % 2, h, :],
                                          EYE[0:QS, 0:QS])
                    mm.then_inc(s["pT_done"], 1)

                def values(n):
                    b, oh = n // 2, n % 2
                    pe.wait_ge(s["pT_copied"], at("pT_copied", i, n + 1))
                    if oh == 0 and b >= 2:
                        pe.wait_ge(s["o_normed"], at("o_normed", i, b - 1))
                    for h in range(HH):
                        c = oh * HC + h * HD
                        mm = pe.matmul(PSUM[0:QS, 4 + b % 2, c:c + HD], PT[:, n % 2, h, :], VW[:, b, c:c + HD],
                                       start=True, stop=True)
                    if oh == 1:
                        mm.then_inc(s["pv_done"], 1)

                for n in range(2 * NB + 2):
                    if n < 2 * NB:
                        scores(n)
                    if 1 <= n <= 2 * NB:
                        turn(n - 1)
                    if n >= 2:
                        values(n - 2)
                pe.wait_ge(s["pT_copied"], at("pT_copied", i, 2 * NB))
                pe.wait_ge(s["o_normed"], at("o_normed", i, NB))
                pe.wait_ge(s["cls_sum"], at("cls_sum", i, 1))
                for n in range(6):
                    oh, (b0, b1) = n // 3, OSPANS[n % 3]
                    if n >= 4:
                        pe.wait_ge(s["oT_copied"], at("oT_copied", i, 4))
                    for b in range(b0, b1):
                        mm = pe.transpose(PSUM[0:HC, n % 4, (b - b0) * QB:(b - b0 + 1) * QB],
                                          OS[:, b, oh * HC:(oh + 1) * HC], EYE[0:QS, 1:QS]) if False else \
                            pe.matmul(PSUM[0:HC, n % 4, (b - b0) * QB:(b - b0 + 1) * QB],
                                      OS[:, b, oh * HC:(oh + 1) * HC], EYE[0:QS, 1:QS], start=True, stop=True)
                    if n % 3 == 2:
                        mm = pe.matmul(PSUM[0:HC, n % 4, 400:401], CO[:, oh * HC:(oh + 1) * HC], EYE[0:1, 0:1],
                                       start=True, stop=True)
                    mm.then_inc(s["oT_done"], 1)
                pe.wait_ge(s["oT_copied"], at("oT_copied", i, 6))
                for tp in range(NP):
                    if tp >= 2:
                        pe.wait_ge(s["x2_ready"], at("x2_ready", i, tp - 1))
                    for t in range(2):
                        c = (2 * tp + t) * 128
                        dst = PSUM[:, 4 + tp % 2, t * C:(t + 1) * C]
                        for j in range(2):
                            pe.matmul(dst, OT[:, j, c:c + 128], WO[:, j, :], start=(j == 0), stop=False)
                        mm = pe.matmul(dst, ONES3[:], ROWS3[:, C:2 * C], start=False, stop=True)
                    mm.then_inc(s["wo_done"], 1)
                pe.wait_ge(s["xn2_ready"], at("xn2_ready", i, 1))
                for a in range(2):
                    for t in range(NT):
                        if a == 0:
                            src = XN[:, t, 0:128]
                            mm = pe.transpose(PSUM[:, t // 4, (t % 4) * 128:(t % 4 + 1) * 128], src, EYE[:])
                        else:
                            src = XN[:, t, 128:256]
                            mm = pe.transpose(PSUM[:, 2 + t // 4, (t % 4) * 128:(t % 4 + 1) * 128], src, EYE[:])
                mm.then_inc(s["xn2T_done"], 1)
                pe.wait_ge(s["xl_ready"], at("xl_ready", i, 2))
                for t in range(NT):
                    tok = slice(t * 128, t * 128 + 128)
                    dst = PSUM[:, 6, t * E:(t + 1) * E]
                    pe.matmul(dst, XH[:, 0, tok], GWAH[:], start=True, stop=False)
                    pe.matmul(dst, XH[:, 0, tok], GWAL[:], start=False, stop=False)
                    pe.matmul(dst, XL[:, 0, tok], GWAH[:], start=False, stop=False)
                    pe.matmul(dst, XH[:, 1, tok], GWB[:], start=False, stop=False)
                    mm = pe.matmul(dst, XL[:, 1, tok], GWB[:], start=False, stop=True)
                mm.then_inc(s["route_done"], 1)
                pe.wait_ge(s["route_shift"], at("route_shift", i, 1))

                def ffn1(n):
                    half, ek = divmod(n, E * HK)
                    tok = slice(half * NH, (half + 1) * NH)
                    w = slice(ek * 128, (ek + 1) * 128)
                    if n >= 2:
                        pe.wait_ge(s["gelu_done"], at("gelu_done", i, n - 1))
                    dst = bank(4 + n % 2)
                    pe.matmul(dst, W1AH[:, w], XH[:, 0, tok], start=True, stop=False)
                    pe.matmul(dst, W1AH[:, w], XL[:, 0, tok], start=False, stop=False)
                    pe.matmul(dst, W1AL[:, w], XH[:, 0, tok], start=False, stop=False)
                    pe.matmul(dst, W1B[:, w], XH[:, 1, tok], start=False, stop=False)
                    pe.matmul(dst, W1B[:, w], XL[:, 1, tok], start=False, stop=True).then_inc(s["ffn1_done"], 1)

                def ffn2(n):
                    g, k = divmod(n, HK)
                    e = g % E
                    if k == 0 and g:
                        pe.wait_ge(s["ffn_added"], at("ffn_added", i, g))
                    pe.wait_ge(s["hh_ready"], at("hh_ready", i, n + 1))
                    pe.wait_ge(s["hl_ready"], at("hl_ready", i, n + 1))
                    for q in range(4):
                        dst = PSUM[:, 6 + q // 2, (q % 2) * C:(q % 2 + 1) * C]
                        tok = slice(q * 128, (q + 1) * 128)
                        if k == 0:
                            pe.matmul(dst, ONES3[:], ROWS3[:, (2 + e) * C:(3 + e) * C], start=(q % 2 == 0), stop=False,
                                      skip_group_check=True)
                        pe.matmul(dst, HHI[:, n % 2, tok], W2H[:, e * HK + k, :], start=False, stop=False,
                                  skip_group_check=True)
                        pe.matmul(dst, HHI[:, n % 2, tok], W2L[:, e * HK + k, :], start=False, stop=False,
                                  skip_group_check=True)
                        mm = pe.matmul(dst, HLO[:, n % 2, tok], W2H[:, e * HK + k, :], start=False,
                                       stop=(k == HK - 1), skip_group_check=True)
                    mm.then_inc(s["ffn2_chunk"], 1)

                for n in range(NCHUNK + 1):
                    if n < NCHUNK:
                        ffn1(n)
                    if n >= 1:
                        ffn2(n - 1)
                pe.wait_ge(s["ffn_added"], at("ffn_added", i, NHALF * E))
                for t in range(NT):
                    for j in range(2):
                        mm = pe.transpose(PSUM[0:HC, 2 * j + t // 4, (t % 4) * 128:(t % 4 + 1) * 128],
                                          X1[:, t, j * HC:(j + 1) * HC], EYE[:])
                mm.then_inc(s["outT_done"], 1)


def kernel(**inputs):
    import numpy as np
    import concourse.bacc as bacc
    from concourse.bass_utils import run_bass_kernel_spmd as run

    a = {k: np.asarray(v) for k, v in inputs.items()}
    r = {k[len("L0_conv_row_"):]: v for k, v in a.items() if k.startswith("L0_conv_row_")}
    c = {k[len("L0_conv_col_"):]: v for k, v in a.items() if k.startswith("L0_conv_col_")}
    f = np.float32

    def halves(w):
        return np.ascontiguousarray(w.reshape(2, HC, -1).transpose(1, 0, 2))

    def vec(v):
        return np.ascontiguousarray(v.reshape(2, HC).T)

    proj = np.zeros((97, 2, 128), f)
    for k, (w, bb) in enumerate(((r["Win"], r["bin"]), (c["Win"], c["bin"]), (r["Wg"], r["bg"]), (c["Wg"], c["bg"]))):
        proj[0:HC, :, 32 * k:32 * k + S] = halves(w.T)
        proj[96, 0, 32 * k:32 * k + S] = bb
    ya, yb = np.zeros((113, 2, C), f), np.zeros((113, 2, C), f)
    ya[0:HC], yb[0:HC] = halves(r["Wskip"].T), halves(c["Wskip"].T)
    ya[96, 0], yb[96, 0] = r["bout"], r["bskip"]
    ya[96, 1], yb[96, 1] = c["bout"], c["bskip"]
    ya[97:, 0], ya[97:, 1] = r["Wout"].T, c["Wout"].T
    yscale = np.full((113, 1), 0.5, f)
    yscale[97:] = 0.125
    sv, su, sa = np.zeros((S, 2 * S), f), np.zeros((S, 2 * S), f), np.zeros((2 * S, 1), f)
    R = r["U"].shape[1]
    for k, p in enumerate((r, c)):
        sv[k * R:(k + 1) * R, k * S:(k + 1) * S] = p["V"].T
        su[k * R:(k + 1) * R, k * S:(k + 1) * S] = p["U"].T
        sa[k * S:(k + 1) * S, 0] = p["a_logit"]
    g2 = np.zeros((4, 32, 4, C), f)
    for k in range(4):
        g2[k, :, k] = a["L0_conv_g2_w"].T
    g2 = g2.reshape(128, 4, C)
    gavg = np.kron(np.eye(HC // GROUP), np.full((GROUP, GROUP), 1.0 / GROUP)).astype(f)
    mask = np.full((QS, 3, HH, KS), NEG, f)
    for v, b in enumerate((0, 1, NB - 1)):
        for q in range(1, QS):
            for k in range(q - 1, q + 2 * PAD):
                if 1 <= b * QB + 1 - PAD + k < T:
                    mask[q, v, :, k] = 0.0
            mask[q, v, :, KW] = 0.0
        mask[0, v, :, PAD:PAD + QB] = 0.0
    mask[0, 0, :, KW] = 0.0
    w1, w2 = a["L1_ffn_w1"], a["L1_ffn_w2"]
    w1t = w1.transpose(1, 0, 2).reshape(C, E * HID)
    ins = dict(
        x=np.ascontiguousarray(a["x"].reshape(B, 2, HC, T).transpose(0, 2, 1, 3)),
        proj_w=proj, y_wa=ya, y_wb=yb, y_scale=yscale, eye=np.eye(128, dtype=f), gavg=gavg,
        cavg=np.full((HC, HC), 1.0 / C, f), norm_w=vec(a["L0_conv_norm_w"]), norm_b=vec(a["L0_conv_norm_b"]),
        g1_wT=halves(a["L0_conv_g1_w"].T), g1_b=a["L0_conv_g1_b"].reshape(1, -1),
        g2_wT=g2,
        bias_row=np.concatenate([a["L0_conv_g2_b"], a["L1_attn_bo"], a["L1_ffn_b2"].reshape(-1)]).reshape(1, -1),
        scan_v=sv, scan_u=su, scan_a=sa,
        wq=halves(a["L1_attn_Wq"]), wk=halves(a["L1_attn_Wk"]), wv=halves(a["L1_attn_Wv"]), wo=halves(a["L1_attn_Wo"]),
        bq=vec(a["L1_attn_bq"]), bk=vec(a["L1_attn_bk"]), bv=vec(a["L1_attn_bv"]),
        mask=mask.reshape(QS, -1),
        w1a=np.ascontiguousarray(w1t[0:128]), w1b=np.ascontiguousarray(np.tile(w1t[128:], (2, 1))),
        w2=np.ascontiguousarray(w2.reshape(E, HK, 128, C).transpose(2, 0, 1, 3)).reshape(128, -1),
        b1=np.ascontiguousarray(a["L1_ffn_b1"].reshape(E * HK, 128).T),
        gate_wa=np.ascontiguousarray(a["L1_ffn_gate_w"][0:128]),
        gate_wb=np.ascontiguousarray(np.tile(a["L1_ffn_gate_w"][128:], (2, 1))),
        gate_b=np.ascontiguousarray(np.tile(a["L1_ffn_gate_b"][None], (128, 1))),
        before=np.ascontiguousarray(np.broadcast_to(np.tril(np.ones((E, E), f), -1), (128, E, E))),
        after=np.ascontiguousarray(np.broadcast_to(np.triu(np.ones((E, E), f), 1), (128, E, E))),
    )
    nc = bacc.Bacc("TRN2", target_bir_lowering=False, num_devices=1)
    aps = {k: nc.dram_tensor("in_" + k, v.shape, mybir.dt.from_np(v.dtype), kind="ExternalInput").ap()
           for k, v in ins.items()}
    out = nc.dram_tensor("out_dram", (B, HC, 2, T), F32, kind="ExternalOutput").ap()
    powers = nc.dram_tensor("powers", (2 * S, 63, 2 * S), F32, kind="Internal").ap()
    hybrid_kernel(nc, **aps, out=out, powers=powers)
    res = run(nc, [{"in_" + k: v for k, v in ins.items()}], core_ids=[0])
    got = res.results[0]["out_dram"]
    return np.ascontiguousarray(got.transpose(0, 2, 1, 3)).reshape(B, C, GH, GW)
```

```python
from contextlib import ExitStack

import concourse.bass as bass
from concourse import mybir

F32 = mybir.dt.float32
F16 = mybir.dt.float16
BF16 = mybir.dt.bfloat16
ALU = mybir.AluOpType
ACT = mybir.ActivationFunctionType
AX = mybir.AxisListType

B, C, GH, GW = 16, 192, 32, 32
T = GH * GW
NT = T // 128
NP = NT // 2
HC = C // 2
S = 16
KP, KC = 128 // S, GW // (128 // S)
HEADS, HD = 6, 32
HH = HEADS // 2
PAD = 16
QB = 93
NB = (T - 1) // QB
KW = QB + 2 * PAD
KS = KW + 1
QS = QB + 1
E, HID = 4, 768
HK = HID // 128
NH = 512
NHALF = T // NH
GROUP = C // 32
NCHUNK = NHALF * E * HK

LINKS_FIRST, LINKS = 14, 44

X_UP, W_UP, H_UP = 1024.0, 64.0, 8.0
NEG = -1e30

PER = dict(
    x_loaded=16, gn_channel=1, gn_mean=1, gn_spread=1, gn_var=1, gn_eps=1, gn_rstd=1, xg_ready=2, xs_ready=2,
    proj_done=1, tanh_done=1, gu_ready=2, gu_moved=16 * 2 * KP, scan_done=1, hs_copied=1, hs_moved=16 * 2 * KP,
    hs_permuted=1, hs_placed=16, xgT_done=NP, h1_read=NP, mixln_eps=1, mixln_rstd=1, h1_pre=1,
    h1_gelu=1, h1T_done=1, h1T_copied=1, mix_done=NP, mix_tanh=NP, mixed=NP,
    ln1_eps=1, ln1_rstd=1, xn1_ready=2, xn1T_done=1, win_act=1, win_dve=1, piece_done=18, piece_act=9, piece_dve=9,
    score_done=2 * NB, max_done=2 * NB, exp_done=2 * NB, pT_done=2 * NB, pT_copied=2 * NB, pv_done=NB,
    o_normed=NB, cls_weight=1, cls_exp=1, cls_coef=1, cls_mult=1, cls_sum=1, oT_done=6, oT_copied=6,
    wo_done=NP, x2_ready=NP, ln2_eps=1, ln2_rstd=1, xn2_ready=1, xn2T_done=1, xh_ready=2, xl_ready=2,
    route_done=1, route_shift=1, route_exp=1, gates_ready=1,
    ffn1_done=NCHUNK, gelu_done=NCHUNK, hh_ready=NCHUNK, hl_ready=NCHUNK, ffn2_chunk=NCHUNK,
    ffn_added=NHALF * E, x2_free=32,
)


def window_view(t, offset, dims):
    base = t[:]
    return bass.AP(tensor=base.tensor, offset=base.offset + offset, ap=[[base.ap[0][0], dims[0]]] + dims[1:])


def hybrid_kernel(nc, x, proj_w, y_wa, y_wb, y_scale, eye, gavg, cavg, norm_w, norm_b, g1_wT, g1_b, g2_wT, bias_row,
                  scan_v, scan_u, scan_a, wq, wk, wv, wo, bq, bk, bv, mask, w1a, w1b, w2, b1, gate_wa, gate_wb,
                  gate_b, before, after, out, powers):
    ctx = ExitStack()
    with ctx:
        def sb(name, shape, dt=F32):
            return ctx.enter_context(nc.sbuf_tensor(name, shape, dt))

        def sem(name):
            return ctx.enter_context(nc.semaphore(name))

        EYE = sb("EYE", [128, 128])
        EYEB = sb("EYEB", [QS, QS], BF16)
        GAVG = sb("GAVG", [HC, HC])
        MASKB = sb("MASKB", [QS, 3, HH * KS], BF16)
        PROJ = sb("PROJ", [97, 2, 128])
        WY = sb("WY", [113, 2, C])
        WG1 = sb("WG1", [HC, 2, 32])
        BG1 = sb("BG1", [128, 32])
        WG2 = sb("WG2", [128, 4, C])
        SCAN = sb("SCAN", [128, 2, 2 * KC - 1, 128])
        WQ, WK, WV, WO = (sb(n, [HC, 2, C]) for n in ("WQ", "WK", "WV", "WO"))
        BQ, BQS, BK, BV = (sb(n, [HC, 2]) for n in ("BQ", "BQS", "BK", "BV"))
        ONES3 = sb("ONES3", [3, 128], BF16)
        ROWS3 = sb("ROWS3", [3, 6 * C], BF16)
        W1AH = sb("W1AH", [128, E * HID], F16)
        W1AL = sb("W1AL", [128, E * HID], F16)
        W1B = sb("W1B", [128, E * HID], F16)
        W2H = sb("W2H", [128, E * HK, C], F16)
        W2L = sb("W2L", [128, E * HK, C], F16)
        B1 = sb("B1", [128, E * HK])
        GWAH, GWAL, GWB = (sb(n, [128, E], F16) for n in ("GWAH", "GWAL", "GWB"))
        GB = sb("GB", [128, E])
        BEFORE, AFTER = sb("BEFORE", [128, E, E]), sb("AFTER", [128, E, E])
        MHALF = sb("MHALF", [128, 8])
        SPARES = sb("SPARES", [1, 2])
        SPARE, PSPARE = SPARES[:, 0:1], SPARES[:, 1:2]

        XR = sb("XR", [HC, 2, T])
        XG = sb("XG", [113, 2, T])
        XS = sb("XS", [HC, 2, T])
        GST = sb("GST", [HC, 2, 2, 6])
        MV = sb("MV", [HC, 2, 2])
        GM, GD, GV, GR, GR1, GNB = (sb(n, [HC, 2]) for n in ("GM", "GD", "GV", "GR", "GR1", "GNB"))
        TGU = sb("TGU", [128, T])
        TG, GU = TGU[64:128, :], TGU[0:64, :]
        HST = TGU[0:S, :].rearrange("s (w h) -> s w h", w=GW)
        GUP = sb("GUP", [128, 2, KC, GW])
        HSP = sb("HSP", [128, 2, KC, GW])
        TST = sb("TST", [128, NT, 6])
        TMV = sb("TMV", [128, NT, 2])
        TV, TR = sb("TV", [128, NT]), sb("TR", [128, NT])
        H1 = sb("H1", [128, NT, 32])
        H1T = sb("H1T", [128, 2, 128])
        TM = sb("TM", [128, 2 * C])
        EM = sb("EM", [128, 2 * C])
        X1 = sb("X1", [128, NT, C])
        XN = sb("XN", [128, NT, 256])
        X2 = sb("X2", [128, NT, C])
        XW = sb("XW", [HC, 2, NB, KS])
        QT = sb("QT", [HC, 2, NB, QS])
        KBD = sb("KBD", [HC, 2, NB, HH, KS])
        VW = sb("VW", [KS, NB, C])
        NMX = sb("NMX", [QS, NB, 2, HH])
        DEN = sb("DEN", [QS, NB, 2, HH])
        RDEN = sb("RDEN", [QS, NB, 2, HH])
        PS = sb("PS", [QS, 2, HH, KS])
        PT = sb("PT", [KS, 2, HH, QS])
        OS = XW[0:QS].rearrange("p a b k -> p (a b k)")[:, 0:NB * C].rearrange("p (b c) -> p b c", b=NB)
        OT = QT[:].rearrange("p a b q -> p (a b q)")[:, 0:2 * T].rearrange("p (a t) -> p a t", a=2)
        CM = sb("CM", [1, HEADS])
        CW = sb("CW", [1, NB, HEADS])
        CSUM = sb("CSUM", [1, HEADS])
        CP = VW[0:1, :, :]
        CO = sb("CO", [1, C])
        XH = sb("XH", [128, 2, T], F16)
        XL = sb("XL", [128, 2, T], F16)
        SC = sb("SC", [128, NT, E])
        SE = sb("SE", [128, NT, E])
        SM = sb("SM", [128, NT])
        CMPA, CMPB = sb("CMPA", [128, NT, E, E]), sb("CMPB", [128, NT, E, E])
        WIN = sb("WIN", [128, NT, E])
        GATE = sb("GATE", [128, NT, E])
        HF = sb("HF", [128, 2, NH])
        HST2 = HF[0:S].rearrange("s a b -> s (a b)")
        HHI = sb("HHI", [128, 2, NH], F16)
        HLO = sb("HLO", [128, 2, NH], F16)

        PSUM = ctx.enter_context(nc.psum_tensor("PSUM", [128, 8, 512], F32))
        Q = PSUM[:, 0:4, :]

        weights_ready = sem("weights_ready")
        with ExitStack() as setup:
            def ssem(name):
                return setup.enter_context(nc.semaphore(name))

            loaded, dve_step, act_step, pe_step = ssem("loaded"), ssem("dve_step"), ssem("act_step"), ssem("pe_step")
            powers_stored, scan_loaded, rows_split, rows_moved = (
                ssem(n) for n in ("powers_stored", "scan_loaded", "rows_split", "rows_moved"))
            pool_step = ssem("pool_step")
            STG = setup.enter_context(nc.sbuf_tensor("STG", [128, 1, 8], F32))
            Y_A, Y_B = XN[0:113, 0:2, 0:C], XN[0:113, 2:4, 0:C]
            YSC = SM[0:113, 0:1]
            NW, NBI, CAVG = STG[0:HC, 0, 0:2], STG[0:HC, 0, 2:4], XN[0:HC, 4, 0:HC]
            G1W = X1[0:HC, 0, 0:64].rearrange("p (j o) -> p j o", j=2)
            G1N = X1[0:HC, 1, 0:64].rearrange("p (j o) -> p j o", j=2)
            NBB = X1[0:HC, 2:4, 0:128]
            G1B = XN[0:1, 5, 0:32]
            ONE1 = XN[0:1, 5, 32:160]
            PW = OS[0:2 * S, :, :].rearrange("p a b -> p (a b)")[:, 0:32 * 32].rearrange("p (k s) -> p k s", k=32)
            MIR = XG[0:2 * S, :, :].rearrange("p a b -> p (a b)")[:, 0:63 * 32].rearrange("p (k s) -> p k s", k=63)
            SV = GUP[0:S, 0, 0, 0:2 * S]
            SU = GUP[0:S, 0, 1, 0:2 * S]
            SA = GUP[0:2 * S, 0, 2, 0:1]
            SIG = GUP[0:2 * S, 0, 2, 1:2]
            DIA = GUP[0:2 * S, 0, 3, 0:2 * S]
            AT = GUP[0:2 * S, 1, 0, 0:2 * S]
            ROW = XR[0:1, 0:2, :].rearrange("p a b -> p (a b)")[:, 0:6 * C]
            ROWR = XS[0:1, 0:2, :].rearrange("p a b -> p (a b)")[:, 0:6 * C]
            ROWP = QT[0:1, :, :, :].rearrange("p a b c -> p (a b c)")[:, 0:9 * C].bitcast(BF16)
            with nc.Block() as block:
                PIECE = 1536
                STAGE = [X1[:].rearrange("p a b -> p (a b)"), XN[:].rearrange("p a b -> p (a b)")[:, 0:PIECE]]
                small = [
                    (EYE[:], eye), (GAVG[:], gavg), (PROJ[:], proj_w), (WG2[:], g2_wT),
                    (WQ[:], wq), (WK[:], wk), (WV[:], wv), (WO[:], wo), (BQ[:], bq), (BK[:], bk), (BV[:], bv),
                    (B1[:], b1), (GB[:], gate_b), (BEFORE[:], before), (AFTER[:], after),
                    (Y_A, y_wa), (Y_B, y_wb), (YSC, y_scale), (CAVG, cavg), (NW, norm_w), (NBI, norm_b),
                    (G1W, g1_wT), (G1B, g1_b), (SV, scan_v), (SU, scan_u), (SA, scan_a), (ROW, bias_row),
                    (VW[0:QS, 0:6, :].rearrange("p a b -> p (a b)")[:, 0:3 * HH * KS], mask),
                    (HF[:, 0, 0:E], gate_wa), (HF[:, 0, 4:4 + E], gate_wb),
                ]
                pieces = []
                for k in range(E * HID // PIECE):
                    pieces.append(("a", k, w1a[:, k * PIECE:(k + 1) * PIECE]))
                    pieces.append(("b", k, w1b[:, k * PIECE:(k + 1) * PIECE]))
                for k in range(E * HK * C // PIECE):
                    pieces.append(("2", k, w2[:, k * PIECE:(k + 1) * PIECE]))
                W2HF = W2H[:].rearrange("p a b -> p (a b)")
                W2LF = W2L[:].rearrange("p a b -> p (a b)")
                piece_loaded, piece_free = [ssem("piece_loaded0"), ssem("piece_loaded1")], ssem("piece_free")
                setup_done = ssem("setup_done")

                @block.sync
                def _(sp):
                    for dst, src in small:
                        sp.dma_start(dst, src).then_inc(loaded, 16)
                    sp.wait_ge(rows_split, 1)
                    sp.dma_start(ROWS3[:], ROWP.rearrange("p (k n) -> p k n", k=3)).then_inc(rows_moved, 16)
                    sp.wait_ge(powers_stored, 1)
                    sp.dma_start(powers, MIR).then_inc(scan_loaded, 16)
                    sp.wait_ge(scan_loaded, 16)
                    for kind in range(2):
                        for i in range(KP):
                            src = bass.AP(tensor=powers.tensor,
                                          offset=powers.offset + kind * S * 63 * 32 + kind * S + (31 - 24 - i) * 32,
                                          ap=[[63 * 32, S], [KP * 32, 2 * KC - 1], [32, KP], [1, S]])
                            for d in range(2 * KC - 1):
                                s1 = bass.AP(tensor=powers.tensor, offset=src.offset + d * KP * 32,
                                             ap=[[63 * 32, S], [32, KP], [1, S]])
                                sp.dma_start(SCAN[S * i:S * i + S, kind, d, :].rearrange("p (k s) -> p k s", k=KP), s1
                                             ).then_inc(scan_loaded, 16)
                    sp.wait_ge(setup_done, 1)
                    for n, (_, _, src) in enumerate(pieces):
                        if n >= 2:
                            sp.wait_ge(piece_free, n - 1)
                        sp.dma_start(STAGE[n % 2], src).then_inc(piece_loaded[n % 2], 16)
                    sp.wait_ge(scan_loaded, 16 * (1 + 2 * KP * (2 * KC - 1)))
                    sp.wait_ge(rows_moved, 16)

                n_dve = [0]
                marks = {}

                @block.vector
                def _(dve):
                    def link(ins):
                        n_dve[0] += 1
                        ins.then_inc(dve_step, 1)
                        dve.wait_ge(dve_step, n_dve[0])

                    for t in (XW, KBD, XG):
                        dve.memset(t[:], 0.0)
                    dve.memset(ONES3[:], 1.0)
                    dve.memset(SPARES[:], 0.0)
                    dve.memset(ONE1, 1.0)
                    link(dve.memset(MHALF[:], -0.5))
                    link(dve.memset(XG[96:97, :, :], 1.0))
                    dve.wait_ge(loaded, 16 * len(small))
                    dve.tensor_copy(EYEB[:], EYE[0:QS, 0:QS])
                    dve.tensor_copy(MASKB[:].rearrange("p a b -> p (a b)"),
                                    VW[0:QS, 0:6, :].rearrange("p a b -> p (a b)")[:, 0:3 * HH * KS])
                    dve.tensor_scalar(BQS[:], BQ[:], HD ** -0.5, None, ALU.mult)
                    link(dve.tensor_tensor(Y_A, Y_A, Y_B, ALU.add))
                    link(dve.tensor_scalar(WY[:], Y_A, YSC, None, ALU.mult))
                    for j in range(2):
                        link(dve.tensor_tensor(WY[0:HC, j, j * HC:(j + 1) * HC], WY[0:HC, j, j * HC:(j + 1) * HC],
                                               EYE[0:HC, 0:HC], ALU.subtract))
                    for j in range(2):
                        link(dve.tensor_scalar(G1N[:, j, :], G1W[:, j, :], NW[:, j:j + 1], None, ALU.mult))
                        link(dve.tensor_scalar(NBB[:, j, :], XG[0:HC, 0, 0:128], NBI[:, j:j + 1], None, ALU.add))
                    marks["g1"] = n_dve[0]
                    dve.wait_ge(pe_step, 2)
                    link(dve.tensor_copy(BG1[:], PSUM[:, 1, 0:32]))
                    for j in range(2):
                        link(dve.tensor_tensor(WG1[:, j, :], G1N[:, j, :], PSUM[0:HC, 0, 0:32], ALU.subtract))
                    link(dve.tensor_scalar(ROW[:, 2 * C:], ROW[:, 2 * C:], W_UP * H_UP, None, ALU.mult))
                    n = 6 * C
                    link(dve.tensor_copy(ROWP[:, 0:n], ROW))
                    link(dve.tensor_tensor(ROWR, ROW, ROWP[:, 0:n], ALU.subtract))
                    link(dve.tensor_copy(ROWP[:, n:2 * n], ROWR))
                    link(dve.tensor_tensor(ROWR, ROWR, ROWP[:, n:2 * n], ALU.subtract))
                    dve.tensor_copy(ROWP[:, 2 * n:3 * n], ROWR).then_inc(rows_split, 1)
                    dve.wait_ge(act_step, 1)
                    link(dve.tensor_scalar(SIG, SIG, 0.5, 0.5, ALU.mult, ALU.add))
                    link(dve.tensor_scalar(DIA, EYE[0:2 * S, 0:2 * S], SIG, None, ALU.mult))
                    link(dve.tensor_copy(PW[:, 0, :], EYE[0:2 * S, 0:2 * S]))
                    dve.wait_ge(pe_step, 3)
                    link(dve.tensor_tensor(PW[:, 1, :], DIA, PSUM[0:2 * S, 2, 0:2 * S], ALU.add))
                    marks["power"] = n_dve[0]
                    m, seen = 1, 3
                    while m < 32:
                        seen += 1
                        dve.wait_ge(pe_step, seen)
                        link(dve.tensor_copy(AT, PSUM[0:2 * S, 3, 0:2 * S]))
                        k = min(m, 31 - m)
                        if k:
                            seen += 1
                            dve.wait_ge(pe_step, seen)
                            link(dve.tensor_copy(PW[:, m + 1:m + 1 + k, :],
                                                 PSUM[0:2 * S, 4, 0:32 * k].rearrange("p (k s) -> p k s", k=k)))
                        m *= 2
                    link(dve.tensor_copy(MIR[:, 31:63, :], PW))
                    for k in range(1, 32):
                        dve.tensor_copy(MIR[:, 31 - k, :], PW[:, k, :])
                    link(dve.tensor_scalar(MIR[:, 31, :], PW[:, 0, :], 2.0, None, ALU.mult))
                    dve.memset(STG[0:1, 0, 4:5], 0.0).then_inc(powers_stored, 1)
                    link(dve.tensor_scalar(GWAH[:], HF[:, 0, 0:E], W_UP, None, ALU.mult))
                    link(dve.scalar_tensor_tensor(GWAL[:], HF[:, 0, 0:E], W_UP, GWAH[:], ALU.mult, ALU.subtract))
                    link(dve.tensor_scalar(GWB[:], HF[:, 0, 4:8], W_UP, None, ALU.mult))
                    link(dve.scalar_tensor_tensor(GWB[64:128], HF[64:128, 0, 4:8], W_UP, GWB[64:128], ALU.mult,
                                                  ALU.subtract))
                    dve.memset(STG[0:1, 0, 5:6], 0.0).then_inc(setup_done, 1)
                    for n, (kind, k, _) in enumerate(pieces):
                        dve.wait_ge(piece_loaded[n % 2], 16 * (n // 2 + 1))
                        sl = slice(k * PIECE, (k + 1) * PIECE)
                        hi = {"a": W1AH, "b": W1B, "2": W2HF}[kind][:, sl]
                        link(dve.tensor_scalar(hi, STAGE[n % 2], W_UP, None, ALU.mult))
                        if kind == "b":
                            last = dve.scalar_tensor_tensor(W1B[64:128, sl], STAGE[n % 2][64:128], W_UP,
                                                            W1B[64:128, sl], ALU.mult, ALU.subtract)
                        else:
                            lo = {"a": W1AL, "2": W2LF}[kind][:, sl]
                            last = dve.scalar_tensor_tensor(lo, STAGE[n % 2], W_UP, hi, ALU.mult, ALU.subtract)
                        last.then_inc(piece_free, 1)
                    dve.wait_ge(piece_free, len(pieces))
                    dve.memset(STG[0:1, 0, 6:7], 0.0).then_inc(weights_ready, 1)

                @block.scalar
                def _(act):
                    act.wait_ge(loaded, 16 * len(small))
                    act.activation(SIG, SA, ACT.Tanh, scale=0.5).then_inc(act_step, 1)

                @block.tensor
                def _(pe):
                    pe.wait_ge(loaded, 16 * len(small))
                    pe.wait_ge(dve_step, marks["g1"])
                    for j in range(2):
                        mm = pe.matmul(PSUM[0:HC, 0, 0:32], CAVG, G1N[:, j, :], start=(j == 0), stop=(j == 1))
                    mm.then_inc(pe_step, 1)
                    pe.matmul(PSUM[:, 1, 0:32], ONE1, G1B, start=True, stop=False)
                    for j in range(2):
                        mm = pe.matmul(PSUM[:, 1, 0:32], NBB[:, j, :], G1W[:, j, :], start=False, stop=(j == 1))
                    mm.then_inc(pe_step, 1)
                    pe.matmul(PSUM[0:2 * S, 2, 0:2 * S], SV, SU, start=True, stop=True).then_inc(pe_step, 1)
                    m = 1
                    steps = marks["power"]
                    pe.wait_ge(dve_step, steps)
                    while m < 32:
                        pe.transpose(PSUM[0:2 * S, 3, 0:2 * S], PW[:, m, :], EYE[0:2 * S, 0:2 * S]).then_inc(pe_step, 1)
                        steps += 1
                        pe.wait_ge(dve_step, steps)
                        k = min(m, 31 - m)
                        if k:
                            pe.matmul(PSUM[0:2 * S, 4, 0:32 * k], AT, PW[:, 1:1 + k, :], start=True, stop=True
                                      ).then_inc(pe_step, 1)
                            steps += 1
                            pe.wait_ge(dve_step, steps)
                        m *= 2

        s = {n: sem("i_" + n) for n in PER}
        dve_link = sem("dve_link")

        def at(name, i, k):
            return i * PER[name] + k

        def first(i):
            return isinstance(i, int)

        def bank(n):
            return PSUM[:, n, :]

        def empty(n):
            for _ in range(n):
                yield

        def step(work):
            next(work, None)

        def windows(copy, j, part, give):
            if part == 0:
                copy(XW[:, j, 1:NB - 1, 0:KW],
                     window_view(PSUM, j * T + QB - PAD + 1, [HC, [QB, NB - 2], [1, KW]]))
                return
            copy(XW[:, j, 0, PAD - 1:KW], window_view(PSUM, j * T, [HC, [1, KW - PAD + 1]]))
            last = (NB - 1) * QB - PAD + 1
            copy(XW[:, j, NB - 1, 0:T - last], window_view(PSUM, j * T + last, [HC, [1, T - last]]))
            copy(XW[:, j, :, KW], window_view(PSUM, j * T, [HC, [0, NB]])).then_inc(give, 1)

        SPANS = [(0, 4), (4, 8), (8, NB)]
        PIECES = 18
        PIECE_SLOT = [18 + (3 * n) // 2 for n in range(PIECES)]
        act_engine = nc.scalar

        def evacuate_piece(eng, n, give):
            src = bank(n % 4)
            is_act = eng is act_engine
            if n < 6:
                oh, (b0, b1) = n // 3, SPANS[n % 3]
                k = b1 - b0
                parts = [(QT[:, oh, b0:b1, 1:QS], src[0:HC, 0:k * QB].rearrange("p (b q) -> p b q", b=k))]
                if n % 3 == 2:
                    col = src[0:HC, 400:401].broadcast_to((HC, NB))
                    parts.append((QT[:, oh, :, 0], col))
                for dst, ps in parts:
                    if is_act:
                        last = eng.activation(dst, ps, ACT.Identity, bias=BQS[:, oh:oh + 1], scale=HD ** -0.5)
                    else:
                        last = eng.tensor_scalar(dst, ps, BQ[:, oh:oh + 1], HD ** -0.5, ALU.add, ALU.mult)
            elif n < 12:
                oh, (b0, b1) = (n - 6) // 3, SPANS[n % 3]
                k = b1 - b0
                for h in range(HH):
                    p = slice(h * HD, (h + 1) * HD)
                    dst = KBD[p, oh, b0:b1, h, :]
                    ps = src[p, 0:k * KS].rearrange("p (b q) -> p b q", b=k)
                    if is_act:
                        last = eng.activation(dst, ps, ACT.Identity, bias=BK[p, oh:oh + 1])
                    else:
                        last = eng.tensor_scalar(dst, ps, BK[p, oh:oh + 1], None, ALU.add)
            else:
                b0 = 2 * (n - 12)
                k = min(2, NB - b0)
                dst = VW[:, b0:b0 + k, :]
                ps = src[0:KS, 0:k * C].rearrange("p (b q) -> p b q", b=k)
                last = eng.copy(dst, ps) if is_act else eng.tensor_copy(dst, ps)
            last.then_inc(give, 1)

        OSPANS = [(0, 4), (4, 8), (8, NB)]

        def evacuate_oT(eng, n, i):
            oh, (b0, b1) = n // 3, OSPANS[n % 3]
            eng.wait_ge(s["oT_done"], at("oT_done", i, n + 1))
            src = bank(n % 4)
            w = (b1 - b0) * QB
            parts = [(OT[:, oh, 1 + b0 * QB:1 + b1 * QB], src[0:HC, 0:w])]
            if n % 3 == 2:
                parts.append((OT[:, oh, 0:1], src[0:HC, 400:401]))
            for dst, ps in parts:
                if eng is act_engine:
                    last = eng.activation(dst, ps, ACT.Identity, bias=BV[:, oh:oh + 1])
                else:
                    last = eng.tensor_scalar(dst, ps, BV[:, oh:oh + 1], None, ALU.add)
            last.then_inc(s["oT_copied"], 1)

        block = ctx.enter_context(nc.Block())

        @block.sync
        def _(sp):
            with sp.Fori(0, B) as i:
                for kind in range(2):
                    sp.wait_ge(s["gu_ready"], at("gu_ready", i, kind + 1))
                    src = GU[32 * kind:32 * kind + S, :].rearrange("s (c i n) -> s c i n", c=KC, i=KP)
                    for k in range(KP):
                        sp.dma_start(GUP[S * k:S * k + S, kind, :, :], src[:, :, k, :]).then_inc(s["gu_moved"], 16)
                sp.wait_ge(s["hs_copied"], at("hs_copied", i, 1))
                for kind in range(2):
                    dst = (HST.rearrange("s (c i) n -> s c i n", i=KP) if kind == 0 else
                           XG[97:113, 1, :].rearrange("s (c i n) -> s c i n", c=KC, i=KP))
                    for k in range(KP):
                        sp.dma_start(dst[:, :, k, :], HSP[S * k:S * k + S, kind, :, :]).then_inc(s["hs_moved"], 16)
                sp.wait_ge(s["hs_permuted"], at("hs_permuted", i, 1))
                sp.dma_start(XG[97:113, 0, :], HST2).then_inc(s["hs_placed"], 16)

        @block.gpsimd
        def _(pool):
            def rstd(i, dst, src, width, wait, give):
                pool.wait_ge(s[wait], at(wait, i, 1))
                pool.tensor_tensor(dst, src, MHALF[0:dst.shape[0], 0:width], ALU.pow).then_inc(s[give], 1)

            def conv_first(i):
                rstd(i, GR[:], GV[:], 2, "gn_eps", "gn_rstd")
                rstd(i, TR[:], TV[:], NT, "mixln_eps", "mixln_rstd")
                pool.wait_ge(s["hs_moved"], at("hs_moved", i, 16 * 2 * KP))
                pool.tensor_tensor(PSPARE, PSPARE, PSPARE, ALU.mult)
                pool.tensor_copy(HST2.rearrange("s (h w) -> s h w", h=GH), HST.rearrange("s w h -> s h w")
                                 ).then_inc(s["hs_permuted"], 1)

            def attention_rest(i):
                pool.wait_ge(s["cls_coef"], at("cls_coef", i, 1))
                pool.tensor_tensor(CP.rearrange("p b (h d) -> p b h d", h=HEADS),
                                   OS[0:1, :, :].rearrange("p b (h d) -> p b h d", h=HEADS),
                                   CW[:].unsqueeze(3).broadcast_to((1, NB, HEADS, HD)), ALU.mult
                                   ).then_inc(s["cls_mult"], 1)
                rstd(i, TR[:], TV[:], NT, "ln2_eps", "ln2_rstd")

            conv_first(0)
            rstd(0, TR[:], TV[:], NT, "ln1_eps", "ln1_rstd")
            with pool.Fori(0, B - 1) as i:
                conv_first(i + 1)
                attention_rest(i)
                rstd(i + 1, TR[:], TV[:], NT, "ln1_eps", "ln1_rstd")
            attention_rest(B - 1)

        @block.scalar
        def _(act):
            def load(i):
                if not first(i):
                    act.wait_ge(s["xs_ready"], at("xs_ready", i, 0))
                act.dma_start(XR[:], x[bass.ds(i, 1)].rearrange("o p j t -> (o p) j t")).then_inc(s["x_loaded"], 16)

            def conv_first(i):
                yield from empty(9)
                act.wait_ge(s["proj_done"], at("proj_done", i, 1))
                act.activation(TG.rearrange("p (a b) -> p a b", a=2), PSUM[64:128, 6:8, :], ACT.Tanh, scale=0.5
                               ).then_inc(s["tanh_done"], 1)
                yield from empty(8)
                act.wait_ge(s["scan_done"], at("scan_done", i, 1))
                act.activation(HSP[:].rearrange("p a b c -> p (a b c)"), PSUM[:, 6, 0:2 * KC * GW], ACT.Copy
                               ).then_inc(s["hs_copied"], 1)
                yield

            def conv_second(i):
                act.wait_ge(s["hs_placed"], at("hs_placed", i, 16))
                act.wait_ge(s["h1_pre"], at("h1_pre", i, 1))
                act.activation(H1[:], H1[:], ACT.Gelu).then_inc(s["h1_gelu"], 1)
                yield
                yield
                act.wait_ge(s["h1T_done"], at("h1T_done", i, 1))
                act.activation(H1T[:].rearrange("p a b -> p (a b)"), PSUM[:, 2, 0:256], ACT.Copy
                               ).then_inc(s["h1T_copied"], 1)
                yield
                for tp in range(NP):
                    act.wait_ge(s["mix_done"], at("mix_done", i, tp + 1))
                    if tp:
                        act.wait_ge(s["mixed"], at("mixed", i, tp))
                    act.activation(TM[:], PSUM[:, 0, 0:2 * C], ACT.Tanh, scale=0.5).then_inc(s["mix_tanh"], 1)
                    yield from empty(2)
                yield from empty(5)
                act.wait_ge(s["xn1T_done"], at("xn1T_done", i, 1))
                windows(act.copy, 0, 0, s["win_act"])
                yield
                windows(act.copy, 0, 1, s["win_act"])
                yield
                for slot in range(PIECE_SLOT[0], PIECE_SLOT[-1] + 1):
                    if slot in PIECE_SLOT and PIECE_SLOT.index(slot) % 2 == 0:
                        n = PIECE_SLOT.index(slot)
                        act.wait_ge(s["piece_done"], at("piece_done", i, n + 1))
                        evacuate_piece(act, n, s["piece_act"])
                    yield

            def attention(i, side):
                for n in range(2 * NB + 2):
                    if n < 2 * NB:
                        b, oh = n // 2, n % 2
                        act.wait_ge(s["max_done"], at("max_done", i, n + 1))
                        if n >= 2:
                            act.wait_ge(s["pT_done"], at("pT_done", i, n - 1))
                        for h in range(HH):
                            e = act.activation(PS[:, n % 2, h, :], PSUM[0:QS, n % 2, h * KS:(h + 1) * KS], ACT.Exp,
                                               bias=NMX[:, b, oh, h:h + 1], accum_out=DEN[:, b, oh, h:h + 1])
                        e.then_inc(s["exp_done"], 1)
                    step(side)
                act.wait_ge(s["cls_weight"], at("cls_weight", i, 1))
                act.activation(CW[:], CW[:], ACT.Exp).then_inc(s["cls_exp"], 1)
                for n in range(6):
                    if n % 2 == 0:
                        evacuate_oT(act, n, i)
                act.wait_ge(s["xn2T_done"], at("xn2T_done", i, 1))
                for a in range(2):
                    act.activation(XH[:, a, :].rearrange("p (a b) -> p a b", a=2), PSUM[:, 2 * a:2 * a + 2, :],
                                   ACT.Copy, scale=X_UP).then_inc(s["xh_ready"], 1)
                act.wait_ge(s["route_shift"], at("route_shift", i, 1))
                act.activation(SE[:], SC[:], ACT.Exp).then_inc(s["route_exp"], 1)

            def store(i, half):
                act.wait_ge(s["ffn_added"], at("ffn_added", i, E * (half + 1)))
                tiles = slice(NT // 2 * half, NT // 2 * (half + 1))
                act.dma_start(out[bass.ds(i, 1)].rearrange("o p t c -> (o p) t c")[:, tiles, :], X2[:, tiles, :]
                              ).then_inc(s["x2_free"], 16)

            def experts(i, side):
                for n in range(NCHUNK):
                    ek = n % (E * HK)
                    act.wait_ge(s["ffn1_done"], at("ffn1_done", i, n + 1))
                    if n >= 2:
                        act.wait_ge(s["hl_ready"], at("hl_ready", i, n - 1))
                    act.activation(HF[:, n % 2, :], PSUM[:, 4 + n % 2, :], ACT.Gelu, scale=1 / (X_UP * W_UP),
                                   bias=B1[:, ek:ek + 1]).then_inc(s["gelu_done"], 1)
                    if n == NCHUNK // 2 + 4:
                        store(i, 0)
                    step(side)
                store(i, 1)

            load(0)
            for _ in conv_first(0):
                pass
            for _ in conv_second(0):
                pass
            with act.Fori(0, B - 1) as i:
                load(i + 1)
                attention(i, conv_first(i + 1))
                side = conv_second(i + 1)
                step(side)
                experts(i, side)
            attention(B - 1, iter(()))
            experts(B - 1, iter(()))
            act.wait_ge(s["x2_free"], at("x2_free", B, 1))

        links, link_base = [0], [0]

        @block.vector
        def _(dve):
            def link(ins):
                links[0] += 1
                ins.then_inc(dve_link, 1)
                dve.wait_ge(dve_link, link_base[0] + links[0])

            def norm_stats(i, src, eps, eps_sem):
                for t in range(NT):
                    last = dve.bn_stats(TST[:, t, :], src[:, t, :])
                link(last)
                aggregate(eps, eps_sem)

            def aggregate(eps, eps_sem):
                dve.memset(SPARE, 0.0)
                for t in range(NT):
                    last = dve.bn_aggr(TMV[:, t, :], TST[:, t, :])
                link(last)
                dve.tensor_scalar(TV[:], TMV[:, :, 1], eps, None, ALU.add).then_inc(s[eps_sem], 1)

            def norm_tokens(src, tiles, c0, dst0):
                for t in tiles:
                    last = dve.tensor_scalar(XN[:, t, dst0:dst0 + C - c0], src[:, t, c0:C], TMV[:, t, 0:1],
                                             TR[:, t:t + 1], ALU.subtract, ALU.mult)
                return last

            def conv_first(i):
                yield from empty(2)
                dve.wait_ge(s["x_loaded"], at("x_loaded", i, 16))
                for j in range(2):
                    for h in range(2):
                        last = dve.bn_stats(GST[:, j, h, :], XR[:, j, 512 * h:512 * h + 512])
                link(last)
                dve.memset(SPARE, 0.0)
                for j in range(2):
                    last = dve.bn_aggr(MV[:, j, :], GST[:, j, :, :].rearrange("p a b -> p (a b)"))
                last.then_inc(s["gn_channel"], 1)
                yield
                dve.wait_ge(s["gn_channel"], at("gn_channel", i, 1))
                dve.wait_ge(s["gn_mean"], at("gn_mean", i, 1))
                link(dve.tensor_copy(GM[:], PSUM[0:HC, 6, 0:2]))
                link(dve.tensor_tensor(GD[:], MV[:, :, 0], GM[:], ALU.subtract))
                link(dve.tensor_tensor(GD[:], GD[:], GD[:], ALU.mult))
                dve.tensor_tensor(GD[:], GD[:], MV[:, :, 1], ALU.add).then_inc(s["gn_spread"], 1)
                yield
                dve.wait_ge(s["gn_var"], at("gn_var", i, 1))
                dve.tensor_scalar(GV[:], PSUM[0:HC, 6, 2:4], 1e-5, None, ALU.add).then_inc(s["gn_eps"], 1)
                yield
                dve.wait_ge(s["gn_rstd"], at("gn_rstd", i, 1))
                link(dve.scalar_tensor_tensor(GNB[:], GM[:], -1.0, GR[:], ALU.mult, ALU.mult))
                link(dve.tensor_scalar(GR1[:], GR[:], 1.0, None, ALU.add))
                if not first(i):
                    dve.wait_ge(s["mix_done"], at("mix_done", i, 0))
                for j in range(2):
                    dve.tensor_scalar(XG[0:HC, j, :], XR[:, j, :], GM[:, j:j + 1], GR[:, j:j + 1], ALU.subtract,
                                      ALU.mult).then_inc(s["xg_ready"], 1)
                    yield
                for j in range(2):
                    dve.tensor_scalar(XS[:, j, :], XR[:, j, :], GR1[:, j:j + 1], GNB[:, j:j + 1], ALU.mult,
                                      ALU.add).then_inc(s["xs_ready"], 1)
                    yield
                yield
                dve.wait_ge(s["tanh_done"], at("tanh_done", i, 1))
                dve.scalar_tensor_tensor(GU[0:S, :].rearrange("p (w h) -> p h w", w=GW),
                                         TG[0:S, :].rearrange("p (h w) -> p h w", w=GW), 1.0,
                                         PSUM[0:S, 6:8, :].rearrange("p a (h w) -> p (a h) w", w=GW),
                                         ALU.add, ALU.mult).then_inc(s["gu_ready"], 1)
                yield
                dve.scalar_tensor_tensor(GU[32:32 + S, :].rearrange("p (a b) -> p a b", a=2),
                                         TG[32:32 + S, :].rearrange("p (a b) -> p a b", a=2), 1.0,
                                         PSUM[32:32 + S, 6:8, :],
                                         ALU.add, ALU.mult).then_inc(s["gu_ready"], 1)
                yield
                for tp in range(NP):
                    dve.wait_ge(s["xgT_done"], at("xgT_done", i, tp + 1))
                    for t in range(2):
                        dve.bn_stats(TST[:, 2 * tp + t, :], PSUM[:, 6 + tp % 2, t * C:(t + 1) * C])
                    dve.tensor_copy(H1[:, 2 * tp:2 * tp + 2, :],
                                    PSUM[:, 6 + tp % 2, 2 * C:2 * C + 64].rearrange("p (t o) -> p t o", t=2)
                                    ).then_inc(s["h1_read"], 1)
                    if tp < NP - 1:
                        yield
                dve.wait_ge(s["h1_read"], at("h1_read", i, NP))
                aggregate(1e-6, "mixln_eps")
                yield
                yield
                dve.wait_ge(s["mixln_rstd"], at("mixln_rstd", i, 1))
                link(dve.tensor_tensor(H1[:], H1[:], TR[:].unsqueeze(2).broadcast_to((128, NT, 32)), ALU.mult))
                dve.tensor_tensor(H1[:], H1[:], BG1[:].unsqueeze(1).broadcast_to((128, NT, 32)), ALU.add
                                  ).then_inc(s["h1_pre"], 1)
                yield

            def conv_second(i):
                yield from empty(4)
                for tp in range(NP):
                    dve.wait_ge(s["mix_tanh"], at("mix_tanh", i, tp + 1))
                    link(dve.scalar_tensor_tensor(EM[:], TM[:], 1.0, PSUM[:, 1 + tp % 2, 0:2 * C], ALU.add, ALU.mult))
                    dve.scalar_tensor_tensor(X1[:, 2 * tp:2 * tp + 2, :].rearrange("p a b -> p (a b)"), EM[:], 0.5,
                                             PSUM[:, 3, 0:2 * C], ALU.mult, ALU.add).then_inc(s["mixed"], 1)
                    yield
                    if tp < NP - 1:
                        yield
                dve.wait_ge(s["mixed"], at("mixed", i, NP))
                norm_stats(i, X1, 1e-5, "ln1_eps")
                yield
                dve.wait_ge(s["ln1_rstd"], at("ln1_rstd", i, 1))
                for k in range(2):
                    norm_tokens(X1, range(4 * k, 4 * k + 4), 0, 0).then_inc(s["xn1_ready"], 1)
                    yield
                yield
                dve.wait_ge(s["xn1T_done"], at("xn1T_done", i, 1))
                windows(dve.tensor_copy, 1, 0, s["win_dve"])
                yield
                windows(dve.tensor_copy, 1, 1, s["win_dve"])
                yield
                yield
                for slot in range(PIECE_SLOT[0], PIECE_SLOT[-1] + 1):
                    if slot in PIECE_SLOT and PIECE_SLOT.index(slot) % 2 == 1:
                        n = PIECE_SLOT.index(slot)
                        dve.wait_ge(s["piece_done"], at("piece_done", i, n + 1))
                        evacuate_piece(dve, n, s["piece_dve"])
                    yield

            def attention(i, side):
                def after_scores(n):
                    b, oh = n // 2, n % 2
                    dve.wait_ge(s["pT_done"], at("pT_done", i, n + 1))
                    dve.tensor_copy(PT[:, n % 2, :, :], PSUM[0:KS, 2 + n % 2, 0:HH * QS].rearrange(
                        "p (h q) -> p h q", h=HH)).then_inc(s["pT_copied"], 1)

                def normalize(b):
                    dve.wait_ge(s["exp_done"], at("exp_done", i, 2 * b + 2))
                    link(dve.reciprocal(RDEN[:, b, :, :], DEN[:, b, :, :]))
                    dve.wait_ge(s["pv_done"], at("pv_done", i, b + 1))
                    dve.tensor_tensor(OS[:, b, :].rearrange("p (h d) -> p h d", h=HEADS),
                                      PSUM[0:QS, 4 + b % 2, 0:C].rearrange("p (h d) -> p h d", h=HEADS),
                                      RDEN[:, b, :, :].rearrange("p a h -> p (a h)").unsqueeze(2).broadcast_to(
                                          (QS, HEADS, HD)), ALU.mult).then_inc(s["o_normed"], 1)

                for n in range(2 * NB + 2):
                    if n < 2 * NB:
                        dve.wait_ge(s["score_done"], at("score_done", i, n + 1))
                        dve.tensor_reduce(NMX[:, n // 2, n % 2, :],
                                          PSUM[0:QS, n % 2, 0:HH * KS].rearrange("p (h k) -> p h k", h=HH), AX.X,
                                          ALU.max, negate=True).then_inc(s["max_done"], 1)
                    if n >= 2:
                        after_scores(n - 2)
                    if n >= 4 and n % 2 == 0:
                        normalize((n - 4) // 2)
                    step(side)
                normalize(NB - 1)
                nm = NMX[0:1].rearrange("p b a h -> p b (a h)")
                link(dve.tensor_reduce(CM[:], NMX[0:1].rearrange("p b a h -> p (a h) b"), AX.X, ALU.min))
                dve.scalar_tensor_tensor(CW[:], nm, -1.0, CM[:].unsqueeze(1).broadcast_to((1, NB, HEADS)), ALU.mult,
                                         ALU.add).then_inc(s["cls_weight"], 1)
                dve.wait_ge(s["cls_exp"], at("cls_exp", i, 1))
                link(dve.tensor_tensor(CW[:], CW[:], DEN[0:1].rearrange("p b a h -> p b (a h)"), ALU.mult))
                link(dve.tensor_reduce(CSUM[:], CW[:].rearrange("p b h -> p h b"), AX.X, ALU.add))
                link(dve.reciprocal(CSUM[:], CSUM[:]))
                dve.tensor_tensor(CW[:], CW[:], CSUM[:].unsqueeze(1).broadcast_to((1, NB, HEADS)), ALU.mult
                                  ).then_inc(s["cls_coef"], 1)
                dve.wait_ge(s["cls_mult"], at("cls_mult", i, 1))
                dve.tensor_reduce(CO[:], CP.rearrange("p b c -> p c b"), AX.X, ALU.add).then_inc(s["cls_sum"], 1)
                for n in range(6):
                    if n % 2:
                        evacuate_oT(dve, n, i)
                dve.wait_ge(s["x2_free"], at("x2_free", i, 1))
                for tp in range(NP):
                    dve.wait_ge(s["wo_done"], at("wo_done", i, tp + 1))
                    pair = slice(2 * tp, 2 * tp + 2)
                    dve.tensor_tensor(X2[:, pair, :].rearrange("p a b -> p (a b)"),
                                      X1[:, pair, :].rearrange("p a b -> p (a b)"),
                                      PSUM[:, 4 + tp % 2, 0:2 * C], ALU.add).then_inc(s["x2_ready"], 1)
                dve.wait_ge(s["x2_ready"], at("x2_ready", i, NP))
                norm_stats(i, X2, 1e-5, "ln2_eps")
                dve.wait_ge(s["ln2_rstd"], at("ln2_rstd", i, 1))
                norm_tokens(X2, range(NT), 0, 0)
                norm_tokens(X2, range(NT), 128, C).then_inc(s["xn2_ready"], 1)
                for a in range(2):
                    dve.wait_ge(s["xh_ready"], at("xh_ready", i, a + 1))
                    dve.scalar_tensor_tensor(XL[:, a, :].rearrange("p (a b) -> p a b", a=2),
                                             PSUM[:, 2 * a:2 * a + 2, :], X_UP,
                                             XH[:, a, :].rearrange("p (a b) -> p a b", a=2), ALU.mult, ALU.subtract
                                             ).then_inc(s["xl_ready"], 1)
                dve.wait_ge(s["route_done"], at("route_done", i, 1))
                gb = GB[:].unsqueeze(1).broadcast_to((128, NT, E))
                link(dve.scalar_tensor_tensor(SC[:], PSUM[:, 4, 0:NT * E].rearrange("p (t e) -> p t e", t=NT),
                                              1 / (X_UP * W_UP), gb, ALU.mult, ALU.add))
                link(dve.tensor_reduce(SM[:], SC[:], AX.X, ALU.max))
                sm = SM[:].unsqueeze(2).broadcast_to((128, NT, E))
                dve.tensor_tensor(SC[:], SC[:], sm, ALU.subtract).then_inc(s["route_shift"], 1)

            def gates(i):
                sm = SM[:].unsqueeze(2).broadcast_to((128, NT, E))
                dve.wait_ge(s["route_exp"], at("route_exp", i, 1))
                link(dve.tensor_reduce(SM[:], SE[:], AX.X, ALU.add))
                link(dve.reciprocal(SM[:], SM[:]))
                link(dve.tensor_tensor(SE[:], SE[:], sm, ALU.mult))
                mine = SE[:].unsqueeze(3).broadcast_to((128, NT, E, E))
                other = SE[:].unsqueeze(2).broadcast_to((128, NT, E, E))
                dve.tensor_tensor(CMPA[:], mine, other, ALU.is_ge)
                link(dve.tensor_tensor(CMPB[:], mine, other, ALU.is_gt))
                dve.tensor_tensor(CMPA[:], CMPA[:], AFTER[:].unsqueeze(1).broadcast_to((128, NT, E, E)), ALU.mult)
                link(dve.tensor_tensor(CMPB[:], CMPB[:], BEFORE[:].unsqueeze(1).broadcast_to((128, NT, E, E)),
                                       ALU.mult))
                link(dve.tensor_tensor(CMPA[:], CMPA[:], CMPB[:], ALU.add))
                link(dve.tensor_reduce(WIN[:], CMPA[:], AX.X, ALU.add))
                link(dve.scalar_tensor_tensor(WIN[:], WIN[:], 2.0, SE[:], ALU.is_ge, ALU.mult))
                link(dve.tensor_reduce(SM[:], WIN[:], AX.X, ALU.add))
                link(dve.tensor_scalar(SM[:], SM[:], 1e-9, None, ALU.add))
                link(dve.reciprocal(SM[:], SM[:]))
                dve.scalar_tensor_tensor(GATE[:], WIN[:], 1 / (W_UP * H_UP), sm, ALU.mult, ALU.mult
                                         ).then_inc(s["gates_ready"], 1)

            def experts(i, side):
                def split(n):
                    dve.wait_ge(s["gelu_done"], at("gelu_done", i, n + 1))
                    if n >= 2:
                        dve.wait_ge(s["ffn2_chunk"], at("ffn2_chunk", i, n - 1))
                    dve.tensor_scalar(HHI[:, n % 2, :], HF[:, n % 2, :], H_UP, None, ALU.mult
                                      ).then_inc(s["hh_ready"], 1)
                    dve.wait_ge(s["hh_ready"], at("hh_ready", i, n + 1))
                    dve.scalar_tensor_tensor(HLO[:, n % 2, :], HF[:, n % 2, :], H_UP, HHI[:, n % 2, :], ALU.mult,
                                             ALU.subtract).then_inc(s["hl_ready"], 1)

                def add_expert(g):
                    half, e = divmod(g, E)
                    dve.wait_ge(s["ffn2_chunk"], at("ffn2_chunk", i, (g + 1) * HK))
                    if g:
                        dve.wait_ge(s["ffn_added"], at("ffn_added", i, g))
                    else:
                        dve.wait_ge(s["gates_ready"], at("gates_ready", i, 1))
                    for q in range(4):
                        t = 4 * half + q
                        last = dve.scalar_tensor_tensor(X2[:, t, :], PSUM[:, 6 + q // 2, (q % 2) * C:(q % 2 + 1) * C],
                                                        GATE[:, t, e:e + 1], X2[:, t, :], ALU.mult, ALU.add)
                    last.then_inc(s["ffn_added"], 1)

                for n in range(NCHUNK):
                    if n > 1 and n % HK == 1:
                        add_expert(n // HK - 1)
                    split(n)
                    if n == 2:
                        gates(i)
                    step(side)
                add_expert(NHALF * E - 1)

            dve.memset(SPARE, 0.0).then_inc(s["x2_free"], 1)
            for _ in conv_first(0):
                pass
            for _ in conv_second(0):
                pass
            assert links[0] == LINKS_FIRST, links[0]
            with dve.Fori(0, B - 1) as i:
                links[0], link_base[0] = 0, LINKS_FIRST + i * LINKS
                attention(i, conv_first(i + 1))
                experts(i, conv_second(i + 1))
                assert links[0] == LINKS, links[0]
            links[0], link_base[0] = 0, LINKS_FIRST + (B - 1) * LINKS
            attention(B - 1, iter(()))
            experts(B - 1, iter(()))

        @block.tensor
        def _(pe):
            def conv_first(i):
                yield from empty(3)
                pe.wait_ge(s["gn_channel"], at("gn_channel", i, 1))
                pe.matmul(PSUM[0:HC, 6, 0:2], GAVG[:], MV[:, :, 0], start=True, stop=True).then_inc(s["gn_mean"], 1)
                yield
                pe.wait_ge(s["gn_spread"], at("gn_spread", i, 1))
                pe.matmul(PSUM[0:HC, 6, 2:4], GAVG[:], GD[:], start=True, stop=True).then_inc(s["gn_var"], 1)
                yield
                yield from empty(2)
                for half in range(2):
                    pe.wait_ge(s["xg_ready"], at("xg_ready", i, 2))
                    for j in range(2):
                        k = 97 - j
                        mm = pe.matmul(bank(6 + half), PROJ[0:k, j, :], XG[0:k, j, half * 512:(half + 1) * 512],
                                       start=(j == 0), stop=(j == 1))
                    if half == 1:
                        mm.then_inc(s["proj_done"], 1)
                    yield
                yield from empty(3)
                pe.wait_ge(s["gu_ready"], at("gu_ready", i, 2))
                for tp in range(NP):
                    if tp >= 2:
                        pe.wait_ge(s["h1_read"], at("h1_read", i, tp - 1))
                    for t in range(2):
                        tok = slice((2 * tp + t) * 128, (2 * tp + t + 1) * 128)
                        for j in range(2):
                            pe.transpose(PSUM[:, 6 + tp % 2, t * C + j * HC:t * C + (j + 1) * HC],
                                         XG[0:HC, j, tok], EYE[0:HC, 0:HC])
                        for j in range(2):
                            mm = pe.matmul(PSUM[:, 6 + tp % 2, 2 * C + t * 32:2 * C + (t + 1) * 32],
                                           XG[0:HC, j, tok], WG1[:, j, :], start=(j == 0), stop=(j == 1))
                    mm.then_inc(s["xgT_done"], 1)
                    yield
                pe.wait_ge(s["h1_read"], at("h1_read", i, NP))
                pe.wait_ge(s["gu_moved"], at("gu_moved", i, 16 * 2 * KP))
                for kind in range(2):
                    for ct in range(KC):
                        for cp in range(KC):
                            mm = pe.matmul(PSUM[:, 6, (kind * KC + ct) * GW:(kind * KC + ct + 1) * GW],
                                           SCAN[:, kind, ct - cp + KC - 1, :], GUP[:, kind, cp, :],
                                           start=(cp == 0), stop=(cp == KC - 1))
                    if kind == 1:
                        mm.then_inc(s["scan_done"], 1)
                    yield

            def conv_second(i):
                pe.wait_ge(s["hs_copied"], at("hs_copied", i, 1))
                yield
                yield
                pe.wait_ge(s["h1_gelu"], at("h1_gelu", i, 1))
                for g in range(2):
                    mm = pe.transpose(PSUM[:, 2, g * 128:(g + 1) * 128],
                                      H1[:, 4 * g:4 * g + 4, :].rearrange("p a b -> p (a b)"), EYE[:])
                mm.then_inc(s["h1T_done"], 1)
                yield
                yield
                pe.wait_ge(s["h1T_copied"], at("h1T_copied", i, 1))
                pe.wait_ge(s["hs_moved"], at("hs_moved", i, 16 * 2 * KP))
                pe.wait_ge(s["hs_placed"], at("hs_placed", i, 16))
                pe.wait_ge(s["xs_ready"], at("xs_ready", i, 2))
                for tp in range(NP):
                    if tp:
                        pe.wait_ge(s["mixed"], at("mixed", i, tp))
                    for t in range(2):
                        tt = 2 * tp + t
                        tok = slice(tt * 128, tt * 128 + 128)
                        col = slice(t * C, (t + 1) * C)
                        pe.matmul(PSUM[:, 0, col], H1T[:, tt // 4, :], WG2[:, tt % 4, :], start=True, stop=False)
                        pe.matmul(PSUM[:, 0, col], ONES3[:], ROWS3[:, 0:C], start=False, stop=True)
                        for j in range(2):
                            pe.matmul(PSUM[:, 1 + tp % 2, col], XG[0:113, j, tok], WY[:, j, :], start=(j == 0),
                                      stop=(j == 1))
                        for j in range(2):
                            mm = pe.transpose(PSUM[:, 3, t * C + j * HC:t * C + (j + 1) * HC], XS[:, j, tok],
                                              EYE[0:HC, 0:HC])
                    mm.then_inc(s["mix_done"], 1)
                    yield from empty(2)
                yield from empty(2)
                pe.wait_ge(s["mixed"], at("mixed", i, NP))
                for k in range(2):
                    pe.wait_ge(s["xn1_ready"], at("xn1_ready", i, k + 1))
                    for t in range(4 * k, 4 * k + 4):
                        for j in range(2):
                            mm = pe.transpose(PSUM[0:HC, 2 * j + t // 4, (t % 4) * 128:(t % 4 + 1) * 128],
                                              XN[:, t, j * HC:(j + 1) * HC], EYE[:])
                    if k == 1:
                        mm.then_inc(s["xn1T_done"], 1)
                    yield
                yield from empty(3)
                pe.wait_ge(s["win_act"], at("win_act", i, 1))
                pe.wait_ge(s["win_dve"], at("win_dve", i, 1))
                for slot in range(PIECE_SLOT[0], PIECE_SLOT[-1] + 1):
                    if slot in PIECE_SLOT:
                        project(i, PIECE_SLOT.index(slot))
                    yield

            def project(i, n):
                if n >= 4:
                    m = n - 4
                    nm = ("piece_act", "piece_dve")[m % 2]
                    pe.wait_ge(s[nm], at(nm, i, m // 2 + 1))
                if n < 12:
                    W = WQ if n < 6 else WK
                    oh, (b0, b1) = (n % 6) // 3, SPANS[n % 3]
                    keys = slice(PAD, PAD + QB) if n < 6 else slice(0, KS)
                    width = (b1 - b0) * (QB if n < 6 else KS)
                    for j in range(2):
                        mm = pe.matmul(PSUM[0:HC, n % 4, 0:width], W[:, j, oh * HC:(oh + 1) * HC],
                                       XW[:, j, b0:b1, keys], start=(j == 0), stop=(j == 1))
                    if n < 6 and n % 3 == 2:
                        for j in range(2):
                            mm = pe.matmul(PSUM[0:HC, n % 4, 400:401], W[:, j, oh * HC:(oh + 1) * HC],
                                           XW[:, j, 0, KW:KS], start=(j == 0), stop=(j == 1))
                else:
                    for b in range(2 * (n - 12), min(2 * (n - 12) + 2, NB)):
                        for j in range(2):
                            mm = pe.matmul(PSUM[0:KS, n % 4, (b % 2) * C:(b % 2 + 1) * C], XW[:, j, b, :],
                                           WV[:, j, :], start=(j == 0), stop=(j == 1))
                mm.then_inc(s["piece_done"], 1)

            def attention(i, side):
                pe.wait_ge(s["piece_act"], at("piece_act", i, PIECES // 2))
                pe.wait_ge(s["piece_dve"], at("piece_dve", i, PIECES // 2))

                def scores(n):
                    b, oh = n // 2, n % 2
                    if n >= 2:
                        pe.wait_ge(s["exp_done"], at("exp_done", i, n - 1))
                    pe.matmul(PSUM[0:QS, n % 2, 0:HH * KS], QT[:, oh, b, :],
                              KBD[:, oh, b, :, :].rearrange("p h k -> p (h k)"), start=True, stop=False)
                    v = 0 if b == 0 else 2 if b == NB - 1 else 1
                    pe.matmul(PSUM[0:QS, n % 2, 0:HH * KS], EYEB[:], MASKB[:, v, :], start=False, stop=True
                              ).then_inc(s["score_done"], 1)

                def turn(n):
                    pe.wait_ge(s["exp_done"], at("exp_done", i, n + 1))
                    if n >= 2:
                        pe.wait_ge(s["pT_copied"], at("pT_copied", i, n - 1))
                    for h in range(HH):
                        mm = pe.transpose(PSUM[0:KS, 2 + n % 2, h * QS:(h + 1) * QS], PS[:, n % 2, h, :],
                                          EYE[0:QS, 0:QS])
                    mm.then_inc(s["pT_done"], 1)

                def values(n):
                    b, oh = n // 2, n % 2
                    pe.wait_ge(s["pT_copied"], at("pT_copied", i, n + 1))
                    if oh == 0 and b >= 2:
                        pe.wait_ge(s["o_normed"], at("o_normed", i, b - 1))
                    for h in range(HH):
                        c = oh * HC + h * HD
                        mm = pe.matmul(PSUM[0:QS, 4 + b % 2, c:c + HD], PT[:, n % 2, h, :], VW[:, b, c:c + HD],
                                       start=True, stop=True)
                    if oh == 1:
                        mm.then_inc(s["pv_done"], 1)

                for n in range(2 * NB + 2):
                    if n < 2 * NB:
                        scores(n)
                    if 1 <= n <= 2 * NB:
                        turn(n - 1)
                    if n >= 2:
                        values(n - 2)
                    step(side)
                pe.wait_ge(s["pT_copied"], at("pT_copied", i, 2 * NB))
                pe.wait_ge(s["o_normed"], at("o_normed", i, NB))
                pe.wait_ge(s["cls_sum"], at("cls_sum", i, 1))
                for n in range(6):
                    oh, (b0, b1) = n // 3, OSPANS[n % 3]
                    if n >= 4:
                        pe.wait_ge(s["oT_copied"], at("oT_copied", i, 4))
                    for b in range(b0, b1):
                        mm = pe.matmul(PSUM[0:HC, n % 4, (b - b0) * QB:(b - b0 + 1) * QB],
                                       OS[:, b, oh * HC:(oh + 1) * HC], EYE[0:QS, 1:QS], start=True, stop=True)
                    if n % 3 == 2:
                        mm = pe.matmul(PSUM[0:HC, n % 4, 400:401], CO[:, oh * HC:(oh + 1) * HC], EYE[0:1, 0:1],
                                       start=True, stop=True)
                    mm.then_inc(s["oT_done"], 1)
                pe.wait_ge(s["oT_copied"], at("oT_copied", i, 6))
                for tp in range(NP):
                    if tp >= 2:
                        pe.wait_ge(s["x2_ready"], at("x2_ready", i, tp - 1))
                    for t in range(2):
                        c = (2 * tp + t) * 128
                        dst = PSUM[:, 4 + tp % 2, t * C:(t + 1) * C]
                        for j in range(2):
                            pe.matmul(dst, OT[:, j, c:c + 128], WO[:, j, :], start=(j == 0), stop=False)
                        mm = pe.matmul(dst, ONES3[:], ROWS3[:, C:2 * C], start=False, stop=True)
                    mm.then_inc(s["wo_done"], 1)
                pe.wait_ge(s["xn2_ready"], at("xn2_ready", i, 1))
                for a in range(2):
                    for t in range(NT):
                        mm = pe.transpose(PSUM[:, 2 * a + t // 4, (t % 4) * 128:(t % 4 + 1) * 128],
                                          XN[:, t, 128 * a:128 * (a + 1)], EYE[:])
                mm.then_inc(s["xn2T_done"], 1)
                pe.wait_ge(s["xl_ready"], at("xl_ready", i, 2))
                for t in range(NT):
                    tok = slice(t * 128, t * 128 + 128)
                    dst = PSUM[:, 4, t * E:(t + 1) * E]
                    pe.matmul(dst, XH[:, 0, tok], GWAH[:], start=True, stop=False)
                    pe.matmul(dst, XH[:, 0, tok], GWAL[:], start=False, stop=False)
                    pe.matmul(dst, XL[:, 0, tok], GWAH[:], start=False, stop=False)
                    pe.matmul(dst, XH[:, 1, tok], GWB[:], start=False, stop=False)
                    mm = pe.matmul(dst, XL[:, 1, tok], GWB[:], start=False, stop=True)
                mm.then_inc(s["route_done"], 1)
                pe.wait_ge(s["route_shift"], at("route_shift", i, 1))

            def experts(i, side):
                def ffn1(n):
                    half, ek = divmod(n, E * HK)
                    tok = slice(half * NH, (half + 1) * NH)
                    w = slice(ek * 128, (ek + 1) * 128)
                    if n >= 2:
                        pe.wait_ge(s["gelu_done"], at("gelu_done", i, n - 1))
                    dst = bank(4 + n % 2)
                    pe.matmul(dst, W1AH[:, w], XH[:, 0, tok], start=True, stop=False)
                    pe.matmul(dst, W1AH[:, w], XL[:, 0, tok], start=False, stop=False)
                    pe.matmul(dst, W1AL[:, w], XH[:, 0, tok], start=False, stop=False)
                    pe.matmul(dst, W1B[:, w], XH[:, 1, tok], start=False, stop=False)
                    pe.matmul(dst, W1B[:, w], XL[:, 1, tok], start=False, stop=True).then_inc(s["ffn1_done"], 1)

                def ffn2(n):
                    g, k = divmod(n, HK)
                    e = g % E
                    if k == 0 and g:
                        pe.wait_ge(s["ffn_added"], at("ffn_added", i, g))
                    pe.wait_ge(s["hh_ready"], at("hh_ready", i, n + 1))
                    pe.wait_ge(s["hl_ready"], at("hl_ready", i, n + 1))
                    for q in range(4):
                        dst = PSUM[:, 6 + q // 2, (q % 2) * C:(q % 2 + 1) * C]
                        tok = slice(q * 128, (q + 1) * 128)
                        if k == 0:
                            pe.matmul(dst, ONES3[:], ROWS3[:, (2 + e) * C:(3 + e) * C], start=(q % 2 == 0), stop=False,
                                      skip_group_check=True)
                        pe.matmul(dst, HHI[:, n % 2, tok], W2H[:, e * HK + k, :], start=False, stop=False,
                                  skip_group_check=True)
                        pe.matmul(dst, HHI[:, n % 2, tok], W2L[:, e * HK + k, :], start=False, stop=False,
                                  skip_group_check=True)
                        mm = pe.matmul(dst, HLO[:, n % 2, tok], W2H[:, e * HK + k, :], start=False,
                                       stop=(k == HK - 1), skip_group_check=True)
                    mm.then_inc(s["ffn2_chunk"], 1)

                for n in range(NCHUNK + 1):
                    if n < NCHUNK:
                        ffn1(n)
                    step(side)
                    if n >= 1:
                        ffn2(n - 1)
                pe.wait_ge(s["gelu_done"], at("gelu_done", i, NCHUNK))
                pe.wait_ge(s["ffn_added"], at("ffn_added", i, NHALF * E))

            for _ in conv_first(0):
                pass
            for _ in conv_second(0):
                pass
            with pe.Fori(0, B - 1) as i:
                attention(i, conv_first(i + 1))
                side = conv_second(i + 1)
                step(side)
                experts(i, side)
            attention(B - 1, iter(()))
            experts(B - 1, iter(()))


def kernel(**inputs):
    import numpy as np
    import concourse.bacc as bacc
    from concourse.bass_utils import run_bass_kernel_spmd as run

    a = {k: np.asarray(v) for k, v in inputs.items()}
    r = {k[len("L0_conv_row_"):]: v for k, v in a.items() if k.startswith("L0_conv_row_")}
    c = {k[len("L0_conv_col_"):]: v for k, v in a.items() if k.startswith("L0_conv_col_")}
    f = np.float32

    def halves(w):
        return np.ascontiguousarray(w.reshape(2, HC, -1).transpose(1, 0, 2))

    def vec(v):
        return np.ascontiguousarray(v.reshape(2, HC).T)

    proj = np.zeros((97, 2, 128), f)
    for k, (w, bb) in enumerate(((r["Win"], r["bin"]), (c["Win"], c["bin"]), (r["Wg"], r["bg"]), (c["Wg"], c["bg"]))):
        proj[0:HC, :, 32 * k:32 * k + S] = halves(w.T)
        proj[96, 0, 32 * k:32 * k + S] = bb
    ya, yb = np.zeros((113, 2, C), f), np.zeros((113, 2, C), f)
    ya[0:HC], yb[0:HC] = halves(r["Wskip"].T), halves(c["Wskip"].T)
    ya[96, 0], yb[96, 0] = r["bout"], r["bskip"]
    ya[96, 1], yb[96, 1] = c["bout"], c["bskip"]
    ya[97:, 0], ya[97:, 1] = r["Wout"].T, c["Wout"].T
    yscale = np.full((113, 1), 0.5, f)
    yscale[97:] = 0.125
    sv, su, sa = np.zeros((S, 2 * S), f), np.zeros((S, 2 * S), f), np.zeros((2 * S, 1), f)
    R = r["U"].shape[1]
    for k, p in enumerate((r, c)):
        sv[k * R:(k + 1) * R, k * S:(k + 1) * S] = p["V"].T
        su[k * R:(k + 1) * R, k * S:(k + 1) * S] = p["U"].T
        sa[k * S:(k + 1) * S, 0] = p["a_logit"]
    g2 = np.zeros((4, 32, 4, C), f)
    for k in range(4):
        g2[k, :, k] = a["L0_conv_g2_w"].T
    g2 = g2.reshape(128, 4, C)
    gavg = np.kron(np.eye(HC // GROUP), np.full((GROUP, GROUP), 1.0 / GROUP)).astype(f)
    mask = np.full((QS, 3, HH, KS), NEG, f)
    for v, b in enumerate((0, 1, NB - 1)):
        for q in range(1, QS):
            for k in range(q - 1, q + 2 * PAD):
                if 1 <= b * QB + 1 - PAD + k < T:
                    mask[q, v, :, k] = 0.0
            mask[q, v, :, KW] = 0.0
        mask[0, v, :, PAD:PAD + QB] = 0.0
    mask[0, 0, :, KW] = 0.0
    w1, w2 = a["L1_ffn_w1"], a["L1_ffn_w2"]
    w1t = w1.transpose(1, 0, 2).reshape(C, E * HID)
    ins = dict(
        x=np.ascontiguousarray(a["x"].reshape(B, 2, HC, T).transpose(0, 2, 1, 3)),
        proj_w=proj, y_wa=ya, y_wb=yb, y_scale=yscale, eye=np.eye(128, dtype=f), gavg=gavg,
        cavg=np.full((HC, HC), 1.0 / C, f), norm_w=vec(a["L0_conv_norm_w"]), norm_b=vec(a["L0_conv_norm_b"]),
        g1_wT=halves(a["L0_conv_g1_w"].T), g1_b=a["L0_conv_g1_b"].reshape(1, -1),
        g2_wT=g2,
        bias_row=np.concatenate([a["L0_conv_g2_b"], a["L1_attn_bo"], a["L1_ffn_b2"].reshape(-1)]).reshape(1, -1),
        scan_v=sv, scan_u=su, scan_a=sa,
        wq=halves(a["L1_attn_Wq"]), wk=halves(a["L1_attn_Wk"]), wv=halves(a["L1_attn_Wv"]), wo=halves(a["L1_attn_Wo"]),
        bq=vec(a["L1_attn_bq"]), bk=vec(a["L1_attn_bk"]), bv=vec(a["L1_attn_bv"]),
        mask=mask.reshape(QS, -1),
        w1a=np.ascontiguousarray(w1t[0:128]), w1b=np.ascontiguousarray(np.tile(w1t[128:], (2, 1))),
        w2=np.ascontiguousarray(w2.reshape(E, HK, 128, C).transpose(2, 0, 1, 3)).reshape(128, -1),
        b1=np.ascontiguousarray(a["L1_ffn_b1"].reshape(E * HK, 128).T),
        gate_wa=np.ascontiguousarray(a["L1_ffn_gate_w"][0:128]),
        gate_wb=np.ascontiguousarray(np.tile(a["L1_ffn_gate_w"][128:], (2, 1))),
        gate_b=np.ascontiguousarray(np.tile(a["L1_ffn_gate_b"][None], (128, 1))),
        before=np.ascontiguousarray(np.broadcast_to(np.tril(np.ones((E, E), f), -1), (128, E, E))),
        after=np.ascontiguousarray(np.broadcast_to(np.triu(np.ones((E, E), f), 1), (128, E, E))),
    )
    nc = bacc.Bacc("TRN2", target_bir_lowering=False, num_devices=1)
    aps = {k: nc.dram_tensor("in_" + k, v.shape, mybir.dt.from_np(v.dtype), kind="ExternalInput").ap()
           for k, v in ins.items()}
    out = nc.dram_tensor("out_dram", (B, 128, NT, C), F32, kind="ExternalOutput").ap()
    powers = nc.dram_tensor("powers", (2 * S, 63, 2 * S), F32, kind="Internal").ap()
    hybrid_kernel(nc, **aps, out=out, powers=powers)
    res = run(nc, [{"in_" + k: v for k, v in ins.items()}], core_ids=[0])
    got = res.results[0]["out_dram"]
    return np.ascontiguousarray(got.transpose(0, 3, 2, 1)).reshape(B, C, GH, GW)
```

```python
from contextlib import ExitStack

import concourse.bass as bass
from concourse import mybir

F32 = mybir.dt.float32
F16 = mybir.dt.float16
BF16 = mybir.dt.bfloat16
ALU = mybir.AluOpType
ACT = mybir.ActivationFunctionType
AX = mybir.AxisListType

B, C, GH, GW = 16, 192, 32, 32
T = GH * GW
NT = T // 128
NP = NT // 2
HC = C // 2
S = 16
KP, KC = 128 // S, GW // (128 // S)
HEADS, HD = 6, 32
HH = HEADS // 2
PAD = 16
QB = 93
NB = (T - 1) // QB
KW = QB + 2 * PAD
KS = KW + 1
QS = QB + 1
E, HID = 4, 768
HK = HID // 128
NH = 512
NHALF = T // NH
GROUP = C // 32
NCHUNK = NHALF * E * HK

LINKS_FIRST, LINKS = 78, 61

X_UP, W_UP, H_UP = 1024.0, 64.0, 8.0
NEG = -1e30

PER = dict(
    x_loaded=16, gn_channel=1, gn_mean=1, gn_spread=1, gn_var=1, gn_eps=1, gn_rstd=1, xg_ready=2, xs_ready=2,
    proj_done=1, tanh_done=1, gu_ready=2, gu_moved=16 * 2 * KP, scan_done=1, hs_copied=1, hs_rows_moved=16 * KP,
    hs_cols_moved=16 * KP, hs_permuted=1, hs_placed=16, xgT_done=NP, h1_read=NP, mixln_eps=1, mixln_rstd=1, h1_pre=1,
    h1_gelu=1, h1T_done=1, h1T_copied=1, mix_done=NP, mix_tanh=NP, mixed=NP,
    ln1_eps=1, ln1_rstd=1, ln1_mean=1, ln1_shift=1, xn1_ready=2, xn1T_done=1,
    win_act=1, win_dve=1, piece_done=18, piece_act=9, piece_dve=9,
    score_done=2 * NB, max_done=2 * NB, exp_done=2 * NB, pT_done=2 * NB, pT_copied=2 * NB, pv_done=NB,
    o_normed=NB, cls_weight=1, cls_exp=1, cls_coef=1, cls_spread=1, cls_ready=1, oT_done=6, oT_copied=6,
    wo_done=NP, x2_ready=NP, ln2_eps=2, ln2_rstd=2, xn2_ready=2, xn2_doubled=2, xn2T_done=4, xh_ready=4, xl_ready=4,
    route_done=2, route_shift=2, route_exp=2, gates_ready=2,
    ffn1_done=NCHUNK, gelu_done=NCHUNK, hh_ready=NCHUNK, hl_ready=NCHUNK, ffn2_chunk=NCHUNK,
    ffn_added=NHALF * E, x2a_free=16, x2b_free=16,
)


def window_view(t, offset, dims):
    base = t[:]
    return bass.AP(tensor=base.tensor, offset=base.offset + offset, ap=[[base.ap[0][0], dims[0]]] + dims[1:])


def hybrid_kernel(nc, x, proj_w, y_wa, y_wb, y_scale, eye, gavg, cavg, norm_w, norm_b, g1_wT, g1_b, g2_wT, bias_row,
                  scan_v, scan_u, scan_a, wq, wk, wv, wo, bq, bk, bv, mask, w1a, w1b, w2, b1, gate_wa, gate_wb,
                  gate_b, before, after, out, powers):
    ctx = ExitStack()
    with ctx:
        def sb(name, shape, dt=F32):
            return ctx.enter_context(nc.sbuf_tensor(name, shape, dt))

        def sem(name):
            return ctx.enter_context(nc.semaphore(name))

        EYE = sb("EYE", [128, 128])
        EYEB = sb("EYEB", [QS, QS], BF16)
        GAVG = sb("GAVG", [HC, HC])
        MASKB = sb("MASKB", [QS, 3, HH * KS], BF16)
        PROJ = sb("PROJ", [97, 2, 128])
        WY = sb("WY", [113, 2, C])
        WG1 = sb("WG1", [HC, 2, 32])
        BG1 = sb("BG1", [128, 32])
        WG2 = sb("WG2", [128, 4, C])
        SCAN = sb("SCAN", [128, 2, 2 * KC - 1, 128])
        WQ, WK, WV, WO = (sb(n, [HC, 2, C]) for n in ("WQ", "WK", "WV", "WO"))
        BQ, BQS, BK, BV = (sb(n, [HC, 2]) for n in ("BQ", "BQS", "BK", "BV"))
        ONES3 = sb("ONES3", [3, 128], BF16)
        ROWS3 = sb("ROWS3", [3, 6 * C], BF16)
        W1AH = sb("W1AH", [128, E * HID], F16)
        W1AL = sb("W1AL", [128, E * HID], F16)
        W1B = sb("W1B", [128, E * HID], F16)
        W2H = sb("W2H", [128, E * HK, C], F16)
        W2L = sb("W2L", [128, E * HK, C], F16)
        B1 = sb("B1", [128, E * HK])
        GWAH, GWAL, GWB = (sb(n, [128, E], F16) for n in ("GWAH", "GWAL", "GWB"))
        GB = sb("GB", [128, E])
        BEFORE, AFTER = sb("BEFORE", [128, E, E]), sb("AFTER", [128, E, E])
        MHALF = sb("MHALF", [128, 8])
        ONE32 = sb("ONE32", [1, HD])
        SPARES = sb("SPARES", [1, 2])
        SPARE, PSPARE = SPARES[:, 0:1], SPARES[:, 1:2]

        XR = sb("XR", [HC, 2, T])
        XG = sb("XG", [113, 2, T])
        XS = sb("XS", [HC, 2, T])
        GST = sb("GST", [HC, 2, 2, 6])
        MV = sb("MV", [HC, 2, 2])
        GM, GD, GV, GR, GR1, GNB = (sb(n, [HC, 2]) for n in ("GM", "GD", "GV", "GR", "GR1", "GNB"))
        TGU = sb("TGU", [128, T])
        TG, GU = TGU[64:128, :], TGU[0:64, :]
        HST = TGU[0:S, :].rearrange("s (w h) -> s w h", w=GW)
        GUP = sb("GUP", [128, 2, KC, GW])
        HSP = sb("HSP", [128, 2, KC, GW])
        TST = sb("TST", [128, NT, 6])
        TMV = sb("TMV", [128, NT, 2])
        TV, TR, NMR = sb("TV", [128, NT]), sb("TR", [128, NT]), sb("NMR", [128, NT])
        GTST, GTMV = sb("GTST", [128, NT, 6]), sb("GTMV", [128, NT, 2])
        GTV, GTR = sb("GTV", [128, NT]), sb("GTR", [128, NT])
        H1 = sb("H1", [128, NT, 32])
        H1T = sb("H1T", [128, 2, 128])
        TM = sb("TM", [128, 2 * C])
        EM = sb("EM", [128, 2 * C])
        X1 = sb("X1", [128, NT, C])
        XN = sb("XN", [128, NT, 256])
        X2 = sb("X2", [128, NT, C])
        HST2 = XN[0:S].rearrange("s a b -> s (a b)")[:, 0:T]
        XW = sb("XW", [HC, 2, NB, KS])
        QT = sb("QT", [HC, 2, NB, QS])
        KBD = sb("KBD", [HC, 2, NB, HH, KS])
        VW = sb("VW", [KS, NB, C])
        NMX = sb("NMX", [QS, NB, 2, HH])
        DEN = sb("DEN", [QS, NB, 2, HH])
        RDEN = sb("RDEN", [QS, NB, 2, HH])
        PS = sb("PS", [QS, 2, HH, KS])
        PT = sb("PT", [KS, 2, HH, QS])
        OS = XW[0:QS].rearrange("p a b k -> p (a b k)")[:, 0:NB * C].rearrange("p (b c) -> p b c", b=NB)
        OT = QT[:].rearrange("p a b q -> p (a b q)")[:, 0:2 * T].rearrange("p (a t) -> p a t", a=2)
        CM = sb("CM", [1, HEADS])
        CW = sb("CW", [1, NB, HEADS])
        CSUM = sb("CSUM", [1, HEADS])
        OC, OC1 = sb("OC", [HC, 2, NB]), sb("OC1", [HC, 2])
        XH = sb("XH", [128, 2, T], F16)
        XL = sb("XL", [128, 2, T], F16)
        SC = sb("SC", [128, NT, E])
        SE = sb("SE", [128, NT, E])
        SM = sb("SM", [128, NT])
        CMPA, CMPB = sb("CMPA", [128, NT // 2, E, E]), sb("CMPB", [128, NT // 2, E, E])
        WIN = sb("WIN", [128, NT, E])
        GATE = sb("GATE", [128, NT, E])
        HF = sb("HF", [128, 2, NH])
        HHI = sb("HHI", [128, 2, NH], F16)
        HLO = sb("HLO", [128, 2, NH], F16)

        PSUM = ctx.enter_context(nc.psum_tensor("PSUM", [128, 8, 512], F32))

        with ExitStack() as setup:
            def ssem(name):
                return setup.enter_context(nc.semaphore(name))

            loaded, dve_step, act_step, pe_step = ssem("loaded"), ssem("dve_step"), ssem("act_step"), ssem("pe_step")
            powers_stored, scan_loaded, rows_split, rows_moved = (
                ssem(n) for n in ("powers_stored", "scan_loaded", "rows_split", "rows_moved"))
            Y_A, Y_B = XN[0:113, 0:2, 0:C], XN[0:113, 2:4, 0:C]
            YSC = SM[0:113, 0:1]
            NW, NBI, CAVG = GM[:], GD[:], XN[0:HC, 4, 0:HC]
            G1W = X1[0:HC, 0, 0:64].rearrange("p (j o) -> p j o", j=2)
            G1N = X1[0:HC, 1, 0:64].rearrange("p (j o) -> p j o", j=2)
            NBB = X1[0:HC, 2:4, 0:128]
            G1B = XN[0:1, 5, 0:32]
            ONE1 = XN[0:1, 5, 32:160]
            PW = OS[0:2 * S, :, :].rearrange("p a b -> p (a b)")[:, 0:32 * 32].rearrange("p (k s) -> p k s", k=32)
            MIR = XG[0:2 * S, :, :].rearrange("p a b -> p (a b)")[:, 0:63 * 32].rearrange("p (k s) -> p k s", k=63)
            SV = GUP[0:S, 0, 0, 0:2 * S]
            SU = GUP[0:S, 0, 1, 0:2 * S]
            SA = GUP[0:2 * S, 0, 2, 0:1]
            SIG = GUP[0:2 * S, 0, 2, 1:2]
            DIA = GUP[0:2 * S, 0, 3, 0:2 * S]
            AT = GUP[0:2 * S, 1, 0, 0:2 * S]
            ROW = XR[0:1, 0:2, :].rearrange("p a b -> p (a b)")[:, 0:6 * C]
            ROWR = XS[0:1, 0:2, :].rearrange("p a b -> p (a b)")[:, 0:6 * C]
            ROWP = QT[0:1, :, :, :].rearrange("p a b c -> p (a b c)")[:, 0:9 * C].bitcast(BF16)
            with nc.Block() as block:
                small = [
                    (EYE[:], eye), (GAVG[:], gavg), (PROJ[:], proj_w), (WG2[:], g2_wT),
                    (WQ[:], wq), (WK[:], wk), (WV[:], wv), (WO[:], wo), (BQ[:], bq), (BK[:], bk), (BV[:], bv),
                    (B1[:], b1), (GB[:], gate_b), (BEFORE[:], before), (AFTER[:], after),
                    (Y_A, y_wa), (Y_B, y_wb), (YSC, y_scale), (CAVG, cavg), (NW, norm_w), (NBI, norm_b),
                    (G1W, g1_wT), (G1B, g1_b), (SV, scan_v), (SU, scan_u), (SA, scan_a), (ROW, bias_row),
                    (VW[0:QS, 0:6, :].rearrange("p a b -> p (a b)")[:, 0:3 * HH * KS], mask),
                    (HF[:, 0, 0:E], gate_wa), (HF[:, 0, 4:4 + E], gate_wb),
                ]

                @block.sync
                def _(sp):
                    for dst, src in small:
                        sp.dma_start(dst, src).then_inc(loaded, 16)
                    sp.wait_ge(rows_split, 1)
                    sp.dma_start(ROWS3[:], ROWP.rearrange("p (k n) -> p k n", k=3)).then_inc(rows_moved, 16)
                    sp.wait_ge(powers_stored, 1)
                    sp.dma_start(powers, MIR).then_inc(scan_loaded, 16)
                    sp.wait_ge(scan_loaded, 16)
                    for kind in range(2):
                        for i in range(KP):
                            first = kind * S * 63 * 32 + kind * S + (31 - 24 - i) * 32
                            src = bass.AP(tensor=powers.tensor, offset=powers.offset + first,
                                          ap=[[63 * 32, S], [32, (2 * KC - 1) * KP], [1, S]])
                            sp.dma_start(SCAN[S * i:S * i + S, kind, :, :].rearrange("p d (k s) -> p (d k) s", k=KP),
                                         src).then_inc(scan_loaded, 16)
                    sp.wait_ge(scan_loaded, 16 * (1 + 2 * KP))
                    sp.wait_ge(rows_moved, 16)

                n_dve = [0]
                marks = {}

                @block.vector
                def _(dve):
                    def link(ins):
                        n_dve[0] += 1
                        ins.then_inc(dve_step, 1)
                        dve.wait_ge(dve_step, n_dve[0])

                    for t in (XW, KBD, XG):
                        dve.memset(t[:], 0.0)
                    dve.memset(ONES3[:], 1.0)
                    dve.memset(SPARES[:], 0.0)
                    dve.memset(ONE32[:], 1.0)
                    dve.memset(ONE1, 1.0)
                    link(dve.memset(MHALF[:], -0.5))
                    link(dve.memset(XG[96:97, :, :], 1.0))
                    dve.wait_ge(loaded, 16 * len(small))
                    dve.tensor_copy(EYEB[:], EYE[0:QS, 0:QS])
                    dve.tensor_copy(MASKB[:].rearrange("p a b -> p (a b)"),
                                    VW[0:QS, 0:6, :].rearrange("p a b -> p (a b)")[:, 0:3 * HH * KS])
                    dve.tensor_scalar(BQS[:], BQ[:], HD ** -0.5, None, ALU.mult)
                    link(dve.tensor_tensor(Y_A, Y_A, Y_B, ALU.add))
                    link(dve.tensor_scalar(WY[:], Y_A, YSC, None, ALU.mult))
                    for j in range(2):
                        link(dve.tensor_tensor(WY[0:HC, j, j * HC:(j + 1) * HC], WY[0:HC, j, j * HC:(j + 1) * HC],
                                               EYE[0:HC, 0:HC], ALU.subtract))
                    for j in range(2):
                        link(dve.tensor_scalar(G1N[:, j, :], G1W[:, j, :], NW[:, j:j + 1], None, ALU.mult))
                        link(dve.tensor_scalar(NBB[:, j, :], XG[0:HC, 0, 0:128], NBI[:, j:j + 1], None, ALU.add))
                    marks["g1"] = n_dve[0]
                    dve.wait_ge(pe_step, 2)
                    link(dve.tensor_copy(BG1[:], PSUM[:, 1, 0:32]))
                    for j in range(2):
                        link(dve.tensor_tensor(WG1[:, j, :], G1N[:, j, :], PSUM[0:HC, 0, 0:32], ALU.subtract))
                    link(dve.tensor_scalar(ROW[:, 2 * C:], ROW[:, 2 * C:], W_UP * H_UP, None, ALU.mult))
                    n = 6 * C
                    link(dve.tensor_copy(ROWP[:, 0:n], ROW))
                    link(dve.tensor_tensor(ROWR, ROW, ROWP[:, 0:n], ALU.subtract))
                    link(dve.tensor_copy(ROWP[:, n:2 * n], ROWR))
                    link(dve.tensor_tensor(ROWR, ROWR, ROWP[:, n:2 * n], ALU.subtract))
                    dve.tensor_copy(ROWP[:, 2 * n:3 * n], ROWR).then_inc(rows_split, 1)
                    dve.wait_ge(act_step, 1)
                    link(dve.tensor_scalar(SIG, SIG, 0.5, 0.5, ALU.mult, ALU.add))
                    link(dve.tensor_scalar(DIA, EYE[0:2 * S, 0:2 * S], SIG, None, ALU.mult))
                    link(dve.tensor_copy(PW[:, 0, :], EYE[0:2 * S, 0:2 * S]))
                    dve.wait_ge(pe_step, 3)
                    link(dve.tensor_tensor(PW[:, 1, :], DIA, PSUM[0:2 * S, 2, 0:2 * S], ALU.add))
                    marks["power"] = n_dve[0]
                    m, seen = 1, 3
                    while m < 32:
                        seen += 1
                        dve.wait_ge(pe_step, seen)
                        link(dve.tensor_copy(AT, PSUM[0:2 * S, 3, 0:2 * S]))
                        k = min(m, 31 - m)
                        if k:
                            seen += 1
                            dve.wait_ge(pe_step, seen)
                            link(dve.tensor_copy(PW[:, m + 1:m + 1 + k, :],
                                                 PSUM[0:2 * S, 4, 0:32 * k].rearrange("p (k s) -> p k s", k=k)))
                        m *= 2
                    link(dve.tensor_copy(MIR[:, 31:63, :], PW))
                    for k in range(1, 32):
                        dve.tensor_copy(MIR[:, 31 - k, :], PW[:, k, :])
                    link(dve.tensor_scalar(MIR[:, 31, :], PW[:, 0, :], 2.0, None, ALU.mult))
                    dve.memset(SPARE, 0.0).then_inc(powers_stored, 1)
                    link(dve.tensor_scalar(GWAH[:], HF[:, 0, 0:E], W_UP, None, ALU.mult))
                    link(dve.scalar_tensor_tensor(GWAL[:], HF[:, 0, 0:E], W_UP, GWAH[:], ALU.mult, ALU.subtract))
                    link(dve.tensor_scalar(GWB[:], HF[:, 0, 4:8], W_UP, None, ALU.mult))
                    link(dve.scalar_tensor_tensor(GWB[64:128], HF[64:128, 0, 4:8], W_UP, GWB[64:128], ALU.mult,
                                                  ALU.subtract))

                @block.scalar
                def _(act):
                    act.wait_ge(loaded, 16 * len(small))
                    act.activation(SIG, SA, ACT.Tanh, scale=0.5).then_inc(act_step, 1)

                @block.tensor
                def _(pe):
                    pe.wait_ge(loaded, 16 * len(small))
                    pe.wait_ge(dve_step, marks["g1"])
                    for j in range(2):
                        mm = pe.matmul(PSUM[0:HC, 0, 0:32], CAVG, G1N[:, j, :], start=(j == 0), stop=(j == 1))
                    mm.then_inc(pe_step, 1)
                    pe.matmul(PSUM[:, 1, 0:32], ONE1, G1B, start=True, stop=False)
                    for j in range(2):
                        mm = pe.matmul(PSUM[:, 1, 0:32], NBB[:, j, :], G1W[:, j, :], start=False, stop=(j == 1))
                    mm.then_inc(pe_step, 1)
                    pe.matmul(PSUM[0:2 * S, 2, 0:2 * S], SV, SU, start=True, stop=True).then_inc(pe_step, 1)
                    m = 1
                    steps = marks["power"]
                    pe.wait_ge(dve_step, steps)
                    while m < 32:
                        pe.transpose(PSUM[0:2 * S, 3, 0:2 * S], PW[:, m, :], EYE[0:2 * S, 0:2 * S]).then_inc(pe_step, 1)
                        steps += 1
                        pe.wait_ge(dve_step, steps)
                        k = min(m, 31 - m)
                        if k:
                            pe.matmul(PSUM[0:2 * S, 4, 0:32 * k], AT, PW[:, 1:1 + k, :], start=True, stop=True
                                      ).then_inc(pe_step, 1)
                            steps += 1
                            pe.wait_ge(dve_step, steps)
                        m *= 2

        s = {n: sem("i_" + n) for n in PER}
        dve_link = sem("dve_link")

        def at(name, i, k):
            return i * PER[name] + k

        def first(i):
            return isinstance(i, int) and i == 0

        def last(i):
            return isinstance(i, int) and i == B - 1

        def bank(n):
            return PSUM[:, n, :]

        def empty(n):
            for _ in range(n):
                yield

        def step(works, times=1):
            for _ in range(times):
                for work in works:
                    next(work, None)

        STEPS_AHEAD = 2
        STEPS = [(1, n % 2) if n < 17 else (2, 1) for n in range(NCHUNK // 2)] + [(1, 1)]

        def windows(copy, j, part, give):
            if part == 0:
                copy(XW[:, j, 1:NB - 1, 0:KW],
                     window_view(PSUM, j * T + QB - PAD + 1, [HC, [QB, NB - 2], [1, KW]]))
                return
            copy(XW[:, j, 0, PAD - 1:KW], window_view(PSUM, j * T, [HC, [1, KW - PAD + 1]]))
            last = (NB - 1) * QB - PAD + 1
            copy(XW[:, j, NB - 1, 0:T - last], window_view(PSUM, j * T + last, [HC, [1, T - last]]))
            copy(XW[:, j, :, KW], window_view(PSUM, j * T, [HC, [0, NB]])).then_inc(give, 1)

        SPANS = [(0, 4), (4, 8), (8, NB)]
        PIECES = 18
        act_engine = nc.scalar

        def evacuate_piece(eng, n, give):
            src = bank(n % 4)
            is_act = eng is act_engine
            if n < 6:
                oh, (b0, b1) = n // 3, SPANS[n % 3]
                k = b1 - b0
                parts = [(QT[:, oh, b0:b1, 1:QS], src[0:HC, 0:k * QB].rearrange("p (b q) -> p b q", b=k))]
                if n % 3 == 2:
                    col = src[0:HC, 400:401].broadcast_to((HC, NB))
                    parts.append((QT[:, oh, :, 0], col))
                for dst, ps in parts:
                    if is_act:
                        last = eng.activation(dst, ps, ACT.Identity, bias=BQS[:, oh:oh + 1], scale=HD ** -0.5)
                    else:
                        last = eng.tensor_scalar(dst, ps, BQ[:, oh:oh + 1], HD ** -0.5, ALU.add, ALU.mult)
            elif n < 12:
                oh, (b0, b1) = (n - 6) // 3, SPANS[n % 3]
                k = b1 - b0
                for h in range(HH):
                    p = slice(h * HD, (h + 1) * HD)
                    dst = KBD[p, oh, b0:b1, h, :]
                    ps = src[p, 0:k * KS].rearrange("p (b q) -> p b q", b=k)
                    if is_act:
                        last = eng.activation(dst, ps, ACT.Identity, bias=BK[p, oh:oh + 1])
                    else:
                        last = eng.tensor_scalar(dst, ps, BK[p, oh:oh + 1], None, ALU.add)
            else:
                b0 = 2 * (n - 12)
                k = min(2, NB - b0)
                dst = VW[:, b0:b0 + k, :]
                ps = src[0:KS, 0:k * C].rearrange("p (b q) -> p b q", b=k)
                last = eng.copy(dst, ps) if is_act else eng.tensor_copy(dst, ps)
            last.then_inc(give, 1)

        O_COL = HH * QS
        X2_FREE = ["x2a_free", "x2b_free"]
        WO_BANK = [3, 2, 4, 5]

        OSPANS = [(5, 8), (8, NB)]

        def oT_piece(n):
            return (n // 2, OSPANS[n % 2], n) if n < 4 else (n - 4, (0, OSPANS[0][0]), n - 4)

        def evacuate_oT(eng, n, i):
            oh, (b0, b1), at_bank = oT_piece(n)
            eng.wait_ge(s["oT_done"], at("oT_done", i, n + 1))
            src = bank(at_bank)[0:HC, 0:(b1 - b0) * QS].rearrange("p (b q) -> p b q", q=QS)
            dst = OT[:, oh, 1 + b0 * QB:1 + b1 * QB].rearrange("p (b q) -> p b q", q=QB)
            if eng is act_engine:
                eng.activation(dst, src[:, :, 1:QS], ACT.Identity, bias=BV[:, oh:oh + 1])
                last = eng.copy(OC[:, oh, b0:b1], src[:, :, 0])
            else:
                eng.tensor_scalar(dst, src[:, :, 1:QS], BV[:, oh:oh + 1], None, ALU.add)
                last = eng.tensor_copy(OC[:, oh, b0:b1], src[:, :, 0])
            last.then_inc(s["oT_copied"], 1)

        PIECE = 768
        WEIGHTS = [(w, kind, n) for w, kind in ((w1a, "a"), (w1b, "b"), (w2, "2")) for n in range(w.shape[1] // PIECE)]
        STAGE = [HF[:].rearrange("p a b -> p (a b)")[:, 0:PIECE], X2[:].rearrange("p a b -> p (a b)")[:, 0:PIECE]]
        weights_loaded, weights_split = [sem("weights_loaded0"), sem("weights_loaded1")], sem("weights_split")

        block = ctx.enter_context(nc.Block())

        @block.sync
        def _(sp):
            with sp.Fori(0, B) as i:
                for kind in range(2):
                    sp.wait_ge(s["gu_ready"], at("gu_ready", i, kind + 1))
                    src = GU[32 * kind:32 * kind + S, :].rearrange("s (c i n) -> s c i n", c=KC, i=KP)
                    for k in range(KP):
                        sp.dma_start(GUP[S * k:S * k + S, kind, :, :], src[:, :, k, :]).then_inc(s["gu_moved"], 16)
                sp.wait_ge(s["hs_copied"], at("hs_copied", i, 1))
                for kind, moved in ((0, s["hs_rows_moved"]), (1, s["hs_cols_moved"])):
                    dst = (HST.rearrange("s (c i) n -> s c i n", i=KP) if kind == 0 else
                           XG[97:113, 1, :].rearrange("s (c i n) -> s c i n", c=KC, i=KP))
                    for k in range(KP):
                        sp.dma_start(dst[:, :, k, :], HSP[S * k:S * k + S, kind, :, :]).then_inc(moved, 16)
                sp.wait_ge(s["hs_permuted"], at("hs_permuted", i, 1))
                sp.dma_start(XG[97:113, 0, :], HST2).then_inc(s["hs_placed"], 16)

        @block.gpsimd
        def _(pool):
            def rstd(i, dst, src, width, wait, give, k=1):
                pool.wait_ge(s[wait], at(wait, i, k))
                pool.tensor_tensor(dst, src, MHALF[0:dst.shape[0], 0:width], ALU.pow).then_inc(s[give], 1)

            def token_rstd(i, half):
                tiles = slice(4 * half, 4 * half + 4)
                rstd(i, TR[:, tiles], TV[:, tiles], 4, "ln2_eps", "ln2_rstd", 2 - half)

            def conv(i):
                rstd(i, GTR[:], GTV[:], NT, "mixln_eps", "mixln_rstd")
                pool.wait_ge(s["hs_rows_moved"], at("hs_rows_moved", i, 16 * KP))
                if not first(i):
                    pool.wait_ge(s["xn2T_done"], at("xn2T_done", i, 0))
                pool.tensor_tensor(PSPARE, PSPARE, PSPARE, ALU.mult)
                pool.tensor_copy(HST2.rearrange("s (h w) -> s h w", h=GH), HST.rearrange("s w h -> s h w")
                                 ).then_inc(s["hs_permuted"], 1)
                rstd(i, TR[:], TV[:], NT, "ln1_eps", "ln1_rstd")
                pool.wait_ge(s["ln1_rstd"], at("ln1_rstd", i, 1))
                pool.wait_ge(s["ln1_mean"], at("ln1_mean", i, 1))
                pool.tensor_tensor(NMR[:], NMR[:], TR[:], ALU.mult).then_inc(s["ln1_shift"], 1)

            def image(i, following=True):
                if following:
                    rstd(i + 1, GR[:], GV[:], 2, "gn_eps", "gn_rstd")
                token_rstd(i, 1)
                token_rstd(i, 0)
                if following:
                    conv(i + 1)

            rstd(0, GR[:], GV[:], 2, "gn_eps", "gn_rstd")
            conv(0)
            image(0)
            with pool.Fori(1, B - 1) as i:
                image(i)
            image(B - 1, following=False)

        @block.scalar
        def _(act):
            def load(i):
                if not first(i):
                    act.wait_ge(s["xs_ready"], at("xs_ready", i, 0))
                act.dma_start(XR[:], x[bass.ds(i, 1)].rearrange("o p j t -> (o p) j t")).then_inc(s["x_loaded"], 16)

            def states_tanh(i):
                act.wait_ge(s["proj_done"], at("proj_done", i, 1))
                act.activation(TG.rearrange("p (a b) -> p a b", a=2), PSUM[64:128, 0:2, :], ACT.Tanh, scale=0.5
                               ).then_inc(s["tanh_done"], 1)

            def conv(i):
                yield from empty(5)
                act.wait_ge(s["scan_done"], at("scan_done", i, 1))
                act.activation(HSP[:].rearrange("p a b c -> p (a b c)"), PSUM[:, 3, 0:2 * KC * GW], ACT.Copy
                               ).then_inc(s["hs_copied"], 1)
                yield
                yield from empty(2)
                act.wait_ge(s["h1_pre"], at("h1_pre", i, 1))
                act.activation(H1[:], H1[:], ACT.Gelu).then_inc(s["h1_gelu"], 1)
                yield
                act.wait_ge(s["h1T_done"], at("h1T_done", i, 1))
                act.activation(H1T[:].rearrange("p a b -> p (a b)"), PSUM[:, 3, 0:256], ACT.Copy
                               ).then_inc(s["h1T_copied"], 1)
                yield
                yield from empty(2)
                for tp in range(NP):
                    act.wait_ge(s["mix_done"], at("mix_done", i, tp + 1))
                    if tp:
                        act.wait_ge(s["mixed"], at("mixed", i, tp))
                    act.activation(TM[:], PSUM[:, 0, 0:2 * C], ACT.Tanh, scale=0.5).then_inc(s["mix_tanh"], 1)
                    yield from empty(2)
                yield from empty(2)
                act.wait_ge(s["ln1_shift"], at("ln1_shift", i, 1))
                for k in range(2):
                    for t in range(4 * k, 4 * k + 4):
                        a = act.activation(XN[:, t, 0:C], X1[:, t, :], ACT.Identity, bias=NMR[:, t:t + 1],
                                           scale=TR[:, t:t + 1])
                    a.then_inc(s["xn1_ready"], 1)
                    yield
                yield
                act.wait_ge(s["xn1T_done"], at("xn1T_done", i, 1))
                windows(act.copy, 0, 0, s["win_act"])
                yield
                windows(act.copy, 0, 1, s["win_act"])
                yield
                for n in range(PIECES):
                    if n % 2 == 0:
                        act.wait_ge(s["piece_done"], at("piece_done", i, n + 1))
                        evacuate_piece(act, n, s["piece_act"])
                    yield

            def gelu(i, n):
                act.wait_ge(s["ffn1_done"], at("ffn1_done", i, n + 1))
                if n >= 2:
                    act.wait_ge(s["hl_ready"], at("hl_ready", i, n - 1))
                ek = n % (E * HK)
                act.activation(HF[:, n % 2, :], PSUM[:, 4 + n % 2, :], ACT.Gelu, scale=1 / (X_UP * W_UP),
                               bias=B1[:, ek:ek + 1]).then_inc(s["gelu_done"], 1)

            def store(i, half):
                act.wait_ge(s["ffn_added"], at("ffn_added", i, E * (2 - half)))
                tiles = slice(NT // 2 * half, NT // 2 * (half + 1))
                act.dma_start(out[bass.ds(i, 1)].rearrange("o p t c -> (o p) t c")[:, tiles, :], X2[:, tiles, :]
                              ).then_inc(s[X2_FREE[half]], 16)

            def double(i, half):
                tiles = slice(4 * half, 4 * half + 4)
                act.wait_ge(s["xn2_ready"], at("xn2_ready", i, 2 - half))
                act.copy(XN[:, tiles, C:256], XN[:, tiles, 128:C]).then_inc(s["xn2_doubled"], 1)

            def high_parts(i, half):
                for a in range(2):
                    act.wait_ge(s["xn2T_done"], at("xn2T_done", i, 2 * (1 - half) + a + 1))
                    act.activation(XH[:, a, half * NH:(half + 1) * NH], bank(2 * half + a), ACT.Copy, scale=X_UP
                                   ).then_inc(s["xh_ready"], 1)

            def route_exp(i, half):
                act.wait_ge(s["route_shift"], at("route_shift", i, 2 - half))
                tiles = slice(4 * half, 4 * half + 4)
                act.activation(SE[:, tiles, :], SC[:, tiles, :], ACT.Exp).then_inc(s["route_exp"], 1)

            def attention(i, before, following):
                if following:
                    load(i + 1)
                if before:
                    route_exp(i - 1, 0)
                for b in range(NB + 1):
                    if b < NB:
                        for n in (2 * b, 2 * b + 1):
                            act.wait_ge(s["max_done"], at("max_done", i, n + 1))
                            if n >= 2:
                                act.wait_ge(s["pT_done"], at("pT_done", i, n - 1))
                            for h in range(HH):
                                e = act.activation(PS[:, n % 2, h, :], PSUM[0:QS, n % 2, h * KS:(h + 1) * KS],
                                                   ACT.Exp, bias=NMX[:, b, n % 2, h:h + 1],
                                                   accum_out=DEN[:, b, n % 2, h:h + 1])
                            e.then_inc(s["exp_done"], 1)
                    if before:
                        if b == 1:
                            store(i - 1, 1)
                        for n in (2 * b, 2 * b + 1):
                            gelu(i - 1, NCHUNK // 2 + n)
                for n in (0, 2):
                    evacuate_oT(act, n, i)
                act.wait_ge(s["cls_weight"], at("cls_weight", i, 1))
                act.activation(CW[:], CW[:], ACT.Exp).then_inc(s["cls_exp"], 1)
                double(i, 1)
                if following:
                    states_tanh(i + 1)
                high_parts(i, 1)
                if before:
                    store(i - 1, 0)
                route_exp(i, 1)

            def rest(i):
                yield from empty(2)
                evacuate_oT(act, 4, i)
                yield
                yield from empty(4)
                double(i, 0)
                yield
                yield
                high_parts(i, 0)
                yield

            def experts(i, half, *side):
                step(side, STEPS_AHEAD)
                for n in range(NCHUNK // 2):
                    gelu(i, (1 - half) * NCHUNK // 2 + n)
                    step(side, sum(STEPS[n]))

            def load_weights(n):
                w, _, k = WEIGHTS[n]
                if n >= 2:
                    act.wait_ge(weights_split, n - 1)
                act.dma_start(STAGE[n % 2], w[:, k * PIECE:(k + 1) * PIECE]).then_inc(weights_loaded[n % 2], 16)

            load(0)
            load_weights(0)
            load_weights(1)
            states_tanh(0)
            for n, _ in enumerate(conv(0)):
                if n % 3 == 1 and n // 3 + 2 < len(WEIGHTS):
                    load_weights(n // 3 + 2)
            attention(0, False, True)
            experts(0, 1, rest(0), conv(1))
            with act.Fori(1, B - 1) as i:
                attention(i, True, True)
                experts(i, 1, rest(i), conv(i + 1))
            attention(B - 1, True, False)
            experts(B - 1, 1, rest(B - 1))
            route_exp(B - 1, 0)
            store(B - 1, 1)
            experts(B - 1, 0)
            store(B - 1, 0)
            for half in range(2):
                act.wait_ge(s[X2_FREE[half]], at(X2_FREE[half], B, 1))

        links, link_base = [0], [0]

        @block.vector
        def _(dve):
            def link(ins):
                links[0] += 1
                ins.then_inc(dve_link, 1)
                dve.wait_ge(dve_link, link_base[0] + links[0])

            def aggregate(tiles, tst, tmv, tv, eps, eps_sem):
                dve.memset(SPARE, 0.0)
                for t in range(*tiles):
                    last = dve.bn_aggr(tmv[:, t, :], tst[:, t, :])
                link(last)
                dve.tensor_scalar(tv[:, slice(*tiles)], tmv[:, slice(*tiles), 1], eps, None, ALU.add
                                  ).then_inc(s[eps_sem], 1)

            def norm_stats(src, tiles, eps, eps_sem):
                for t in range(*tiles):
                    last = dve.bn_stats(TST[:, t, :], src[:, t, :])
                link(last)
                aggregate(tiles, TST, TMV, TV, eps, eps_sem)

            def norm_tokens(src, tiles):
                for t in tiles:
                    last = dve.tensor_scalar(XN[:, t, 0:C], src[:, t, :], TMV[:, t, 0:1], TR[:, t:t + 1],
                                             ALU.subtract, ALU.mult)
                return last

            def norm_channels(i):
                dve.wait_ge(s["x_loaded"], at("x_loaded", i, 16))
                for j in range(2):
                    for h in range(2):
                        last = dve.bn_stats(GST[:, j, h, :], XR[:, j, 512 * h:512 * h + 512])
                link(last)
                dve.memset(SPARE, 0.0)
                for j in range(2):
                    last = dve.bn_aggr(MV[:, j, :], GST[:, j, :, :].rearrange("p a b -> p (a b)"))
                last.then_inc(s["gn_channel"], 1)

            def norm_spread(i):
                dve.wait_ge(s["gn_channel"], at("gn_channel", i, 1))
                dve.wait_ge(s["gn_mean"], at("gn_mean", i, 1))
                link(dve.tensor_copy(GM[:], PSUM[0:HC, 3, 0:2]))
                link(dve.tensor_tensor(GD[:], MV[:, :, 0], GM[:], ALU.subtract))
                link(dve.tensor_tensor(GD[:], GD[:], GD[:], ALU.mult))
                dve.tensor_tensor(GD[:], GD[:], MV[:, :, 1], ALU.add).then_inc(s["gn_spread"], 1)

            def norm_variance(i):
                dve.wait_ge(s["gn_var"], at("gn_var", i, 1))
                dve.tensor_scalar(GV[:], PSUM[0:HC, 3, 2:4], 1e-5, None, ALU.add).then_inc(s["gn_eps"], 1)

            def norm_image(i):
                dve.wait_ge(s["gn_rstd"], at("gn_rstd", i, 1))
                if not first(i):
                    dve.wait_ge(s["mix_done"], at("mix_done", i, 0))
                for j in range(2):
                    dve.tensor_scalar(XG[0:HC, j, :], XR[:, j, :], GM[:, j:j + 1], GR[:, j:j + 1], ALU.subtract,
                                      ALU.mult).then_inc(s["xg_ready"], 1)

            def add_image(i):
                link(dve.scalar_tensor_tensor(GNB[:], GM[:], -1.0, GR[:], ALU.mult, ALU.mult))
                link(dve.tensor_scalar(GR1[:], GR[:], 1.0, None, ALU.add))
                for j in range(2):
                    dve.tensor_scalar(XS[:, j, :], XR[:, j, :], GR1[:, j:j + 1], GNB[:, j:j + 1], ALU.mult,
                                      ALU.add).then_inc(s["xs_ready"], 1)

            def conv(i):
                dve.wait_ge(s["tanh_done"], at("tanh_done", i, 1))
                dve.scalar_tensor_tensor(GU[0:S, :].rearrange("p (w h) -> p h w", w=GW),
                                         TG[0:S, :].rearrange("p (h w) -> p h w", w=GW), 1.0,
                                         PSUM[0:S, 0:2, :].rearrange("p a (h w) -> p (a h) w", w=GW),
                                         ALU.add, ALU.mult).then_inc(s["gu_ready"], 1)
                yield
                dve.scalar_tensor_tensor(GU[32:32 + S, :].rearrange("p (a b) -> p a b", a=2),
                                         TG[32:32 + S, :].rearrange("p (a b) -> p a b", a=2), 1.0,
                                         PSUM[32:32 + S, 0:2, :],
                                         ALU.add, ALU.mult).then_inc(s["gu_ready"], 1)
                yield
                yield from empty(2)
                for tp in range(NP):
                    dve.wait_ge(s["xgT_done"], at("xgT_done", i, tp + 1))
                    for t in range(2):
                        dve.bn_stats(GTST[:, 2 * tp + t, :], PSUM[:, tp % 2, t * C:(t + 1) * C])
                    dve.tensor_copy(H1[:, 2 * tp:2 * tp + 2, :],
                                    PSUM[:, tp % 2, 2 * C:2 * C + 64].rearrange("p (t o) -> p t o", t=2)
                                    ).then_inc(s["h1_read"], 1)
                    if tp < NP - 1:
                        yield
                dve.wait_ge(s["h1_read"], at("h1_read", i, NP))
                aggregate((0, NT), GTST, GTMV, GTV, 1e-6, "mixln_eps")
                yield
                dve.wait_ge(s["mixln_rstd"], at("mixln_rstd", i, 1))
                link(dve.tensor_tensor(H1[:], H1[:], GTR[:].unsqueeze(2).broadcast_to((128, NT, 32)), ALU.mult))
                dve.tensor_tensor(H1[:], H1[:], BG1[:].unsqueeze(1).broadcast_to((128, NT, 32)), ALU.add
                                  ).then_inc(s["h1_pre"], 1)
                yield
                yield from empty(4)
                for tp in range(NP):
                    dve.wait_ge(s["mix_tanh"], at("mix_tanh", i, tp + 1))
                    link(dve.scalar_tensor_tensor(EM[:], TM[:], 1.0, PSUM[:, 1 + tp % 2, 0:2 * C], ALU.add, ALU.mult))
                    dve.scalar_tensor_tensor(X1[:, 2 * tp:2 * tp + 2, :].rearrange("p a b -> p (a b)"), EM[:], 0.5,
                                             PSUM[:, 3, 0:2 * C], ALU.mult, ALU.add).then_inc(s["mixed"], 1)
                    yield
                    dve.wait_ge(s["mixed"], at("mixed", i, tp + 1))
                    for t in range(2 * tp, 2 * tp + 2):
                        last_stats = dve.bn_stats(TST[:, t, :], X1[:, t, :])
                    if tp == NP - 1:
                        link(last_stats)
                        aggregate((0, NT), TST, TMV, TV, 1e-5, "ln1_eps")
                        dve.tensor_scalar(NMR[:], TMV[:, :, 0], -1.0, None, ALU.mult).then_inc(s["ln1_mean"], 1)
                    yield
                yield from empty(4)
                dve.wait_ge(s["xn1T_done"], at("xn1T_done", i, 1))
                windows(dve.tensor_copy, 1, 0, s["win_dve"])
                yield
                windows(dve.tensor_copy, 1, 1, s["win_dve"])
                yield
                for n in range(PIECES):
                    if n % 2 == 1:
                        dve.wait_ge(s["piece_done"], at("piece_done", i, n + 1))
                        evacuate_piece(dve, n, s["piece_dve"])
                    yield

            def split(i, n):
                dve.wait_ge(s["gelu_done"], at("gelu_done", i, n + 1))
                if n >= 2:
                    dve.wait_ge(s["ffn2_chunk"], at("ffn2_chunk", i, n - 1))
                dve.tensor_scalar(HHI[:, n % 2, :], HF[:, n % 2, :], H_UP, None, ALU.mult
                                  ).then_inc(s["hh_ready"], 1)
                dve.wait_ge(s["hh_ready"], at("hh_ready", i, n + 1))
                dve.scalar_tensor_tensor(HLO[:, n % 2, :], HF[:, n % 2, :], H_UP, HHI[:, n % 2, :], ALU.mult,
                                         ALU.subtract).then_inc(s["hl_ready"], 1)

            def add_expert(i, g):
                half, e = 1 - g // E, g % E
                dve.wait_ge(s["ffn2_chunk"], at("ffn2_chunk", i, (g + 1) * HK))
                if g:
                    dve.wait_ge(s["ffn_added"], at("ffn_added", i, g))
                if e == 0:
                    dve.wait_ge(s["gates_ready"], at("gates_ready", i, 2 - half))
                for q in range(4):
                    t = 4 * half + q
                    last = dve.scalar_tensor_tensor(X2[:, t, :], PSUM[:, 6 + q // 2, (q % 2) * C:(q % 2 + 1) * C],
                                                    GATE[:, t, e:e + 1], X2[:, t, :], ALU.mult, ALU.add)
                last.then_inc(s["ffn_added"], 1)

            def attention(i, before, following):
                half0 = NCHUNK // 2

                def copy_turned(n):
                    dve.wait_ge(s["pT_done"], at("pT_done", i, n + 1))
                    dve.tensor_copy(PT[:, n % 2, :, :], PSUM[0:KS, 2 + n % 2, 0:HH * QS].rearrange(
                        "p (h q) -> p h q", h=HH)).then_inc(s["pT_copied"], 1)

                def normalize(b):
                    dve.wait_ge(s["exp_done"], at("exp_done", i, 2 * b + 2))
                    link(dve.reciprocal(RDEN[:, b, :, :], DEN[:, b, :, :]))
                    dve.wait_ge(s["pv_done"], at("pv_done", i, b + 1))
                    dve.tensor_tensor(OS[:, b, :].rearrange("p (h d) -> p h d", h=HEADS),
                                      PSUM[0:QS, 2, O_COL:O_COL + C].rearrange("p (h d) -> p h d", h=HEADS),
                                      RDEN[:, b, :, :].rearrange("p a h -> p (a h)").unsqueeze(2).broadcast_to(
                                          (QS, HEADS, HD)), ALU.mult).then_inc(s["o_normed"], 1)

                for b in range(NB + 1):
                    if following and b == 3:
                        norm_spread(i + 1)
                    if b < NB:
                        for n in (2 * b, 2 * b + 1):
                            dve.wait_ge(s["score_done"], at("score_done", i, n + 1))
                            dve.tensor_reduce(NMX[:, b, n % 2, :],
                                              PSUM[0:QS, n % 2, 0:HH * KS].rearrange("p (h k) -> p h k", h=HH),
                                              AX.X, ALU.max, negate=True).then_inc(s["max_done"], 1)
                    if following and b == 3:
                        norm_variance(i + 1)
                    if before and b >= 4 and b % 3 == 1:
                        add_expert(i - 1, E + (b - 4) // 3)
                    if b >= 1:
                        copy_turned(2 * b - 2)
                        if before:
                            split(i - 1, half0 + 2 * b - 2)
                        copy_turned(2 * b - 1)
                        if before:
                            split(i - 1, half0 + 2 * b - 1)
                        normalize(b - 1)
                    if before and b == 0:
                        gates(i - 1, 0)
                    if following and b == 1:
                        norm_channels(i + 1)
                    if following and b == 4:
                        norm_image(i + 1)
                    if following and b == 5:
                        add_image(i + 1)
                if before:
                    split(i - 1, NCHUNK - 2)
                for n in (1, 3):
                    evacuate_oT(dve, n, i)
                nm = NMX[0:1].rearrange("p b a h -> p b (a h)")
                link(dve.tensor_reduce(CM[:], NMX[0:1].rearrange("p b a h -> p (a h) b"), AX.X, ALU.min))
                dve.scalar_tensor_tensor(CW[:], nm, -1.0, CM[:].unsqueeze(1).broadcast_to((1, NB, HEADS)), ALU.mult,
                                         ALU.add).then_inc(s["cls_weight"], 1)
                if before:
                    split(i - 1, NCHUNK - 1)
                dve.wait_ge(s["x2b_free"], at("x2b_free", i, 1))
                for tp in (2, 3):
                    add_attention(i, tp)
                    dve.wait_ge(s["x2_ready"], at("x2_ready", i, tp - 1))
                    for t in (2 * tp, 2 * tp + 1):
                        last_stats = dve.bn_stats(TST[:, t, :], X2[:, t, :])
                link(last_stats)
                aggregate((4, 8), TST, TMV, TV, 1e-5, "ln2_eps")
                dve.wait_ge(s["cls_exp"], at("cls_exp", i, 1))
                link(dve.tensor_tensor(CW[:], CW[:], DEN[0:1].rearrange("p b a h -> p b (a h)"), ALU.mult))
                link(dve.tensor_reduce(CSUM[:], CW[:].rearrange("p b h -> p h b"), AX.X, ALU.add))
                link(dve.reciprocal(CSUM[:], CSUM[:]))
                dve.tensor_tensor(CW[:], CW[:], CSUM[:].unsqueeze(1).broadcast_to((1, NB, HEADS)), ALU.mult
                                  ).then_inc(s["cls_coef"], 1)
                dve.wait_ge(s["ln2_rstd"], at("ln2_rstd", i, 1))
                norm_tokens(X2, range(4, 8)).then_inc(s["xn2_ready"], 1)
                if before:
                    add_expert(i - 1, 2 * E - 1)
                low_parts(i, 1)
                route(i, 1)

            def add_attention(i, tp):
                pair = slice(2 * tp, 2 * tp + 2)
                k = (tp + 2) % 4
                dve.wait_ge(s["wo_done"], at("wo_done", i, k + 1))
                dve.tensor_tensor(X2[:, pair, :].rearrange("p a b -> p (a b)"),
                                  X1[:, pair, :].rearrange("p a b -> p (a b)"),
                                  PSUM[:, WO_BANK[tp], 0:2 * C], ALU.add).then_inc(s["x2_ready"], 1)

            def low_parts(i, half):
                for a in range(2):
                    k = 2 * (1 - half) + a + 1
                    dve.wait_ge(s["xh_ready"], at("xh_ready", i, k))
                    tok = slice(half * NH, (half + 1) * NH)
                    dve.scalar_tensor_tensor(XL[:, a, tok], bank(2 * half + a), X_UP, XH[:, a, tok], ALU.mult,
                                             ALU.subtract).then_inc(s["xl_ready"], 1)

            def route(i, half):
                tiles = slice(4 * half, 4 * half + 4)
                dve.wait_ge(s["route_done"], at("route_done", i, 2 - half))
                gb = GB[:].unsqueeze(1).broadcast_to((128, 4, E))
                link(dve.scalar_tensor_tensor(SC[:, tiles], PSUM[:, 2, 0:4 * E].rearrange("p (t e) -> p t e", t=4),
                                              1 / (X_UP * W_UP), gb, ALU.mult, ALU.add))
                link(dve.tensor_reduce(SM[:, tiles], SC[:, tiles], AX.X, ALU.max))
                sm = SM[:, tiles].unsqueeze(2).broadcast_to((128, 4, E))
                dve.tensor_tensor(SC[:, tiles], SC[:, tiles], sm, ALU.subtract).then_inc(s["route_shift"], 1)

            def gates(i, half):
                tiles = slice(4 * half, 4 * half + 4)
                se, sm1, win = SE[:, tiles], SM[:, tiles], WIN[:, tiles]
                sm = sm1.unsqueeze(2).broadcast_to((128, 4, E))
                dve.wait_ge(s["route_exp"], at("route_exp", i, 2 - half))
                link(dve.tensor_reduce(sm1, se, AX.X, ALU.add))
                link(dve.reciprocal(sm1, sm1))
                link(dve.tensor_tensor(se, se, sm, ALU.mult))
                mine = se.unsqueeze(3).broadcast_to((128, 4, E, E))
                other = se.unsqueeze(2).broadcast_to((128, 4, E, E))
                dve.tensor_tensor(CMPA[:], mine, other, ALU.is_ge)
                link(dve.tensor_tensor(CMPB[:], mine, other, ALU.is_gt))
                dve.tensor_tensor(CMPA[:], CMPA[:], AFTER[:].unsqueeze(1).broadcast_to((128, 4, E, E)), ALU.mult)
                link(dve.tensor_tensor(CMPB[:], CMPB[:], BEFORE[:].unsqueeze(1).broadcast_to((128, 4, E, E)),
                                       ALU.mult))
                link(dve.tensor_tensor(CMPA[:], CMPA[:], CMPB[:], ALU.add))
                link(dve.tensor_reduce(win, CMPA[:], AX.X, ALU.add))
                link(dve.scalar_tensor_tensor(win, win, 2.0, se, ALU.is_ge, ALU.mult))
                link(dve.tensor_reduce(sm1, win, AX.X, ALU.add))
                link(dve.tensor_scalar(sm1, sm1, 1e-9, None, ALU.add))
                link(dve.reciprocal(sm1, sm1))
                dve.scalar_tensor_tensor(GATE[:, tiles], win, 1 / (W_UP * H_UP), sm, ALU.mult, ALU.mult
                                         ).then_inc(s["gates_ready"], 1)

            def rest(i):
                yield from empty(2)
                evacuate_oT(dve, 5, i)
                dve.wait_ge(s["oT_copied"], at("oT_copied", i, 6))
                dve.wait_ge(s["cls_spread"], at("cls_spread", i, 1))
                link(dve.tensor_tensor(OC[:], OC[:], PSUM[0:HC, 2, 0:2 * NB].rearrange("p (a b) -> p a b", a=2),
                                       ALU.mult))
                link(dve.tensor_reduce(OC1[:], OC[:], AX.X, ALU.add))
                dve.tensor_tensor(OT[:, :, 0], OC1[:], BV[:], ALU.add).then_inc(s["cls_ready"], 1)
                yield
                gates(i, 1)
                yield
                dve.wait_ge(s["x2a_free"], at("x2a_free", i, 1))
                for tp in (0, 1):
                    add_attention(i, tp)
                yield
                dve.wait_ge(s["x2_ready"], at("x2_ready", i, 4))
                norm_stats(X2, (0, 4), 1e-5, "ln2_eps")
                yield
                dve.wait_ge(s["ln2_rstd"], at("ln2_rstd", i, 2))
                norm_tokens(X2, range(4)).then_inc(s["xn2_ready"], 1)
                yield
                yield
                yield from empty(2)
                low_parts(i, 0)
                yield
                yield
                route(i, 0)
                yield

            def experts(i, half, *side):
                g0, n0 = (1 - half) * E, (1 - half) * NCHUNK // 2
                step(side, STEPS_AHEAD)
                for n in range(NCHUNK // 2):
                    if n > 1 and n % HK == 1:
                        add_expert(i, g0 + n // HK - 1)
                    split(i, n0 + n)
                    step(side, sum(STEPS[n]))
                add_expert(i, g0 + E - 1)

            def split_weights(n):
                _, kind, k = WEIGHTS[n]
                cols = slice(k * PIECE, (k + 1) * PIECE)
                hi = {"a": W1AH[:], "b": W1B[:], "2": W2H[:].rearrange("p a b -> p (a b)")}[kind][:, cols]
                dve.wait_ge(weights_loaded[n % 2], 16 * (n // 2 + 1))
                link(dve.tensor_scalar(hi, STAGE[n % 2], W_UP, None, ALU.mult))
                if kind == "b":
                    low = dve.scalar_tensor_tensor(hi[64:128], STAGE[n % 2][64:128], W_UP, hi[64:128], ALU.mult,
                                                   ALU.subtract)
                else:
                    lo = {"a": W1AL[:], "2": W2L[:].rearrange("p a b -> p (a b)")}[kind][:, cols]
                    low = dve.scalar_tensor_tensor(lo, STAGE[n % 2], W_UP, hi, ALU.mult, ALU.subtract)
                low.then_inc(weights_split, 1)

            def links_from(base):
                made = links[0]
                links[0], link_base[0] = 0, base
                return made

            for half in range(2):
                dve.memset(SPARE, 0.0).then_inc(s[X2_FREE[half]], 1)
                dve.wait_ge(s[X2_FREE[half]], 1)
            for part in (norm_channels, norm_spread, norm_variance, norm_image, add_image):
                part(0)
            for n, _ in enumerate(conv(0)):
                if n % 3 == 0 and n // 3 < len(WEIGHTS):
                    split_weights(n // 3)
            attention(0, False, True)
            experts(0, 1, rest(0), conv(1))
            assert links[0] == LINKS_FIRST, links[0]
            with dve.Fori(1, B - 1) as i:
                links_from(LINKS_FIRST - LINKS + i * LINKS)
                attention(i, True, True)
                experts(i, 1, rest(i), conv(i + 1))
                assert links[0] == LINKS, links[0]
            links_from(LINKS_FIRST + (B - 2) * LINKS)
            attention(B - 1, True, False)
            experts(B - 1, 1, rest(B - 1))
            gates(B - 1, 0)
            experts(B - 1, 0)

        @block.tensor
        def _(pe):
            def group_mean(i):
                pe.wait_ge(s["gn_channel"], at("gn_channel", i, 1))
                pe.matmul(PSUM[0:HC, 3, 0:2], GAVG[:], MV[:, :, 0], start=True, stop=True).then_inc(s["gn_mean"], 1)

            def group_variance(i):
                pe.wait_ge(s["gn_spread"], at("gn_spread", i, 1))
                pe.matmul(PSUM[0:HC, 3, 2:4], GAVG[:], GD[:], start=True, stop=True).then_inc(s["gn_var"], 1)

            def project_states(i):
                pe.wait_ge(s["xg_ready"], at("xg_ready", i, 2))
                for half in range(2):
                    for j in range(2):
                        k = 97 - j
                        mm = pe.matmul(bank(half), PROJ[0:k, j, :], XG[0:k, j, half * 512:(half + 1) * 512],
                                       start=(j == 0), stop=(j == 1))
                mm.then_inc(s["proj_done"], 1)

            def conv(i):
                yield from empty(4)
                pe.wait_ge(s["gu_ready"], at("gu_ready", i, 2))
                for tp in range(NP):
                    if tp >= 2:
                        pe.wait_ge(s["h1_read"], at("h1_read", i, tp - 1))
                    for t in range(2):
                        tok = slice((2 * tp + t) * 128, (2 * tp + t + 1) * 128)
                        for j in range(2):
                            pe.transpose(PSUM[:, tp % 2, t * C + j * HC:t * C + (j + 1) * HC],
                                         XG[0:HC, j, tok], EYE[0:HC, 0:HC])
                        for j in range(2):
                            mm = pe.matmul(PSUM[:, tp % 2, 2 * C + t * 32:2 * C + (t + 1) * 32],
                                           XG[0:HC, j, tok], WG1[:, j, :], start=(j == 0), stop=(j == 1))
                    mm.then_inc(s["xgT_done"], 1)
                    if tp == 1:
                        pe.wait_ge(s["gu_moved"], at("gu_moved", i, 16 * 2 * KP))
                        for kind in range(2):
                            for d in (0, 1, -1, 2, -2, 3, -3):
                                first_in, n = max(0, -d), KC - abs(d)
                                c = (kind * KC + first_in + d) * GW
                                mm = pe.matmul(PSUM[:, 3, c:c + n * GW], SCAN[:, kind, d + KC - 1, :],
                                               GUP[:, kind, first_in:first_in + n, :], start=(d == 0),
                                               stop=(d == 1 - KC), skip_group_check=True)
                        mm.then_inc(s["scan_done"], 1)
                    yield
                yield
                pe.wait_ge(s["h1_read"], at("h1_read", i, NP))
                pe.wait_ge(s["hs_copied"], at("hs_copied", i, 1))
                pe.wait_ge(s["h1_gelu"], at("h1_gelu", i, 1))
                for g in range(2):
                    mm = pe.transpose(PSUM[:, 3, g * 128:(g + 1) * 128],
                                      H1[:, 4 * g:4 * g + 4, :].rearrange("p a b -> p (a b)"), EYE[:])
                mm.then_inc(s["h1T_done"], 1)
                yield
                yield from empty(2)
                pe.wait_ge(s["h1T_copied"], at("h1T_copied", i, 1))
                pe.wait_ge(s["hs_cols_moved"], at("hs_cols_moved", i, 16 * KP))
                pe.wait_ge(s["hs_placed"], at("hs_placed", i, 16))
                pe.wait_ge(s["xs_ready"], at("xs_ready", i, 2))
                for tp in range(NP):
                    if tp:
                        pe.wait_ge(s["mixed"], at("mixed", i, tp))
                    if tp == 1 and not first(i):
                        pe.wait_ge(s["route_shift"], at("route_shift", i, 0))
                    for t in range(2):
                        tt = 2 * tp + t
                        tok = slice(tt * 128, tt * 128 + 128)
                        col = slice(t * C, (t + 1) * C)
                        pe.matmul(PSUM[:, 0, col], H1T[:, tt // 4, :], WG2[:, tt % 4, :], start=True, stop=False)
                        pe.matmul(PSUM[:, 0, col], ONES3[:], ROWS3[:, 0:C], start=False, stop=True)
                        for j in range(2):
                            pe.matmul(PSUM[:, 1 + tp % 2, col], XG[0:113, j, tok], WY[:, j, :], start=(j == 0),
                                      stop=(j == 1))
                        for j in range(2):
                            mm = pe.transpose(PSUM[:, 3, t * C + j * HC:t * C + (j + 1) * HC], XS[:, j, tok],
                                              EYE[0:HC, 0:HC])
                    mm.then_inc(s["mix_done"], 1)
                    yield from empty(2)
                yield from empty(3)
                pe.wait_ge(s["mixed"], at("mixed", i, NP))
                for k in range(2):
                    pe.wait_ge(s["xn1_ready"], at("xn1_ready", i, k + 1))
                    for t in range(4 * k, 4 * k + 4):
                        for j in range(2):
                            mm = pe.transpose(PSUM[0:HC, 2 * j + t // 4, (t % 4) * 128:(t % 4 + 1) * 128],
                                              XN[:, t, j * HC:(j + 1) * HC], EYE[:])
                    if k == 1:
                        mm.then_inc(s["xn1T_done"], 1)
                    yield
                yield from empty(2)
                pe.wait_ge(s["win_act"], at("win_act", i, 1))
                pe.wait_ge(s["win_dve"], at("win_dve", i, 1))
                for n in range(PIECES):
                    project(i, n)
                    yield

            def project(i, n):
                if n >= 4:
                    m = n - 4
                    nm = ("piece_act", "piece_dve")[m % 2]
                    pe.wait_ge(s[nm], at(nm, i, m // 2 + 1))
                if n < 12:
                    W = WQ if n < 6 else WK
                    oh, (b0, b1) = (n % 6) // 3, SPANS[n % 3]
                    keys = slice(PAD, PAD + QB) if n < 6 else slice(0, KS)
                    width = (b1 - b0) * (QB if n < 6 else KS)
                    for j in range(2):
                        mm = pe.matmul(PSUM[0:HC, n % 4, 0:width], W[:, j, oh * HC:(oh + 1) * HC],
                                       XW[:, j, b0:b1, keys], start=(j == 0), stop=(j == 1))
                    if n < 6 and n % 3 == 2:
                        for j in range(2):
                            mm = pe.matmul(PSUM[0:HC, n % 4, 400:401], W[:, j, oh * HC:(oh + 1) * HC],
                                           XW[:, j, 0, KW:KS], start=(j == 0), stop=(j == 1))
                else:
                    for b in range(2 * (n - 12), min(2 * (n - 12) + 2, NB)):
                        for j in range(2):
                            mm = pe.matmul(PSUM[0:KS, n % 4, (b % 2) * C:(b % 2 + 1) * C], XW[:, j, b, :],
                                           WV[:, j, :], start=(j == 0), stop=(j == 1))
                mm.then_inc(s["piece_done"], 1)

            def ffn1(i, n):
                half, ek = 1 - n // (E * HK), n % (E * HK)
                tok = slice(half * NH, (half + 1) * NH)
                w = slice(ek * 128, (ek + 1) * 128)
                if n >= 2:
                    pe.wait_ge(s["gelu_done"], at("gelu_done", i, n - 1))
                dst = bank(4 + n % 2)
                pe.matmul(dst, W1AH[:, w], XH[:, 0, tok], start=True, stop=False)
                pe.matmul(dst, W1AH[:, w], XL[:, 0, tok], start=False, stop=False)
                pe.matmul(dst, W1AL[:, w], XH[:, 0, tok], start=False, stop=False)
                pe.matmul(dst, W1B[:, w], XH[:, 1, tok], start=False, stop=False)
                pe.matmul(dst, W1B[:, w], XL[:, 1, tok], start=False, stop=True).then_inc(s["ffn1_done"], 1)

            def ffn2(i, n):
                g, k = divmod(n, HK)
                e = g % E
                if k == 0 and not (g == 0 and first(i)):
                    pe.wait_ge(s["ffn_added"], at("ffn_added", i, g))
                pe.wait_ge(s["hh_ready"], at("hh_ready", i, n + 1))
                pe.wait_ge(s["hl_ready"], at("hl_ready", i, n + 1))
                for q in range(4):
                    dst = PSUM[:, 6 + q // 2, (q % 2) * C:(q % 2 + 1) * C]
                    tok = slice(q * 128, (q + 1) * 128)
                    if k == 0:
                        pe.matmul(dst, ONES3[:], ROWS3[:, (2 + e) * C:(3 + e) * C], start=(q % 2 == 0), stop=False,
                                  skip_group_check=True)
                    pe.matmul(dst, HHI[:, n % 2, tok], W2H[:, e * HK + k, :], start=False, stop=False,
                              skip_group_check=True)
                    pe.matmul(dst, HHI[:, n % 2, tok], W2L[:, e * HK + k, :], start=False, stop=False,
                              skip_group_check=True)
                    mm = pe.matmul(dst, HLO[:, n % 2, tok], W2H[:, e * HK + k, :], start=False,
                                   stop=(k == HK - 1), skip_group_check=True)
                mm.then_inc(s["ffn2_chunk"], 1)

            def attention(i, before, following):
                half0 = NCHUNK // 2
                pe.wait_ge(s["piece_act"], at("piece_act", i, PIECES // 2))
                pe.wait_ge(s["piece_dve"], at("piece_dve", i, PIECES // 2))

                def scores(n):
                    b, oh = n // 2, n % 2
                    if n >= 2:
                        pe.wait_ge(s["exp_done"], at("exp_done", i, n - 1))
                    pe.matmul(PSUM[0:QS, n % 2, 0:HH * KS], QT[:, oh, b, :],
                              KBD[:, oh, b, :, :].rearrange("p h k -> p (h k)"), start=True, stop=False)
                    v = 0 if b == 0 else 2 if b == NB - 1 else 1
                    pe.matmul(PSUM[0:QS, n % 2, 0:HH * KS], EYEB[:], MASKB[:, v, :], start=False, stop=True
                              ).then_inc(s["score_done"], 1)

                def turn(n):
                    pe.wait_ge(s["exp_done"], at("exp_done", i, n + 1))
                    if n >= 2:
                        pe.wait_ge(s["pT_copied"], at("pT_copied", i, n - 1))
                        pe.wait_ge(s["o_normed"], at("o_normed", i, n // 2))
                    for h in range(HH):
                        mm = pe.transpose(PSUM[0:KS, 2 + n % 2, h * QS:(h + 1) * QS], PS[:, n % 2, h, :],
                                          EYE[0:QS, 0:QS])
                    mm.then_inc(s["pT_done"], 1)

                def values(n):
                    b, oh = n // 2, n % 2
                    pe.wait_ge(s["pT_copied"], at("pT_copied", i, n + 1))
                    for h in range(HH):
                        c = oh * HC + h * HD
                        mm = pe.matmul(PSUM[0:QS, 2, O_COL + c:O_COL + c + HD], PT[:, n % 2, h, :],
                                       VW[:, b, c:c + HD], start=True, stop=True)
                    if oh == 1:
                        mm.then_inc(s["pv_done"], 1)

                for b in range(NB + 1):
                    if b < NB:
                        scores(2 * b)
                        scores(2 * b + 1)
                    if following and b == 3:
                        group_variance(i + 1)
                    if b >= 1:
                        turn(2 * b - 2)
                        if following and b == 3:
                            pe.wait_ge(s["gn_eps"], at("gn_eps", i + 1, 1))
                        turn(2 * b - 1)
                    if before:
                        ffn1(i - 1, half0 + 2 * b)
                        ffn1(i - 1, half0 + 2 * b + 1)
                    if b >= 1:
                        if before:
                            ffn2(i - 1, half0 + 2 * b - 2)
                        values(2 * b - 2)
                        values(2 * b - 1)
                        if before:
                            ffn2(i - 1, half0 + 2 * b - 1)
                    if following and b == 2:
                        group_mean(i + 1)
                pe.wait_ge(s["pT_copied"], at("pT_copied", i, 2 * NB))
                pe.wait_ge(s["o_normed"], at("o_normed", i, NB))
                for n in range(4):
                    turn_output(n)
                if before:
                    ffn2(i - 1, NCHUNK - 2)
                pe.wait_ge(s["oT_copied"], at("oT_copied", i, 4))
                for tp in (2, 3):
                    output(i, tp)
                if before:
                    ffn2(i - 1, NCHUNK - 1)
                if following:
                    project_states(i + 1)
                turn_tokens(i, 1)
                router(i, 1)

            def turn_output(n):
                oh, (b0, b1), at_bank = oT_piece(n)
                for b in range(b0, b1):
                    mm = pe.transpose(PSUM[0:HC, at_bank, (b - b0) * QS:(b - b0 + 1) * QS],
                                      OS[:, b, oh * HC:(oh + 1) * HC], EYE[0:QS, 0:QS])
                mm.then_inc(s["oT_done"], 1)

            def output(i, tp):
                for t in range(2):
                    c = (2 * tp + t) * 128
                    dst = PSUM[:, WO_BANK[tp], t * C:(t + 1) * C]
                    for j in range(2):
                        pe.matmul(dst, OT[:, j, c:c + 128], WO[:, j, :], start=(j == 0), stop=False)
                    mm = pe.matmul(dst, ONES3[:], ROWS3[:, C:2 * C], start=False, stop=True)
                mm.then_inc(s["wo_done"], 1)

            def turn_tokens(i, half):
                pe.wait_ge(s["xn2_ready"], at("xn2_ready", i, 2 - half))
                for a in range(2):
                    if a == 1:
                        pe.wait_ge(s["xn2_doubled"], at("xn2_doubled", i, 2 - half))
                    for t in range(4):
                        mm = pe.transpose(PSUM[:, 2 * half + a, t * 128:(t + 1) * 128],
                                          XN[:, 4 * half + t, 128 * a:128 * (a + 1)], EYE[:])
                    mm.then_inc(s["xn2T_done"], 1)

            def router(i, half):
                pe.wait_ge(s["xl_ready"], at("xl_ready", i, 4 - 2 * half))
                for t in range(4):
                    tok = slice((4 * half + t) * 128, (4 * half + t + 1) * 128)
                    dst = PSUM[:, 2, t * E:(t + 1) * E]
                    pe.matmul(dst, XH[:, 0, tok], GWAH[:], start=True, stop=False)
                    pe.matmul(dst, XH[:, 0, tok], GWAL[:], start=False, stop=False)
                    pe.matmul(dst, XL[:, 0, tok], GWAH[:], start=False, stop=False)
                    pe.matmul(dst, XH[:, 1, tok], GWB[:], start=False, stop=False)
                    mm = pe.matmul(dst, XL[:, 1, tok], GWB[:], start=False, stop=True)
                mm.then_inc(s["route_done"], 1)

            def rest(i):
                yield from empty(2)
                if not last(i):
                    pe.wait_ge(s["gu_ready"], at("gu_ready", i + 1, 2))
                pe.wait_ge(s["route_shift"], at("route_shift", i, 1))
                pe.wait_ge(s["cls_coef"], at("cls_coef", i, 1))
                for n in (4, 5):
                    turn_output(n)
                for h in range(HEADS):
                    mm = pe.matmul(PSUM[h % HH * HD:(h % HH + 1) * HD, 2, h // HH * NB:(h // HH + 1) * NB], ONE32[:],
                                   CW[:, :, h], start=True, stop=True)
                mm.then_inc(s["cls_spread"], 1)
                yield
                pe.wait_ge(s["oT_copied"], at("oT_copied", i, 6))
                pe.wait_ge(s["cls_ready"], at("cls_ready", i, 1))
                for tp in (0, 1):
                    output(i, tp)
                yield
                yield
                pe.wait_ge(s["x2_ready"], at("x2_ready", i, 4))
                yield
                yield from empty(3)
                if not last(i):
                    pe.wait_ge(s["h1_read"], at("h1_read", i + 1, NP))
                turn_tokens(i, 0)
                yield
                yield from empty(2)
                router(i, 0)
                yield

            def experts(i, half, *side):
                n0 = (1 - half) * NCHUNK // 2
                step(side, STEPS_AHEAD)
                for n in range(NCHUNK // 2 + 1):
                    if n < NCHUNK // 2:
                        ffn1(i, n0 + n)
                    step(side, STEPS[n][0])
                    if n >= 1:
                        ffn2(i, n0 + n - 1)
                    step(side, STEPS[n][1])

            for part in (group_mean, group_variance, project_states):
                part(0)
            for _ in conv(0):
                pass
            attention(0, False, True)
            pe.wait_ge(weights_split, len(WEIGHTS))
            experts(0, 1, rest(0), conv(1))
            with pe.Fori(1, B - 1) as i:
                attention(i, True, True)
                experts(i, 1, rest(i), conv(i + 1))
            attention(B - 1, True, False)
            experts(B - 1, 1, rest(B - 1))
            experts(B - 1, 0)


def kernel(**inputs):
    import numpy as np
    import concourse.bacc as bacc
    from concourse.bass_utils import run_bass_kernel_spmd as run

    a = {k: np.asarray(v) for k, v in inputs.items()}
    r = {k[len("L0_conv_row_"):]: v for k, v in a.items() if k.startswith("L0_conv_row_")}
    c = {k[len("L0_conv_col_"):]: v for k, v in a.items() if k.startswith("L0_conv_col_")}
    f = np.float32

    def halves(w):
        return np.ascontiguousarray(w.reshape(2, HC, -1).transpose(1, 0, 2))

    def vec(v):
        return np.ascontiguousarray(v.reshape(2, HC).T)

    proj = np.zeros((97, 2, 128), f)
    for k, (w, bb) in enumerate(((r["Win"], r["bin"]), (c["Win"], c["bin"]), (r["Wg"], r["bg"]), (c["Wg"], c["bg"]))):
        proj[0:HC, :, 32 * k:32 * k + S] = halves(w.T)
        proj[96, 0, 32 * k:32 * k + S] = bb
    ya, yb = np.zeros((113, 2, C), f), np.zeros((113, 2, C), f)
    ya[0:HC], yb[0:HC] = halves(r["Wskip"].T), halves(c["Wskip"].T)
    ya[96, 0], yb[96, 0] = r["bout"], r["bskip"]
    ya[96, 1], yb[96, 1] = c["bout"], c["bskip"]
    ya[97:, 0], ya[97:, 1] = r["Wout"].T, c["Wout"].T
    yscale = np.full((113, 1), 0.5, f)
    yscale[97:] = 0.125
    sv, su, sa = np.zeros((S, 2 * S), f), np.zeros((S, 2 * S), f), np.zeros((2 * S, 1), f)
    R = r["U"].shape[1]
    for k, p in enumerate((r, c)):
        sv[k * R:(k + 1) * R, k * S:(k + 1) * S] = p["V"].T
        su[k * R:(k + 1) * R, k * S:(k + 1) * S] = p["U"].T
        sa[k * S:(k + 1) * S, 0] = p["a_logit"]
    g2 = np.zeros((4, 32, 4, C), f)
    for k in range(4):
        g2[k, :, k] = a["L0_conv_g2_w"].T
    g2 = g2.reshape(128, 4, C)
    gavg = np.kron(np.eye(HC // GROUP), np.full((GROUP, GROUP), 1.0 / GROUP)).astype(f)
    mask = np.full((QS, 3, HH, KS), NEG, f)
    for v, b in enumerate((0, 1, NB - 1)):
        for q in range(1, QS):
            for k in range(q - 1, q + 2 * PAD):
                if 1 <= b * QB + 1 - PAD + k < T:
                    mask[q, v, :, k] = 0.0
            mask[q, v, :, KW] = 0.0
        mask[0, v, :, PAD:PAD + QB] = 0.0
    mask[0, 0, :, KW] = 0.0
    w1, w2 = a["L1_ffn_w1"], a["L1_ffn_w2"]
    w1t = w1.transpose(1, 0, 2).reshape(C, E * HID)
    ins = dict(
        x=np.ascontiguousarray(a["x"].reshape(B, 2, HC, T).transpose(0, 2, 1, 3)),
        proj_w=proj, y_wa=ya, y_wb=yb, y_scale=yscale, eye=np.eye(128, dtype=f), gavg=gavg,
        cavg=np.full((HC, HC), 1.0 / C, f), norm_w=vec(a["L0_conv_norm_w"]), norm_b=vec(a["L0_conv_norm_b"]),
        g1_wT=halves(a["L0_conv_g1_w"].T), g1_b=a["L0_conv_g1_b"].reshape(1, -1),
        g2_wT=g2,
        bias_row=np.concatenate([a["L0_conv_g2_b"], a["L1_attn_bo"], a["L1_ffn_b2"].reshape(-1)]).reshape(1, -1),
        scan_v=sv, scan_u=su, scan_a=sa,
        wq=halves(a["L1_attn_Wq"]), wk=halves(a["L1_attn_Wk"]), wv=halves(a["L1_attn_Wv"]), wo=halves(a["L1_attn_Wo"]),
        bq=vec(a["L1_attn_bq"]), bk=vec(a["L1_attn_bk"]), bv=vec(a["L1_attn_bv"]),
        mask=mask.reshape(QS, -1),
        w1a=np.ascontiguousarray(w1t[0:128]), w1b=np.ascontiguousarray(np.tile(w1t[128:], (2, 1))),
        w2=np.ascontiguousarray(w2.reshape(E, HK, 128, C).transpose(2, 0, 1, 3)).reshape(128, -1),
        b1=np.ascontiguousarray(a["L1_ffn_b1"].reshape(E * HK, 128).T),
        gate_wa=np.ascontiguousarray(a["L1_ffn_gate_w"][0:128]),
        gate_wb=np.ascontiguousarray(np.tile(a["L1_ffn_gate_w"][128:], (2, 1))),
        gate_b=np.ascontiguousarray(np.tile(a["L1_ffn_gate_b"][None], (128, 1))),
        before=np.ascontiguousarray(np.broadcast_to(np.tril(np.ones((E, E), f), -1), (128, E, E))),
        after=np.ascontiguousarray(np.broadcast_to(np.triu(np.ones((E, E), f), 1), (128, E, E))),
    )
    nc = bacc.Bacc("TRN2", target_bir_lowering=False, num_devices=1)
    aps = {k: nc.dram_tensor("in_" + k, v.shape, mybir.dt.from_np(v.dtype), kind="ExternalInput").ap()
           for k, v in ins.items()}
    out = nc.dram_tensor("out_dram", (B, 128, NT, C), F32, kind="ExternalOutput").ap()
    powers = nc.dram_tensor("powers", (2 * S, 63, 2 * S), F32, kind="Internal").ap()
    hybrid_kernel(nc, **aps, out=out, powers=powers)
    res = run(nc, [{"in_" + k: v for k, v in ins.items()}], core_ids=[0])
    got = res.results[0]["out_dram"]
    return np.ascontiguousarray(got.transpose(0, 3, 2, 1)).reshape(B, C, GH, GW)
```
